# Optimizing a Trainium2 kernel written in Bass

```python
import numpy as np
import jax
import jax.numpy as jnp

def _softmax(x, axis=-1):
    return jax.nn.softmax(x, axis=axis)

def _gelu(x):
    return jax.nn.gelu(x, approximate=True)

def _silu(x):
    return jax.nn.silu(x)

def _sigmoid(x):
    return jax.nn.sigmoid(x)

def _layernorm(x, axis=-1, eps=1e-05):
    m = jnp.mean(x, axis=axis, keepdims=True)
    v = jnp.var(x, axis=axis, keepdims=True)
    return (x - m) / jnp.sqrt(v + eps)

def _scatter_add(tgt, idx, src, axis=0):
    return tgt.at[idx].add(src)

def _segment_sum(src, seg, n):
    return jax.ops.segment_sum(src, seg, n)
kernel_name = 'mk_seq_postln_d1_jaxref_r8_1b80a9'

def setup_inputs(seed: int=0):
    np.random.seed(seed)
    _w = jnp.asarray

    def _L0_attn_setup():
        import jax, jax.numpy as jnp
        import numpy as np
        EPS = 1.1920929e-07
        NUM_HEADS = 16
        SOFTCAP = 50.0

        def rms_norm(x):
            return x * jax.lax.rsqrt(jnp.mean(x * x, axis=-1, keepdims=True) + EPS)
        key = jax.random.key(seed)
        ks = jax.random.split(key, 5)
        B, S, D = (2, 256, 128)
        x = jax.random.normal(ks[0], (B, S, D), dtype=jnp.float32)
        w_q = jax.random.normal(ks[1], (D, D), dtype=jnp.float32) * 0.02
        w_k = jax.random.normal(ks[2], (D, D), dtype=jnp.float32) * 0.02
        w_v = jax.random.normal(ks[3], (D, D), dtype=jnp.float32) * 0.02
        w_o = jax.random.normal(ks[4], (D, D), dtype=jnp.float32) * 0.02
        return {'x': x, 'w_q': w_q, 'w_k': w_k, 'w_v': w_v, 'w_o': w_o}
    _L0_attn_in = _L0_attn_setup()

    def _L0_ffn_setup():
        import jax, jax.numpy as jnp
        import numpy as np
        B, S, D, H, F = (4, 512, 128, 16, 512)
        CAP = 0.125
        ROPE_BASE = 10000.0

        def rmsnorm(x, g):
            return x * jax.lax.rsqrt(jnp.mean(x * x, -1, keepdims=True) + 1e-06) * g

        def rope(t, pos):
            hd = t.shape[-1]
            inv = 1.0 / ROPE_BASE ** (jnp.arange(0, hd, 2, dtype=jnp.float32) / hd)
            f = pos[:, None, :, None].astype(jnp.float32) * inv
            emb = jnp.concatenate([f, f], axis=-1)
            cos, sin = (jnp.cos(emb), jnp.sin(emb))
            rot = jnp.concatenate([-t[..., hd // 2:], t[..., :hd // 2]], axis=-1)
            return t * cos + rot * sin
        key = jax.random.key(seed)
        ks = jax.random.split(key, 9)
        scale = 0.02
        x = jax.random.normal(ks[0], (B, S, D), jnp.float32)
        causal = jnp.where(jnp.tril(jnp.ones((S, S), bool)), 0.0, -1000000000.0).astype(jnp.float32)
        attention_mask = jnp.broadcast_to(causal[None, None], (B, 1, S, S))
        position_ids = jnp.broadcast_to(jnp.arange(S, dtype=jnp.int32), (B, S))
        return {'x': x, 'attention_mask': attention_mask, 'position_ids': position_ids, 'router_w': jax.random.normal(ks[1], (D, 1), jnp.float32) * scale, 'router_b': jnp.zeros((1,), jnp.float32), 'wq': jax.random.normal(ks[2], (D, D), jnp.float32) * scale, 'wk': jax.random.normal(ks[3], (D, D), jnp.float32) * scale, 'wv': jax.random.normal(ks[4], (D, D), jnp.float32) * scale, 'wo': jax.random.normal(ks[5], (D, D), jnp.float32) * scale, 'w1': jax.random.normal(ks[6], (D, F), jnp.float32) * scale, 'w2': jax.random.normal(ks[7], (F, D), jnp.float32) * scale, 'ln1': jnp.ones((D,), jnp.float32), 'ln2': jnp.ones((D,), jnp.float32)}
    _L0_ffn_in = _L0_ffn_setup()
    _d = {'L0_attn_x': _L0_attn_in['x'], 'L0_attn_w_q': _L0_attn_in['w_q'], 'L0_attn_w_k': _L0_attn_in['w_k'], 'L0_attn_w_v': _L0_attn_in['w_v'], 'L0_attn_w_o': _L0_attn_in['w_o'], 'L0_ffn_attention_mask': _L0_ffn_in['attention_mask'], 'L0_ffn_position_ids': _L0_ffn_in['position_ids'], 'L0_ffn_router_w': _L0_ffn_in['router_w'], 'L0_ffn_router_b': _L0_ffn_in['router_b'], 'L0_ffn_wq': _L0_ffn_in['wq'], 'L0_ffn_wk': _L0_ffn_in['wk'], 'L0_ffn_wv': _L0_ffn_in['wv'], 'L0_ffn_wo': _L0_ffn_in['wo'], 'L0_ffn_w1': _L0_ffn_in['w1'], 'L0_ffn_w2': _L0_ffn_in['w2'], 'L0_ffn_ln1': _L0_ffn_in['ln1'], 'L0_ffn_ln2': _L0_ffn_in['ln2']}
    _x0 = _d['L0_attn_x']
    _d['L0_attn_x'] = jax.random.normal(jax.random.fold_in(jax.random.key(seed), 1), (16, 512, 128), dtype=_x0.dtype)
    del _x0
    return _d

def reference(L0_attn_x, L0_attn_w_q, L0_attn_w_k, L0_attn_w_v, L0_attn_w_o, L0_ffn_attention_mask, L0_ffn_position_ids, L0_ffn_router_w, L0_ffn_router_b, L0_ffn_wq, L0_ffn_wk, L0_ffn_wv, L0_ffn_wo, L0_ffn_w1, L0_ffn_w2, L0_ffn_ln1, L0_ffn_ln2):

    def _L0_attn_ref(x, w_q, w_k, w_v, w_o):
        import jax, jax.numpy as jnp
        import numpy as np
        EPS = 1.1920929e-07
        NUM_HEADS = 16
        SOFTCAP = 50.0

        def rms_norm(x):
            return x * jax.lax.rsqrt(jnp.mean(x * x, axis=-1, keepdims=True) + EPS)
        B, S, D = x.shape
        H = NUM_HEADS
        dk = D // H

        def split_heads(y):
            return y.reshape(B, S, H, dk).transpose(0, 2, 1, 3)
        q = split_heads(x @ w_q.T)
        k = split_heads(x @ w_k.T)
        v = split_heads(x @ w_v.T)
        q = rms_norm(q)
        k = rms_norm(k)
        scores = jnp.einsum('bhqd,bhkd->bhqk', q, k) / jnp.sqrt(jnp.float32(dk))
        scores = jnp.tanh(scores / SOFTCAP) * SOFTCAP
        causal = jnp.tril(jnp.ones((S, S), dtype=bool))
        scores = jnp.where(causal[None, None], scores, -jnp.inf)
        probs = jax.nn.softmax(scores, axis=-1)
        y = jnp.einsum('bhqk,bhkd->bhqd', probs, v)
        y = y.transpose(0, 2, 1, 3).reshape(B, S, D)
        return y @ w_o.T

    def _L0_ffn_ref(x, attention_mask, position_ids, router_w, router_b, wq, wk, wv, wo, w1, w2, ln1, ln2):
        import jax, jax.numpy as jnp
        import numpy as np
        B, S, D, H, F = (4, 512, 128, 16, 512)
        CAP = 0.125
        ROPE_BASE = 10000.0

        def rmsnorm(x, g):
            return x * jax.lax.rsqrt(jnp.mean(x * x, -1, keepdims=True) + 1e-06) * g

        def rope(t, pos):
            hd = t.shape[-1]
            inv = 1.0 / ROPE_BASE ** (jnp.arange(0, hd, 2, dtype=jnp.float32) / hd)
            f = pos[:, None, :, None].astype(jnp.float32) * inv
            emb = jnp.concatenate([f, f], axis=-1)
            cos, sin = (jnp.cos(emb), jnp.sin(emb))
            rot = jnp.concatenate([-t[..., hd // 2:], t[..., :hd // 2]], axis=-1)
            return t * cos + rot * sin
        b, s, d = x.shape
        hd = d // H
        weights = (x @ router_w)[..., 0] + router_b[0]
        k = int(CAP * s)
        topv, topi = jax.lax.top_k(weights, k)
        thr = topv[:, -1]
        sel_mask = (weights > thr[:, None]).astype(x.dtype)
        kc = k - 1
        sel_idx = jnp.sort(topi[:, :kc], axis=1)
        bidx = jnp.arange(b)[:, None]
        x_sel = x[bidx, sel_idx]
        pos_sel = position_ids[bidx, sel_idx]
        w_sel = weights[bidx, sel_idx]
        m = attention_mask[:, 0]
        m_sel = m[bidx[:, :, None], sel_idx[:, :, None], sel_idx[:, None, :]]
        hn = rmsnorm(x_sel, ln1)

        def heads(t):
            return t.reshape(b, kc, H, hd).transpose(0, 2, 1, 3)
        q = rope(heads(hn @ wq), pos_sel)
        kk = rope(heads(hn @ wk), pos_sel)
        v = heads(hn @ wv)
        sc = jnp.einsum('bhqd,bhkd->bhqk', q, kk) / np.sqrt(hd).astype(np.float32)
        sc = sc + m_sel[:, None]
        a = jax.nn.softmax(sc, axis=-1)
        o = jnp.einsum('bhqk,bhkd->bhqd', a, v).transpose(0, 2, 1, 3).reshape(b, kc, d) @ wo
        x1 = x_sel + o
        x2 = x1 + jax.nn.gelu(rmsnorm(x1, ln2) @ w1) @ w2
        proc = x2 * w_sel[..., None]
        out = jnp.zeros_like(x).at[bidx, sel_idx].set(proc)
        return out + x * (1.0 - sel_mask)[..., None]
    x = L0_attn_x
    x = _layernorm(x + _L0_attn_ref(x, L0_attn_w_q, L0_attn_w_k, L0_attn_w_v, L0_attn_w_o), axis=-1)
    x = _layernorm(x + _L0_ffn_ref(x, L0_ffn_attention_mask, L0_ffn_position_ids, L0_ffn_router_w, L0_ffn_router_b, L0_ffn_wq, L0_ffn_wk, L0_ffn_wv, L0_ffn_wo, L0_ffn_w1, L0_ffn_w2, L0_ffn_ln1, L0_ffn_ln2), axis=-1)
    return x

_drawn_inputs = setup_inputs


def setup_inputs(seed=0):
    import zlib

    import numpy as np

    out = dict(_drawn_inputs(seed))
    spreads = {'L0_ffn_ln1': (1.0, 0.6), 'L0_ffn_ln2': (1.0, 0.6)}
    factors = {'L0_attn_w_q': 8.0,
     'L0_attn_w_k': 8.0,
     'L0_attn_w_v': 6.365,
     'L0_attn_w_o': 6.342,
     'L0_ffn_router_w': 8.0,
     'L0_ffn_wq': 8.0,
     'L0_ffn_wk': 8.0,
     'L0_ffn_wv': 8.0,
     'L0_ffn_wo': 8.0,
     'L0_ffn_w1': 8.0,
     'L0_ffn_w2': 8.0}
    for name, (base, spread) in spreads.items():
        noise = np.random.default_rng([zlib.crc32(name.encode()), seed]).standard_normal(out[name].shape)
        drawn = base * np.exp(spread * noise) if base else spread * noise
        out[name] = jnp.asarray(drawn.astype(out[name].dtype))
    for name, factor in factors.items():
        out[name] = (out[name] * factor).astype(out[name].dtype)
    return out
```

```python
from contextlib import ExitStack

import numpy as np

import concourse.bass as bass
from concourse import mybir

ALU = mybir.AluOpType
ACT = mybir.ActivationFunctionType
AX = mybir.AxisListType
F32 = mybir.dt.float32
F16 = mybir.dt.float16
I32 = mybir.dt.int32

P = 128
B, S, D = 16, 512, 128
H, DH = 16, 8
F = 512
NT = S // P
MASKS = 4
KSEL = int(0.125 * S) - 1
SLOTS = 64
PAIRS = B // 2
SOFTCAP = 50.0
EPS_QK = 1.1920929e-07
EPS_LN = 1e-05
EPS_RMS = 1e-06
QK_SCALE = 64.0
ROPE_BASE = 10000.0
RSQRT_GUESS = 1597463007.0

COL = {(0, 1): 0, (0, 3): 384, (0, 0): 512, (0, 2): 1024, (1, 2): 1280, (1, 1): 1536, (1, 3): 1920, (1, 0): 2048}
GROUP = 5 * 512
UNIT = ((0, 1024), (1024, GROUP))
UNIT_BLOCKS = (((0, 1), (0, 3), (0, 0)), ((0, 2), (1, 2), (1, 1), (1, 3), (1, 0)))


def newton(name):
    return [f"{name}_{s}" for s in ("var", "guess", "a0", "b0", "c0", "a1", "b1", "c1", "a2", "b2", "c2")]


LN = ["sum", "dif", "sq", "mean", "dif2", "dev"]
VE_PREP = (["xT"] + [f"{n}{t}" for t in range(NT) for n in ("qk", "va", "vb")] + ["sq", "ss"] + newton("qkr")
           + ["qkn", "hi_q", "hi_k", "lo_q", "lo_k"] + [f"{n}{t}" for t in range(NT) for n in ("qst", "kst")])
VE_FIN = ["yU0", "rd0", "y0", "yU1", "rd1", "y1", "yT", "res"] + [f"bs{c}" for c in range(NT)] + \
    LN + newton("ln") + [f"x1_{c}" for c in range(NT)]
VE_ROUTE = ["xw", "w", "wb_", "wb"] + [f"ge{c}" for c in range(NT)] + [f"eq{c}" for c in range(NT)] + \
    ["rank", "coef", "E", "xs"]
VE_MOD = ["zb0", "zb1", "ss"] + newton("r1") + ["hn", "ET", "R", "hnT", "RT", "cosp", "sin0", "sin1", "rope", "vv0", "vv1",
     "qkT", "msel", "sc0", "mx0", "sub0", "sc1", "mx1", "sub1", "den", "rden", "PT0", "PT1", "o0", "o1", "oT", "x1f",
     "ss2"] + newton("r2") + ["hn2", "h2T", "h", "hh", "hp", "hu", "g"]
VE_LATE = ["x2", "proc"] + [n for k in range(2) for n in
                            [f"z{k}"] + [f"bs{c}_{k}" for c in range(NT)] + [f"{n}_{k}" for n in LN]
                            + newton(f"ln_{k}") + [f"o{c}_{k}" for c in range(NT)]]
PE_PREP = ["xT"] + [f"qkv{t}" for t in range(NT)] + [f"st{t}" for t in range(NT)]
PE_FIN = ["y0T", "y1T", "yT", "wo"]
PE_ROUTE = ["wrow", "gather"]
PE_MOD = ["ET", "R", "hnT", "RT", "qkv", "qkT", "msel", "S0", "S1", "P0T", "P1T", "PV", "oT", "wo", "h2T", "w1"]
PE_LATE = ["w2", "sc0", "sc1"]

BATCH_SIDE = {0: ["prep.xT"], 1: ["fin.yU1", "prep.qkv0"], 2: ["fin.y1", "prep.qkv1", "prep.qkv2"],
              3: ["fin.yT", "prep.qkv3", "prep.norm"], 4: ["fin.wo"], 5: ["own.yU0", "route.w", "prep.st0", "prep.st1"],
              6: ["prep.st2", "prep.st3"], 7: ["own.y0"]}
PAIR_SIDE = {0: ["late.w2", "gather.0"], 1: ["late.sc0", "late.sc1"], 6: ["route.rank.1"],
             8: ["gather.1", "mod.pick"], 9: ["mod.hnT"], 10: ["mod.qkv"], 11: ["mod.qkT"],
             12: ["mod.S", "mod.exp"], 13: ["mod.PT"], 14: ["mod.wo", "route.rank.0"], 15: ["mod.w1", "mod.tanh"]}


class Batch:

    def __init__(self, pair, k):
        self.pair, self.k = pair + k // 2, k % 2
        self.no = self.pair * 2 + self.k

    def __add__(self, n):
        return Batch(self.pair, self.k + n)

    def __sub__(self, n):
        return self + -n

    def at_least(self, n):
        return not isinstance(self.no, int) or self.no >= n


class Track:

    def __init__(self, sem, names):
        self.sem, self.names, self.next = sem, names, 0
        assert len(set(names)) == len(names)

    def done(self, ins, name):
        assert self.names[self.next] == name, (self.names[self.next], name)
        self.next = (self.next + 1) % len(self.names)
        ins.then_inc(self.sem, 1)

    def wait(self, eng, unit, name):
        if isinstance(unit, Batch):
            unit = unit.no
        if isinstance(unit, int) and unit < 0:
            return
        eng.wait_ge(self.sem, unit * len(self.names) + (self.names.index(name) + 1))


def build(nc, x, w_q, w_k, w_v, w_o, amask, pos, router_w, router_b, wq, wk, wv, wo, w1, w2, ln1, ln2, out):
    ctx = ExitStack()
    with ctx:
        def sb(name, shape, dt=F32):
            return ctx.enter_context(nc.sbuf_tensor(name, shape, dt))

        def sem(name):
            return ctx.enter_context(nc.semaphore(name))

        ident = sb("ident", [P, P])
        ident16 = sb("ident16", [P, P], F16)
        later = sb("later", [P, S])
        slot_no = sb("slot_no", [P, SLOTS])
        slot_i = sb("slot_i", [P, SLOTS], I32)
        head_of = sb("head_of", [P, H])
        half_of = sb("half_of", [P, 2, DH])
        ones1 = sb("ones1", [1, P])
        wT = sb("wT", [P, 4, P])
        rw_col = sb("rw_col", [P, 1])
        rw_row = sb("rw_row", [P, P])
        rb_one = sb("rb_one", [1, 1])
        rb = sb("rb", [P, 1])
        g1 = sb("g1", [P, 1])
        g2 = sb("g2", [P, 1])
        wqkv2 = sb("wqkv2", [P, 3, P])
        wo2 = sb("wo2", [P, P])
        w1_sb = sb("w1_sb", [P, F])
        w2_sb = sb("w2_sb", [P, F // P, P])
        masks = sb("masks", [P, 2, NT, S])
        NPC = MASKS * NT
        pos_i = sb("pos_i", [NPC, P], I32)
        pos_f = sb("pos_f", [NPC, P])
        inv = sb("inv", [P, DH // 2])
        angle = sb("angle", [P, NPC, 4])
        turn_i = sb("turn_i", [P, 2, NPC, 4], I32)
        turn = sb("turn", [P, 2, NPC, 4])
        red = sb("red", [P, 2, NPC, 4])
        trig = sb("trig", [P, NPC, 2 * DH])

        x_in = sb("x_in", [P, 2, NT, D])
        xT = sb("xT", [P, S])
        qk = sb("qk", [P, 2, NT, D])
        qn_v = sb("qn_v", [P, 3, 2 * NT * H])
        st = sb("st", [P, 2, NT, H, 4, DH], F16)
        qk2 = st[:, :, :, :, :, :].rearrange("p s t h c d -> p (s t h c d)")[:, 0:4 * NT * D].bitcast(F32)\
            .rearrange("p (s t d) -> p s t d", s=2, t=NT)
        q_st = sb("q_st", [P, 2, 4, S], F16)
        k_st = sb("k_st", [P, 2, 4, S], F16)
        v_aug = sb("v_aug", [P, 2, NT, H, 32])
        th = sb("th", [P, 2, GROUP])
        pr = sb("pr", [P, 4, GROUP])
        w_raw = pr[:, 0, 0:4 * P].rearrange("p (t d) -> p t d", t=4)
        wo_perm = pr[:, 0, 4 * P:5 * P]
        rw_wide = pr[:, 0, 5 * P:6 * P]
        y_u = sb("y_u", [P, S])
        rd = sb("rd", [P, NT * 8])
        y_tm = sb("y_tm", [P, NT, D])
        yT = sb("yT", [P, S])
        x_res = sb("x_res", [P, 2, NT, D])
        r1 = sb("r1", [P, NT, D])
        stats = sb("stats", [P, NT, 6])
        mv = sb("mv", [P, 3, NT])
        ln_v = sb("ln_v", [P, 3, NT])
        x1 = sb("x1", [P, 2, NT, D + 1])

        w_wide = sb("w_wide", [P, S])
        junk = sb("junk", [P, S])
        cnt_ge = sb("cnt_ge", [P, NT])
        cnt_eq = sb("cnt_eq", [P, NT])
        rank = sb("rank", [P, NT])
        coef = sb("coef", [P, 2, NT])
        E = sb("E", [P, NT, P])
        xs = sb("xs", [P, D + 1 + 2 * DH])
        z_base = sb("z_base", [P, 2, NT, D])
        sel_v = sb("sel_v", [P, 3, 1])
        sel_ss = sb("sel_ss", [P, 1])
        hn = sb("hn", [P, D])
        ET = sb("ET", [P, S])
        R = w_wide
        RT = sb("RT", [P, NT, P])
        hnT = sb("hnT", [P, 2, 2, SLOTS])
        hb = sb("hb", [P, F])
        t_cos, t_sin = (hb[:, 256 * i:256 * i + 256].rearrange("p (h d) -> p h d", d=DH) for i in range(2))
        qk_r = sb("qk_r", [P, 2 * H * DH])
        vv = sb("vv", [P, H // 2, 2, 2 * DH])
        qkT = sb("qkT", [P, 2, P])
        k_wide = sb("k_wide", [P, 2, H, SLOTS])
        msel = sb("msel", [P, SLOTS])
        sc = sb("sc", [P, 8, SLOTS])
        mx = sb("mx", [P, 8])
        pool_mark = sb("pool_mark", [P, 8])
        pm = sb("pm", [P, H, SLOTS])
        den = sb("den", [P, H])
        rden = sb("rden", [P, H])
        PT = k_wide[:, 0].rearrange("p h s -> p (h s)").rearrange("p (n c) -> p n c", n=H // 2)
        o_tm = sb("o_tm", [P, H // 2, 2, DH])
        oT = sb("oT", [P, P])
        x1f = sb("x1f", [P, D])
        h2T = sb("h2T", [P, P])
        hq = sb("hq", [P, F])
        hu = sb("hu", [P, F])
        x2 = sb("x2", [P, D])
        proc = sb("proc", [P, D])
        stats2 = sb("stats2", [P, NT, 6])
        mv2 = sb("mv2", [P, 3, NT])
        lo_v = sb("lo_v", [P, 3, NT])
        y_out = sb("y_out", [P, 2, NT, D])

        ps_s = ctx.enter_context(nc.psum_tensor("ps_s", [P, GROUP], F32))
        ps_y = ctx.enter_context(nc.psum_tensor("ps_y", [P, S], F32))
        ps_a = ctx.enter_context(nc.psum_tensor("ps_a", [P, S], F32))
        ps_m = ctx.enter_context(nc.psum_tensor("ps_m", [P, S], F32))

        weights_in = sem("weights_in")
        const_ready = sem("const_ready")
        setup_pe = sem("setup_pe")
        setup_ve = sem("setup_ve")
        setup_act = sem("setup_act")
        zeroed = sem("zeroed")
        mask_loaded = sem("mask_loaded")
        x_in_loaded = [sem(f"x_in_loaded{i}") for i in range(2)]
        x_res_loaded = [sem(f"x_res_loaded{i}") for i in range(2)]
        out_stored = [sem(f"out_stored{i}") for i in range(2)]
        scores_ready = sem("scores_ready")
        tanh_done = sem("tanh_done")
        exp_done = sem("exp_done")
        masked = sem("masked")
        pv_done = sem("pv_done")
        k_wide_ready = sem("k_wide_ready")
        probs_ready = sem("probs_ready")
        gate_ready = sem("gate_ready")
        ve = {n: Track(sem(f"ve_{n}"), names) for n, names in
              (("prep", VE_PREP), ("fin", VE_FIN), ("route", VE_ROUTE), ("mod", VE_MOD), ("late", VE_LATE))}
        pe = {n: Track(sem(f"pe_{n}"), names) for n, names in
              (("prep", PE_PREP), ("fin", PE_FIN), ("route", PE_ROUTE), ("mod", PE_MOD), ("late", PE_LATE))}

        WEIGHT_DMAS = 24
        N_CONST = 9
        block = ctx.enter_context(nc.Block())

        def live(n, top):
            n = n.no if isinstance(n, Batch) else n
            return not isinstance(n, int) or 0 <= n < top

        def iterations(eng, body, first, last):
            for p in range(-1, first):
                body(p)
            with eng.Fori(first, last + 1) as p:
                body(p)
            for p in range(last + 1, PAIRS + 2):
                body(p)

        def side_steps(p, s):
            k, r = divmod(s, 8)
            steps = []
            for name in BATCH_SIDE[r]:
                kind = name.split(".")[0]
                unit = Batch(p, k + {"prep": 1, "fin": -1, "route": -1, "own": 0}[kind])
                if live(unit, B):
                    par = (k + 1) % 2 if kind != "own" else k
                    steps.append((name.replace("own.", "fin."), unit, par))
            for name in PAIR_SIDE.get(s, []):
                kind = name.split(".")[0]
                if kind == "gather":
                    unit, par = Batch(p, -2 + int(name[-1])), int(name[-1])
                    ok = live(unit, B)
                    name = "route.gather"
                elif kind == "route":
                    par = int(name[-1])
                    unit = Batch(p, -par)
                    ok = live(unit, B)
                    name = "route.rank"
                else:
                    unit = p - 1 if kind == "mod" else p - 2
                    par = None
                    ok = live(unit, PAIRS)
                if ok:
                    steps.append((name, unit, par))
            return steps

        def group(p, s, lag=0):
            s -= lag
            b = Batch(p, s // 8)
            return (b, b.k, s % 8) if live(b, B) else None

        @block.sync
        def _(sp):
            def load_mask(m, k):
                sp.dma_start(masks[:, k], amask[m, 0].rearrange("(c p) j -> p c j", p=P)).then_inc(mask_loaded, 16)

            for i, (w, t) in enumerate(((w_q, 0), (w_k, 1), (w_v, 2), (w_o, 3))):
                sp.dma_start(w_raw[:, t, :], w).then_inc(weights_in, 16)
            for b in range(2):
                sp.dma_start(x_in[:, b], x[b].rearrange("(t p) d -> p t d", p=P)).then_inc(x_in_loaded[b], 16)
            for t, w in enumerate((wq, wk, wv)):
                sp.dma_start(wqkv2[:, t, :], w).then_inc(weights_in, 16)
            sp.dma_start(wo2[:, :], wo).then_inc(weights_in, 16)
            sp.dma_start(w1_sb[:, :], w1).then_inc(weights_in, 16)
            sp.dma_start(w2_sb[:, :, :], w2.rearrange("(c p) d -> p c d", p=P)).then_inc(weights_in, 16)
            sp.dma_start(rw_col[:, :], router_w).then_inc(weights_in, 16)
            sp.dma_start(rb_one[:, :], router_b.rearrange("(a n) -> a n", a=1)).then_inc(weights_in, 16)
            sp.dma_start(g1[:, :], ln1.rearrange("(n a) -> n a", a=1)).then_inc(weights_in, 16)
            sp.dma_start(g2[:, :], ln2.rearrange("(n a) -> n a", a=1)).then_inc(weights_in, 16)
            sp.dma_start(pos_i[:, :], pos.rearrange("b (c p) -> (b c) p", p=P)).then_inc(weights_in, 16)
            for k in range(2):
                load_mask(k, k)

            def load_res(b, k):
                ve["fin"].wait(sp, b - 2, "res")
                sp.dma_start(x_res[:, k], x[b.no].rearrange("(t p) d -> p t d", p=P)).then_inc(x_res_loaded[k], 16)

            def load_x(b, k):
                pe["prep"].wait(sp, b - 2, "xT")
                sp.dma_start(x_in[:, k], x[b.no].rearrange("(t p) d -> p t d", p=P)).then_inc(x_in_loaded[k], 16)

            def store(q, k):
                ve["late"].wait(sp, q, f"o{NT - 1}_{k}")
                sp.dma_start(out[2 * q + k].rearrange("(t p) d -> p t d", p=P), y_out[:, k])\
                  .then_inc(out_stored[k], 16)

            def body(p):
                if live(p, PAIRS):
                    load_res(Batch(p, 0), 0)
                if live(p + 1, PAIRS) and live(p, PAIRS):
                    load_x(Batch(p, 3), 1)
                if live(p - 2, PAIRS):
                    store(p - 2, 0)
                    store(p - 2, 1)
                if live(p, PAIRS):
                    load_res(Batch(p, 1), 1)
                if live(p + 2, PAIRS):
                    load_x(Batch(p, 4), 0)
                if isinstance(p, int) and p in (1, 2):
                    pe["mod"].wait(sp, p - 1, "R")
                    for k in range(2):
                        if min(2 * p + k, MASKS - 1) != min(2 * p - 2 + k, MASKS - 1):
                            load_mask(min(2 * p + k, MASKS - 1), k)
            iterations(sp, body, 3, PAIRS - 3)
            for k in range(2):
                sp.wait_ge(out_stored[k], 16 * PAIRS)

        @block.gpsimd
        def _(pool):
            nc.gpsimd.memset(ident[:, :], 0.0).then_inc(const_ready, 1)
            nc.gpsimd.memset(ident16[:, :], 0.0).then_inc(const_ready, 1)
            nc.gpsimd.memset(later[:, :], 1.0).then_inc(const_ready, 1)
            nc.gpsimd.memset(head_of[:, :], 1.0).then_inc(const_ready, 1)
            nc.gpsimd.memset(half_of[:, :, :], 1.0).then_inc(const_ready, 1)
            nc.gpsimd.memset(ones1[:, :], 1.0).then_inc(const_ready, 1)
            nc.gpsimd.iota(slot_i[:, :], pattern=[[1, SLOTS]], base=0, channel_multiplier=0).then_inc(const_ready, 1)
            pool.wait_ge(const_ready, 7)
            nc.gpsimd.affine_select(out=ident[:, :], in_=ident[:, :], compare_op=ALU.not_equal, fill=1.0, base=0,
                                    pattern=[[-1, P]], channel_multiplier=1).then_inc(const_ready, 1)
            nc.gpsimd.affine_select(out=ident16[:, :], in_=ident16[:, :], compare_op=ALU.not_equal, fill=1.0, base=0,
                                    pattern=[[-1, P]], channel_multiplier=1).then_inc(const_ready, 1)
            nc.gpsimd.affine_select(out=later[:, :], in_=later[:, :], compare_op=ALU.is_ge, fill=0.0, base=0,
                                    pattern=[[1, S]], channel_multiplier=-1).then_inc(const_ready, 1)
            nc.gpsimd.affine_select(out=head_of[:, :], in_=head_of[:, :], compare_op=ALU.is_ge, fill=0.0, base=0,
                                    pattern=[[-DH, H]], channel_multiplier=1).then_inc(const_ready, 1)
            nc.gpsimd.affine_select(out=half_of[:, :, :], in_=half_of[:, :, :], compare_op=ALU.is_ge, fill=0.0, base=0,
                                    pattern=[[-64, 2], [0, DH]], channel_multiplier=1).then_inc(const_ready, 1)
            nc.gpsimd.tensor_copy(slot_no[:, :], slot_i[:, :]).then_inc(const_ready, 1)
            pool.wait_ge(const_ready, 13)
            nc.gpsimd.affine_select(out=head_of[:, :], in_=head_of[:, :], compare_op=ALU.is_ge, fill=0.0, base=DH - 1,
                                    pattern=[[DH, H]], channel_multiplier=-1).then_inc(const_ready, 1)
            nc.gpsimd.affine_select(out=half_of[:, :, :], in_=half_of[:, :, :], compare_op=ALU.is_ge, fill=0.0,
                                    base=63, pattern=[[64, 2], [0, DH]], channel_multiplier=-1)\
                .then_inc(const_ready, 1)
            nc.gpsimd.memset(slot_no[:, KSEL:], -1.0).then_inc(const_ready, 1)
            nc.gpsimd.memset(v_aug[:, :, :, :, :], 0.0).then_inc(zeroed, 1)
            nc.gpsimd.memset(pm[:, :, :], 0.0).then_inc(zeroed, 1)
            pool.wait_ge(zeroed, 2)
            for s in range(2):
                nc.gpsimd.memset(v_aug[:, :, :, :, :].rearrange("p a t (g s j) c -> p (a t g) s j c", g=4, s=2)
                                 [:, :, s, :, 16 * s + DH], 1.0).then_inc(zeroed, 1)

            def causal(g, n0, n, col, step):
                buf = pr[:, g % 4, col:col + P]
                if n > 1:
                    buf = pr[:, g % 4, col:col + step * n].rearrange("p (n c) -> p n c", c=step)[:, :, 0:P]
                return nc.gpsimd.affine_select(out=buf, in_=buf, compare_op=ALU.is_ge, fill=0.0, base=0,
                                               pattern=[[0, n], [1, P]] if n > 1 else [[1, P]], channel_multiplier=-1)

            def body(p):
                for s in range(16):
                    g = group(p, s, 1)
                    if g:
                        b, _, gi = g
                        pool.wait_ge(exp_done, b.no * 8 + (gi + 1))
                        nc.gpsimd.tensor_tensor(pool_mark[:, gi:gi + 1], head_of[:, 0:1], head_of[:, 0:1], ALU.mult)
                        causal(gi, 0, 1, 0, P)
                        causal(gi, 0, 2, 384, P)
                        causal(gi, 0, 3, 1024, 256)
                        causal(gi, 0, 2, 1920, P).then_inc(masked, 1)
                    for name, unit, par in side_steps(p, s):
                        if name == "mod.qkT":
                            ve["mod"].wait(pool, unit, "qkT")
                            pe["mod"].wait(pool, unit - 1, "PV")
                            for k in range(2):
                                nc.gpsimd.tensor_tensor(
                                    k_wide[:, k], qkT[:, 1, None, SLOTS * k:SLOTS * k + SLOTS]
                                    .to_broadcast([P, H, SLOTS]), head_of[:, :, None].to_broadcast([P, H, SLOTS]),
                                    ALU.mult).then_inc(k_wide_ready, 1)
            iterations(pool, body, 2, PAIRS - 1)

        @block.scalar
        def _(act):
            act.wait_ge(setup_ve, SETUP_RED)
            nc.scalar.activation(turn[:, :, :, :], red[:, :, :, :], ACT.Sin).then_inc(setup_act, 1)

            def body(p):
                for s in range(16):
                    g = group(p, s)
                    if g:
                        b, _, gi = g
                        for u, (c0, c1) in enumerate(UNIT):
                            act.wait_ge(scores_ready, b.no * 16 + (2 * gi + u + 1))
                            if gi >= 2 or b.at_least(1):
                                act.wait_ge(exp_done, b.no * 8 + (gi - 1))
                            nc.scalar.activation(th[:, gi % 2, c0:c1], ps_s[:, c0:c1], ACT.Tanh,
                                                 scale=1.0 / (QK_SCALE ** 2 * DH ** 0.5 * SOFTCAP))\
                                .then_inc(tanh_done, 1)
                    g = group(p, s, 1)
                    if g:
                        b, _, gi = g
                        act.wait_ge(tanh_done, b.no * 16 + (2 * gi + 2))
                        if gi >= 4 or b.at_least(1):
                            act.wait_ge(pv_done, b.no * 4 + (gi // 2 - 1))
                        nc.scalar.activation(pr[:, gi % 4, :], th[:, gi % 2, :], ACT.Exp, scale=SOFTCAP)\
                            .then_inc(exp_done, 1)
                    for name, unit, par in side_steps(p, s):
                        if name == "mod.exp":
                            ve["mod"].wait(act, unit, "sub1")
                            nc.scalar.activation(pm[:, :, 0:KSEL], pm[:, :, 0:KSEL], ACT.Exp).then_inc(probs_ready, 1)
                        if name == "mod.tanh":
                            ve["mod"].wait(act, unit, "hu")
                            nc.scalar.activation(hq[:, :], hu[:, :], ACT.Tanh, scale=float(np.sqrt(2.0 / np.pi)))\
                                .then_inc(gate_ready, 1)
            iterations(act, body, 1, PAIRS - 1)

        @block.vector
        def _(v):
            count = [0]

            def setup(ins):
                count[0] += 1
                ins.then_inc(setup_ve, 1)
                v.wait_ge(setup_ve, count[0])

            v.wait_ge(weights_in, 16 * 15)
            v.wait_ge(const_ready, 16)
            v.wait_ge(zeroed, 4)
            for half in range(2):
                for s in range(2):
                    setup(nc.vector.tensor_copy(
                        wo_perm[:, 64 * half:64 * half + 64].rearrange("p (j a s d) -> p s j a d", j=2, a=2, s=2)[:, s],
                        w_raw[:, 3, 64 * half:64 * half + 64].rearrange("p (a s j d) -> p s j a d", j=2, a=2, s=2)[:, s]))
            setup(nc.vector.tensor_copy(rw_wide, rw_col[:, 0:1].to_broadcast([P, P])))
            setup(nc.vector.tensor_copy(pos_f[:, :], pos_i[:, :]))
            for i in range(DH // 2):
                setup(nc.vector.memset(inv[:, i:i + 1], float(np.float32(1.0 / ROPE_BASE ** (2 * i / DH)))))
            v.wait_ge(setup_pe, 1)
            setup(nc.vector.tensor_copy(wT[:, :, :], ps_a[:, :].rearrange("p (t d) -> p t d", t=4)))
            v.wait_ge(setup_pe, 2)
            setup(nc.vector.tensor_copy(rw_row[:, :], ps_m[:, 0:P]))
            setup(nc.vector.tensor_copy(rb[:, :], ps_m[:, 256:257]))
            setup(nc.vector.tensor_tensor(angle[:, :, :], ps_m[:, P:P + NPC, None].to_broadcast([P, NPC, 4]),
                                          inv[:, None, :].to_broadcast([P, NPC, 4]), ALU.mult))
            for i, quarter in enumerate((0.25, 0.0)):
                setup(nc.vector.tensor_scalar(turn_i[:, i], angle[:, :, :], 1.0 / (2 * np.pi), quarter,
                                              ALU.mult, ALU.add))
            setup(nc.vector.tensor_copy(turn[:, :, :, :], turn_i[:, :, :, :]))
            c1 = 6.28125
            c2 = float(np.float32(np.floor((2 * np.pi - c1) * 2 ** 20) / 2 ** 20))
            c3 = float(2 * np.pi - c1 - c2)
            for i in range(2):
                setup(nc.vector.scalar_tensor_tensor(red[:, i], turn[:, i], -c1, angle[:, :, :], ALU.mult, ALU.add))
                setup(nc.vector.scalar_tensor_tensor(red[:, i], turn[:, i], -c2, red[:, i], ALU.mult, ALU.add))
                setup(nc.vector.scalar_tensor_tensor(red[:, i], turn[:, i], -c3, red[:, i], ALU.mult, ALU.add))
            setup(nc.vector.tensor_scalar(red[:, 0], red[:, 0], float(np.pi / 2), None, ALU.add))
            setup(nc.vector.tensor_scalar(red[:, :, :, :], red[:, :, :, :], 3.1415925, -3.1415925, ALU.min, ALU.max))
            assert count[0] == SETUP_RED, count[0]
            v.wait_ge(setup_act, 1)
            for i in range(2):
                setup(nc.vector.tensor_copy(trig[:, :, 4 * i:4 * i + 4], turn[:, 0]))
            setup(nc.vector.tensor_scalar(trig[:, :, 8:12], turn[:, 1], -1.0, None, ALU.mult))
            setup(nc.vector.tensor_copy(trig[:, :, 12:16], turn[:, 1]))
            assert count[0] == SETUP_ALL, count[0]

            def chain(track, unit):
                def step(make, name, after=None):
                    i = track.names.index(name)
                    prev = after or (track.names[i - 1] if i else None)
                    if prev:
                        track.wait(v, unit, prev)
                    track.done(make(), name)
                return step

            def rsqrt(step, name, buf, src, mul, eps, shape_of=lambda a: a):
                var, y, t = buf[:, 0], buf[:, 1], buf[:, 2]
                step(lambda: nc.vector.tensor_scalar(var, src, mul, eps, ALU.mult, ALU.add), f"{name}_var")
                step(lambda: nc.vector.tensor_scalar(y.bitcast(I32), var.bitcast(I32), -0.5, RSQRT_GUESS,
                                                     ALU.mult, ALU.add), f"{name}_guess")
                for i in range(3):
                    step(lambda: nc.vector.tensor_tensor(t, y, y, ALU.mult), f"{name}_a{i}")
                    step(lambda: nc.vector.scalar_tensor_tensor(t, t, -0.5, var, ALU.mult, ALU.mult), f"{name}_b{i}")
                    step(lambda: nc.vector.scalar_tensor_tensor(y, t, 1.5, y, ALU.add, ALU.mult), f"{name}_c{i}")

            def prep_xT(b, k):
                pe["prep"].wait(v, b, "xT")
                pe["prep"].wait(v, b - 1, "qkv3")
                ve["prep"].done(nc.vector.tensor_copy(xT[:, :], ps_a[:, :]), "xT")

            def prep_qkv(b, k, t):
                pe["prep"].wait(v, b, f"qkv{t}")
                if t == 0:
                    ve["prep"].wait(v, b - 1, "lo_k")
                    if b.at_least(2):
                        v.wait_ge(pv_done, (b - 1).no * 4)
                ve["prep"].done(nc.vector.tensor_copy(
                    qk[:, :, t, :], ps_a[:, 0:2 * D].rearrange("p (s d) -> p s d", s=2)), f"qk{t}")
                for s in range(2):
                    o = v_aug[:, k, t, :, :].rearrange("p (g s j) c -> p s g j c", g=4, s=2)
                    i = ps_a[:, 2 * D:3 * D].rearrange("p (g s j d) -> p s g j d", g=4, s=2, j=2)
                    ve["prep"].done(nc.vector.tensor_copy(o[:, s, :, :, 16 * s:16 * s + DH], i[:, s]), f"v{'ab'[s]}{t}")

            def prep_norm(b, k):
                step = chain(ve["prep"], b)
                NV = 2 * NT * H
                pe["prep"].wait(v, b - 1, "st3")
                step(lambda: nc.vector.tensor_tensor(qk2, qk[:, :, :, :], qk[:, :, :, :], ALU.mult), "sq")
                step(lambda: nc.vector.tensor_reduce(
                    qn_v[:, 2], qk2.rearrange("p s t (h d) -> p (s t h) d", d=DH), AX.X, ALU.add), "ss")
                rsqrt(step, "qkr", qn_v, qn_v[:, 2], 1.0 / (DH * QK_SCALE ** 2), EPS_QK / QK_SCALE ** 2)
                qf = qk[:, :, :, :].rearrange("p s t (h d) -> p (s t h) d", d=DH)
                step(lambda: nc.vector.tensor_tensor(qf, qf, qn_v[:, 1, :, None].to_broadcast([P, NV, DH]), ALU.mult),
                     "qkn")
                q_parts = st[:, 0].rearrange("p t h c d -> p (t h) c d")
                k_parts = st[:, 1].rearrange("p t h c d -> p (t h) c d")
                q_src = qk[:, 0].rearrange("p t (h d) -> p (t h) d", d=DH)[:, :, None, :].to_broadcast([P, NT * H, 2, DH])
                k_src = qk[:, 1].rearrange("p t (h d) -> p (t h) d", d=DH)[:, :, None, :].to_broadcast([P, NT * H, 2, DH])
                step(lambda: nc.vector.tensor_copy(q_parts[:, :, 0:2, :], q_src), "hi_q", "qkn")
                step(lambda: nc.vector.tensor_copy(k_parts[:, :, 0:4:2, :], k_src), "hi_k", "qkn")
                step(lambda: nc.vector.tensor_tensor(q_parts[:, :, 2:4, :], q_src, q_parts[:, :, 0:2, :],
                                                     ALU.subtract), "lo_q", "hi_q")
                step(lambda: nc.vector.tensor_tensor(k_parts[:, :, 1:4:2, :], k_src, k_parts[:, :, 0:4:2, :],
                                                     ALU.subtract), "lo_k", "hi_k")

            def prep_st(b, k, t):
                pe["prep"].wait(v, b, f"st{t}")
                if t == 0 and b.at_least(2):
                    v.wait_ge(scores_ready, (b - 1).no * 16)
                parts = ps_a[:, :].bitcast(F16).rearrange("p (s g q) -> p s g q", s=2, g=4)
                ve["prep"].done(nc.vector.tensor_copy(q_st[:, k, :, P * t:P * t + P], parts[:, 0]), f"qst{t}")
                ve["prep"].done(nc.vector.tensor_copy(k_st[:, k, :, P * t:P * t + P], parts[:, 1]), f"kst{t}")

            def fin_yU(b, half):
                v.wait_ge(pv_done, b.no * 4 + (2 * half + 2))
                if half:
                    pe["fin"].wait(v, b, "y0T")
                else:
                    pe["fin"].wait(v, b - 1, "y1T")
                ve["fin"].done(nc.vector.tensor_copy(y_u[:, :], ps_y[:, :]), f"yU{half}")

            def fin_y(b, half):
                pe["fin"].wait(v, b, f"y{half}T")
                if half == 0:
                    pe["fin"].wait(v, b - 1, "yT")
                rows = ps_m[:, :].rearrange("p (n c) -> p n c", c=16)
                ve["fin"].done(nc.vector.reciprocal(rd[:, :], rows[:, :, DH]), f"rd{half}")
                ve["fin"].wait(v, b, f"rd{half}")
                ve["fin"].done(nc.vector.tensor_tensor(
                    y_tm[:, :, 64 * half:64 * half + 64].rearrange("p t (n d) -> p t n d", d=DH),
                    rows[:, :, 0:DH].rearrange("p (t n) d -> p t n d", t=NT),
                    rd[:, :].rearrange("p (t n) -> p t n", t=NT)[:, :, :, None].to_broadcast([P, NT, 8, DH]),
                    ALU.mult), f"y{half}")

            def fin_yT(b, k):
                pe["fin"].wait(v, b, "yT")
                pe["fin"].wait(v, b - 1, "wo")
                ve["fin"].done(nc.vector.tensor_copy(yT[:, :], ps_m[:, :]), "yT")

            def layer_norm(step, tag, src, st6, m, buf, after):
                for c in range(NT):
                    step(lambda: nc.vector.bn_stats(st6[:, c, :], src[:, c, :]), f"bs{c}{tag}", after)
                even, odd = st6[:, :, 1], st6[:, :, 4]
                step(lambda: nc.vector.tensor_tensor(m[:, 0], even, odd, ALU.add), f"sum{tag}")
                step(lambda: nc.vector.tensor_tensor(m[:, 1], even, odd, ALU.subtract), f"dif{tag}", f"bs{NT - 1}{tag}")
                step(lambda: nc.vector.tensor_tensor(m[:, 2], st6[:, :, 2], st6[:, :, 5], ALU.add), f"sq{tag}",
                     f"bs{NT - 1}{tag}")
                step(lambda: nc.vector.tensor_scalar(m[:, 0], m[:, 0], 0.5, None, ALU.mult), f"mean{tag}", f"sum{tag}")
                step(lambda: nc.vector.tensor_tensor(m[:, 1], m[:, 1], m[:, 1], ALU.mult), f"dif2{tag}", f"dif{tag}")
                step(lambda: nc.vector.scalar_tensor_tensor(m[:, 2], m[:, 1], D / 4.0, m[:, 2], ALU.mult, ALU.add),
                     f"dev{tag}")
                rsqrt(step, f"ln{tag}", buf, m[:, 2], 1.0 / D, EPS_LN)

            def fin_wo(b, k):
                step = chain(ve["fin"], b)
                pe["fin"].wait(v, b, "wo")
                v.wait_ge(x_res_loaded[k], b.pair * 16 + 16)
                ve["fin"].wait(v, b - 1, f"x1_{NT - 1}")
                step(lambda: nc.vector.tensor_tensor(r1[:, :, :], ps_m[:, :].rearrange("p (t d) -> p t d", t=NT),
                                                     x_res[:, k], ALU.add), "res")
                layer_norm(step, "", r1, stats, mv, ln_v, "res")
                ve["mod"].wait(v, b.pair - 1, f"zb{k}")
                for c in range(NT):
                    step(lambda: nc.vector.tensor_scalar(x1[:, k, c, 0:D], r1[:, c, :], mv[:, 0, c:c + 1],
                                                         ln_v[:, 1, c:c + 1], ALU.subtract, ALU.mult),
                         f"x1_{c}", "ln_c2")

            def route_w(b, k):
                step = chain(ve["route"], b)
                ve["fin"].wait(v, b, f"x1_{NT - 1}")
                ve["route"].wait(v, b - 1, f"eq{NT - 1}")
                pe["route"].wait(v, b - 2, "gather")
                step(lambda: nc.vector.tensor_tensor(junk[:, :].rearrange("p (t d) -> p t d", t=NT), x1[:, k, :, 0:D],
                                                     rw_row[:, None, :].to_broadcast([P, NT, D]), ALU.mult), "xw")
                step(lambda: nc.vector.tensor_reduce(x1[:, k, :, D:D + 1],
                                                     junk[:, :].rearrange("p (t d) -> p t d", t=NT), AX.X, ALU.add), "w")
                step(lambda: nc.vector.tensor_scalar(x1[:, k, :, D:D + 1], x1[:, k, :, D:D + 1], rb[:, 0:1], None,
                                                     ALU.add), "wb_")
                pe["route"].wait(v, b - 1, "wrow")
                if k == 0:
                    pe["mod"].wait(v, b.pair - 1, "RT")
                step(lambda: nc.vector.tensor_copy(w_wide[:, :].rearrange("p (t m) -> p t m", t=NT),
                                                   x1[:, k, :, D:D + 1].to_broadcast([P, NT, P])), "wb")

            def route_rank(b, k):
                step = chain(ve["route"], b)
                pe["route"].wait(v, b, "wrow")
                for c in range(NT):
                    step(lambda: nc.vector.tensor_scalar(junk[:, :], ps_m[:, :], x1[:, k, c, D:D + 1], 0.0, ALU.is_ge,
                                                         ALU.add, accum_out=cnt_ge[:, c:c + 1]), f"ge{c}")
                for c in range(NT):
                    n = S - P * c
                    step(lambda: nc.vector.scalar_tensor_tensor(
                        junk[:, 0:n], ps_m[:, P * c:], x1[:, k, c, D:D + 1], later[:, 0:n], ALU.is_equal, ALU.mult,
                        accum_out=cnt_eq[:, c:c + 1]), f"eq{c}")
                step(lambda: nc.vector.tensor_tensor(rank[:, :], cnt_ge[:, :], cnt_eq[:, :], ALU.subtract), "rank")
                step(lambda: nc.vector.tensor_scalar(coef[:, k, :], cnt_ge[:, :], float(KSEL) + 0.5, 1.0, ALU.is_gt,
                                                     ALU.add), "coef")
                q = b.pair - 1
                pe["mod"].wait(v, q, "msel")
                step(lambda: nc.vector.tensor_tensor(
                    E[:, :, SLOTS * k:SLOTS * k + SLOTS], rank[:, :, None].to_broadcast([P, NT, SLOTS]),
                    slot_no[:, None, :].to_broadcast([P, NT, SLOTS]), ALU.is_equal), "E")

            def route_gather(b, k):
                pe["route"].wait(v, b, "gather")
                q = b.pair - 1
                ve["late"].wait(v, q, "proc")
                rows = slice(SLOTS * k, SLOTS * k + SLOTS)
                ve["route"].done(nc.vector.tensor_copy(xs[rows, :], ps_m[rows, 0:D + 1 + 2 * DH]), "xs")

            def mod_pick(q, _):
                step = chain(ve["mod"], q)
                ve["late"].wait(v, q - 1, "z1")
                for k in range(2):
                    step(lambda: nc.vector.tensor_tensor(
                        z_base[:, k], x1[:, k, :, 0:D], coef[:, k, :, None].to_broadcast([P, NT, D]), ALU.mult),
                        f"zb{k}")
                ve["route"].wait(v, Batch(q, 1), "xs")
                step(lambda: nc.vector.tensor_tensor_reduce(hn[:, :], xs[:, 0:D], xs[:, 0:D], 1.0, 0.0, ALU.mult,
                                                            ALU.add, sel_ss[:, :]), "ss")
                rsqrt(step, "r1", sel_v, sel_ss[:, :], 1.0 / D, EPS_RMS)
                step(lambda: nc.vector.tensor_scalar(hn[:, :], xs[:, 0:D], sel_v[:, 1], None, ALU.mult), "hn")
                pe["mod"].wait(v, q, "ET")
                pe["late"].wait(v, q - 1, "sc1")
                step(lambda: nc.vector.tensor_copy(ET[:, :], ps_m[:, :]), "ET")
                pe["mod"].wait(v, q, "R")
                pe["route"].wait(v, Batch(q, 1), "wrow")
                step(lambda: nc.vector.tensor_copy(R[:, :], ps_m[:, :]), "R")

            def mod_hnT(q, _):
                step = chain(ve["mod"], q)
                pe["mod"].wait(v, q, "hnT")
                step(lambda: nc.vector.tensor_scalar(
                    hnT[:, :, :, :], ps_m[:, 0:P].rearrange("p (k s) -> p k s", k=2)[:, :, None, :]
                    .to_broadcast([P, 2, 2, SLOTS]), g1[:, 0:1], None, ALU.mult), "hnT")
                pe["mod"].wait(v, q, "RT")
                step(lambda: nc.vector.tensor_copy(RT[:, :, :], ps_m[:, :].rearrange("p (c s) -> p c s", c=NT)), "RT")

            def mod_qkv(q, _):
                step = chain(ve["mod"], q)
                pe["mod"].wait(v, q, "qkv")
                t = ps_m[:, 0:2 * D].rearrange("p (h d) -> p h d", d=DH)
                cos = xs[:, D + 1:D + 1 + DH]
                sin = xs[:, D + 1 + DH:D + 1 + 2 * DH]
                step(lambda: nc.vector.tensor_tensor(t_cos, t, cos[:, None, :].to_broadcast([P, 2 * H, DH]),
                                                     ALU.mult), "cosp")
                for i in range(2):
                    step(lambda: nc.vector.tensor_tensor(
                        t_sin[:, :, 4 * i:4 * i + 4], t[:, :, 4 - 4 * i:8 - 4 * i],
                        sin[:, None, 4 * i:4 * i + 4].to_broadcast([P, 2 * H, 4]), ALU.mult), f"sin{i}", "cosp")
                step(lambda: nc.vector.tensor_tensor(qk_r[:, :].rearrange("p (h d) -> p h d", d=DH), t_cos,
                                                     t_sin, ALU.add), "rope")
                for k in range(2):
                    step(lambda: nc.vector.tensor_tensor(
                        vv[:, :, k, :], ps_m[:, 2 * D + D * k:3 * D + D * k].rearrange("p (n c) -> p n c", n=H // 2),
                        half_of[:, :, :].rearrange("p a d -> p (a d)")[:, None, :].to_broadcast([P, H // 2, 2 * DH]),
                        ALU.mult), f"vv{k}")

            def mod_qkT(q, _):
                step = chain(ve["mod"], q)
                pe["mod"].wait(v, q, "qkT")
                step(lambda: nc.vector.tensor_copy(qkT[:, :, :], ps_m[:, 0:2 * P].rearrange("p (s c) -> p s c", s=2)),
                     "qkT")
                pe["mod"].wait(v, q, "msel")
                step(lambda: nc.vector.tensor_copy(msel[:, :], ps_m[:, 0:SLOTS]), "msel")

            def mod_S(q, _):
                step = chain(ve["mod"], q)
                for h in range(2):
                    pe["mod"].wait(v, q, f"S{h}")
                    step(lambda: nc.vector.scalar_tensor_tensor(
                        sc[:, :, :], ps_m[:, :].rearrange("p (h s) -> p h s", h=8), float(DH ** -0.5),
                        msel[:, None, :].to_broadcast([P, 8, SLOTS]), ALU.mult, ALU.add), f"sc{h}")
                    step(lambda: nc.vector.tensor_reduce(mx[:, :], sc[:, :, 0:KSEL], AX.X, ALU.max), f"mx{h}")
                    step(lambda: nc.vector.tensor_tensor(
                        pm[:, 8 * h:8 * h + 8, 0:KSEL], sc[:, :, 0:KSEL], mx[:, :, None].to_broadcast([P, 8, KSEL]),
                        ALU.subtract), f"sub{h}")

            def mod_PT(q, _):
                step = chain(ve["mod"], q)
                v.wait_ge(probs_ready, q + 1)
                step(lambda: nc.vector.tensor_reduce(den[:, :], pm[:, :, 0:KSEL], AX.X, ALU.add), "den")
                step(lambda: nc.vector.reciprocal(rden[:, :], den[:, :]), "rden")
                for h in range(2):
                    pe["mod"].wait(v, q, f"P{h}T")
                    step(lambda: nc.vector.tensor_copy(PT[:, 4 * h:4 * h + 4, :],
                                                       ps_m[:, :].rearrange("p (n s) -> p n s", n=4)), f"PT{h}")
                pe["mod"].wait(v, q, "PV")
                for k in range(2):
                    rows = slice(SLOTS * k, SLOTS * k + SLOTS)
                    step(lambda: nc.vector.tensor_tensor(
                        o_tm[rows], ps_m[rows, 0:2 * D].rearrange("p (n k a d) -> p k n a d", n=H // 2, k=2, a=2)[:, k],
                        rden[rows, :].rearrange("p (n a) -> p n a", a=2)[:, :, :, None]
                        .to_broadcast([SLOTS, H // 2, 2, DH]), ALU.mult), f"o{k}")

            def mod_wo(q, _):
                step = chain(ve["mod"], q)
                pe["mod"].wait(v, q, "oT")
                step(lambda: nc.vector.tensor_copy(oT[:, :], ps_m[:, 0:P]), "oT")
                pe["mod"].wait(v, q, "wo")
                step(lambda: nc.vector.tensor_tensor(x1f[:, :], xs[:, 0:D], ps_m[:, 0:D], ALU.add), "x1f")
                step(lambda: nc.vector.tensor_tensor_reduce(hn[:, :], x1f[:, :], x1f[:, :], 1.0, 0.0, ALU.mult,
                                                            ALU.add, sel_ss[:, :]), "ss2")
                rsqrt(step, "r2", sel_v, sel_ss[:, :], 1.0 / D, EPS_RMS)
                step(lambda: nc.vector.tensor_scalar(hn[:, :], x1f[:, :], sel_v[:, 1], None, ALU.mult), "hn2")

            def mod_w1(q, _):
                step = chain(ve["mod"], q)
                pe["mod"].wait(v, q, "h2T")
                step(lambda: nc.vector.tensor_scalar(h2T[:, :], ps_m[:, 0:P], g2[:, 0:1], None, ALU.mult), "h2T")
                pe["mod"].wait(v, q, "w1")
                step(lambda: nc.vector.tensor_copy(hb[:, :], ps_m[:, :]), "h")
                step(lambda: nc.vector.tensor_tensor(hq[:, :], hb[:, :], hb[:, :], ALU.mult), "hh")
                step(lambda: nc.vector.tensor_scalar(hq[:, :], hq[:, :], 0.044715, 1.0, ALU.mult, ALU.add), "hp")
                pe["late"].wait(v, q - 1, "w2")
                step(lambda: nc.vector.tensor_tensor(hu[:, :], hq[:, :], hb[:, :], ALU.mult), "hu")

            def mod_gate(q, _):
                v.wait_ge(gate_ready, q + 1)
                ve["mod"].done(nc.vector.scalar_tensor_tensor(hu[:, :], hq[:, :], 1.0, hb[:, :], ALU.add, ALU.mult), "g")

            def late_w2(q, _):
                step = chain(ve["late"], q)
                pe["late"].wait(v, q, "w2")
                step(lambda: nc.vector.scalar_tensor_tensor(x2[:, :], ps_m[:, 0:D], 0.5, x1f[:, :], ALU.mult, ALU.add),
                     "x2")
                step(lambda: nc.vector.tensor_scalar(proc[:, :], x2[:, :], xs[:, D:D + 1], None, ALU.mult), "proc")

            def late_sc(q, k):
                step = chain(ve["late"], q)
                pe["late"].wait(v, q, f"sc{k}")
                if not isinstance(q, int) or q >= 1:
                    v.wait_ge(out_stored[k], q * 16)
                step(lambda: nc.vector.tensor_tensor(y_out[:, k], ps_m[:, :].rearrange("p (t d) -> p t d", t=NT),
                                                     z_base[:, k], ALU.add), f"z{k}")
                layer_norm(step, f"_{k}", y_out[:, k], stats2, mv2, lo_v, f"z{k}")
                for c in range(NT):
                    step(lambda: nc.vector.tensor_scalar(y_out[:, k, c, :], y_out[:, k, c, :], mv2[:, 0, c:c + 1],
                                                         lo_v[:, 1, c:c + 1], ALU.subtract, ALU.mult),
                         f"o{c}_{k}", f"ln_{k}_c2")

            table = {"prep.xT": prep_xT, "prep.norm": prep_norm,
                     **{f"prep.qkv{t}": (lambda b, k, t=t: prep_qkv(b, k, t)) for t in range(NT)},
                     **{f"prep.st{t}": (lambda b, k, t=t: prep_st(b, k, t)) for t in range(NT)},
                     "fin.yU0": lambda b, k: fin_yU(b, 0), "fin.yU1": lambda b, k: fin_yU(b, 1),
                     "fin.y0": lambda b, k: fin_y(b, 0), "fin.y1": lambda b, k: fin_y(b, 1),
                     "fin.yT": fin_yT, "fin.wo": fin_wo, "route.w": route_w, "route.rank": route_rank,
                     "route.gather": route_gather, "mod.pick": mod_pick, "mod.hnT": mod_hnT, "mod.qkv": mod_qkv,
                     "mod.qkT": mod_qkT, "mod.S": mod_S, "mod.PT": mod_PT, "mod.wo": mod_wo, "mod.w1": mod_w1,
                     "mod.tanh": mod_gate, "late.w2": late_w2, "late.sc0": lambda q, _: late_sc(q, 0),
                     "late.sc1": lambda q, _: late_sc(q, 1)}

            def body(p):
                for s in range(16):
                    for name, unit, par in side_steps(p, s):
                        if name in table:
                            table[name](unit, par)
            iterations(v, body, 3, PAIRS - 2)

        @block.tensor
        def _(t_):
            mm = nc.tensor.matmul
            tr = nc.tensor.transpose
            t_.wait_ge(const_ready, 16)
            t_.wait_ge(weights_in, 16 * 15)
            t_.wait_ge(setup_ve, 10)
            for i in range(4):
                last = tr(ps_a[:, P * i:P * i + P], w_raw[:, i, :] if i < 3 else wo_perm, ident[:, :])
            last.then_inc(setup_pe, 1)
            tr(ps_m[:, 0:P], rw_wide, ident[:, :])
            tr(ps_m[:, P:P + NPC], pos_f[:, :], ident[0:NPC, 0:NPC])
            mm(ps_m[:, 256:257], ones1[:, :], rb_one[:, :], start=True, stop=True).then_inc(setup_pe, 1)
            t_.wait_ge(setup_ve, SETUP_ALL)

            def scores(b, k, gi, u):
                if gi > 0 or b.at_least(1):
                    t_.wait_ge(tanh_done, b.no * 16 + (2 * gi + u - 1))
                for hb_, kb in UNIT_BLOCKS[u]:
                    g, j = 2 * (gi // 4) + hb_, gi % 4
                    c = COL[(hb_, kb)]
                    last = mm(ps_s[:, c:c + S - P * kb], k_st[32 * j:32 * j + 32, k, g, P * kb:P * kb + P],
                              q_st[32 * j:32 * j + 32, k, g, P * kb:S], start=True, stop=True)
                last.then_inc(scores_ready, 1)

            def pv(b, k, q):
                t_.wait_ge(masked, b.no * 8 + (2 * q + 2))
                if q % 2 == 0:
                    ve["fin"].wait(t_, b if q else b - 1, "yU0" if q else "yU1")
                for kb in range(NT):
                    for j in range(4):
                        ab, gi = j % 2, 2 * q + j // 2
                        h = 8 * (q // 2) + 4 * ab + gi % 4
                        c = COL[(ab, kb)]
                        last = mm(ps_y[32 * j:32 * j + 32, P * kb:S], v_aug[:, k, kb, h, :],
                                  pr[:, gi % 4, c:c + S - P * kb], start=(q % 2 == 0 and kb == 0),
                                  stop=(q % 2 == 1 and kb == 3), skip_group_check=True)
                last.then_inc(pv_done, 1)

            def four(src, track, name, idn=None):
                for c in range(4):
                    last = tr(ps_m[:, P * c:P * c + P], src(c), ident[:, :])
                track.done(last, name)

            def prep_xT(b, k):
                t_.wait_ge(x_in_loaded[k], b.pair * 16 + 16)
                ve["prep"].wait(t_, b - 1, f"kst{NT - 1}")
                for c in range(NT):
                    last = tr(ps_a[:, P * c:P * c + P], x_in[:, k, c, :], ident[:, :])
                pe["prep"].done(last, "xT")

            def prep_qkv(b, k, t):
                ve["prep"].wait(t_, b, "xT" if t == 0 else f"vb{t - 1}")
                pe["prep"].done(mm(ps_a[:, 0:3 * D], xT[:, P * t:P * t + P],
                                   wT[:, 0:3, :].rearrange("p a d -> p (a d)"), start=True, stop=True), f"qkv{t}")

            def prep_st(b, k, t):
                ve["prep"].wait(t_, b, "lo_k" if t == 0 else f"kst{t - 1}")
                dst = ps_a[:, :].bitcast(F16)
                for s in range(2):
                    for g in range(4):
                        c = (4 * s + g) * P
                        last = tr(dst[:, c:c + P], st[:, s, t, 4 * g:4 * g + 4].rearrange("p h c d -> p (h c d)"),
                                  ident16[:, :])
                pe["prep"].done(last, f"st{t}")

            def fin_y(b, half, k):
                ve["fin"].wait(t_, b, f"yU{half}")
                if not half:
                    ve["route"].wait(t_, b - 1, f"eq{NT - 1}")
                elif k:
                    ve["late"].wait(t_, b.pair - 1, "z1")
                else:
                    ve["mod"].wait(t_, b.pair - 1, "RT")
                four(lambda c: y_u[:, P * c:P * c + P], pe["fin"], f"y{half}T")

            def fin_yT(b, k):
                ve["fin"].wait(t_, b, "y1")
                if not k:
                    ve["mod"].wait(t_, b.pair - 1, "vv1")
                four(lambda c: y_tm[:, c, :], pe["fin"], "yT")

            def fin_wo(b, k):
                ve["fin"].wait(t_, b, "yT")
                if not k:
                    ve["mod"].wait(t_, b.pair - 1, "msel")
                for c in range(NT):
                    last = mm(ps_m[:, P * c:P * c + P], yT[:, P * c:P * c + P], wT[:, 3, :], start=True, stop=True)
                pe["fin"].done(last, "wo")

            def route_rank(b, k):
                ve["route"].wait(t_, b, "wb")
                ve["fin"].wait(t_, b, "res")
                if k == 0:
                    ve["mod"].wait(t_, b.pair - 1, "x1f")
                four(lambda c: w_wide[:, P * c:P * c + P], pe["route"], "wrow")

            def route_gather(b, k):
                ve["route"].wait(t_, b, "E")
                if k == 0:
                    ve["late"].wait(t_, b.pair - 1, "x2")
                    ve["fin"].wait(t_, b + 1, "y0")
                elif GATHER_AFTER(b):
                    ve["fin"].wait(t_, b + 1, "y0")
                mask = trig_mask(b)
                rows = slice(SLOTS * k, SLOTS * k + SLOTS)
                for c in range(NT):
                    mm(ps_m[rows, 0:D + 1], E[:, c, rows], x1[:, k, c, :], start=(c == 0), stop=(c == NT - 1))
                for c in range(NT):
                    last = mm(ps_m[rows, D + 1:D + 1 + 2 * DH], E[:, c, rows], trig[:, NT * mask + c, :],
                              start=(c == 0), stop=(c == NT - 1))
                pe["route"].done(last, "gather")

            def trig_mask(b):
                return min(b.no, MASKS - 1) if isinstance(b.no, int) else MASKS - 1

            def mod_pick(q, _):
                ve["route"].wait(t_, Batch(q, 1), "xs")
                four(lambda c: E[:, c, :], pe["mod"], "ET")
                ve["mod"].wait(t_, q, "ET")
                t_.wait_ge(mask_loaded, {0: 32, 1: 64}.get(q, 80) if isinstance(q, int) else 80)
                for k in range(2):
                    for c in range(NT):
                        last = mm(ps_m[SLOTS * k:SLOTS * k + SLOTS, :], E[:, c, SLOTS * k:SLOTS * k + SLOTS],
                                  masks[:, k, c, :], start=(c == 0), stop=(c == NT - 1))
                pe["mod"].done(last, "R")

            def mod_hnT(q, _):
                ve["mod"].wait(t_, q, "R")
                pe["mod"].done(tr(ps_m[:, 0:P], hn[:, :], ident[:, :]), "hnT")
                ve["mod"].wait(t_, q, "hnT")
                four(lambda c: R[:, P * c:P * c + P], pe["mod"], "RT")

            def mod_qkv(q, _):
                ve["mod"].wait(t_, q, "RT")
                if BEFORE_LAST(q):
                    ve["fin"].wait(t_, Batch(q, 2), "y1")
                mm(ps_m[:, 0:2 * D], hnT[:, :, :, :].rearrange("p k a s -> p (k a s)")[:, SLOTS:3 * SLOTS], wqkv2[:, 0:2, :].rearrange("p a d -> p (a d)"), start=True,
                   stop=True)
                for k in range(2):
                    last = mm(ps_m[:, D * (2 + k):D * (3 + k)], hnT[:, k, :, :].rearrange("p a s -> p (a s)"),
                              wqkv2[:, 2, :], start=True, stop=True)
                pe["mod"].done(last, "qkv")

            def mod_qkT(q, _):
                ve["mod"].wait(t_, q, "vv1")
                if BEFORE_LAST(q):
                    ve["fin"].wait(t_, Batch(q, 2), "yT")
                for s in range(2):
                    last = tr(ps_m[:, P * s:P * s + P], qk_r[:, D * s:D * s + D], ident[:, :])
                pe["mod"].done(last, "qkT")
                ve["mod"].wait(t_, q, "qkT")
                for k in range(2):
                    rows = slice(SLOTS * k, SLOTS * k + SLOTS)
                    for c in range(NT):
                        last = mm(ps_m[rows, 0:SLOTS], RT[:, c, rows], E[:, c, rows], start=(c == 0),
                                  stop=(c == NT - 1))
                pe["mod"].done(last, "msel")

            def mod_S(q, _):
                t_.wait_ge(k_wide_ready, 2 * q + 2)
                ve["mod"].wait(t_, q, "msel")
                if BEFORE_LAST(q):
                    ve["fin"].wait(t_, Batch(q, 2), "res")
                for h in range(2):
                    if h:
                        ve["mod"].wait(t_, q, "sc0")
                    for k in range(2):
                        rows = slice(SLOTS * k, SLOTS * k + SLOTS)
                        last = mm(ps_m[rows, :], qkT[:, 0, rows],
                                  k_wide[:, k, 8 * h:8 * h + 8, :].rearrange("p h s -> p (h s)"), start=True, stop=True)
                    pe["mod"].done(last, f"S{h}")

            def mod_PT(q, _):
                t_.wait_ge(probs_ready, q + 1)
                ve["mod"].wait(t_, q, "sc1")
                for h in range(2):
                    if h:
                        ve["mod"].wait(t_, q, "PT0")
                    four(lambda c: pm[:, 8 * h + 2 * c:8 * h + 2 * c + 2, :].rearrange("p a s -> p (a s)"), pe["mod"],
                         f"P{h}T")
                ve["mod"].wait(t_, q, "PT1")
                for n in range(H // 2):
                    last = mm(ps_m[:, 32 * n:32 * n + 32], PT[:, n, :], vv[:, n, :, :].rearrange("p k c -> p (k c)"),
                              start=True, stop=True)
                pe["mod"].done(last, "PV")

            def mod_wo(q, _):
                ve["mod"].wait(t_, q, "o1")
                pe["mod"].done(tr(ps_m[:, 0:P], o_tm[:, :, :, :].rearrange("p n a d -> p (n a d)"), ident[:, :]), "oT")
                ve["mod"].wait(t_, q, "oT")
                pe["mod"].done(mm(ps_m[:, 0:D], oT[:, :], wo2[:, :], start=True, stop=True), "wo")

            def mod_w1(q, _):
                ve["mod"].wait(t_, q, "hn2")
                if BEFORE_LAST(q):
                    ve["fin"].wait(t_, Batch(q, 3), "y0")
                pe["mod"].done(tr(ps_m[:, 0:P], hn[:, :], ident[:, :]), "h2T")
                ve["mod"].wait(t_, q, "h2T")
                for c in range(F // P):
                    last = mm(ps_m[:, P * c:P * c + P], w1_sb[:, P * c:P * c + P], h2T[:, :], start=True, stop=True)
                pe["mod"].done(last, "w1")

            def late_w2(q, _):
                ve["mod"].wait(t_, q, "g")
                for c in range(F // P):
                    last = mm(ps_m[:, 0:D], hu[:, P * c:P * c + P], w2_sb[:, c, :], start=(c == 0),
                              stop=(c == F // P - 1))
                pe["late"].done(last, "w2")

            def late_sc(q, k):
                ve["late"].wait(t_, q, "z0" if k else "proc")
                if k == 0 and BEFORE_LAST(q):
                    ve["route"].wait(t_, Batch(q, 2), "xs")
                rows = slice(SLOTS * k, SLOTS * k + SLOTS)
                for c in range(NT):
                    last = mm(ps_m[:, P * c:P * c + P], ET[rows, P * c:P * c + P], proc[rows, :], start=True, stop=True)
                pe["late"].done(last, f"sc{k}")

            def BEFORE_LAST(q):
                return not isinstance(q, int) or q < PAIRS - 1

            def GATHER_AFTER(b):
                return not isinstance(b.no, int) or b.no < B - 1

            table = {"prep.xT": prep_xT,
                     **{f"prep.qkv{t}": (lambda b, k, t=t: prep_qkv(b, k, t)) for t in range(NT)},
                     **{f"prep.st{t}": (lambda b, k, t=t: prep_st(b, k, t)) for t in range(NT)},
                     "fin.y0": lambda b, k: fin_y(b, 0, k), "fin.y1": lambda b, k: fin_y(b, 1, k),
                     "fin.yT": fin_yT, "fin.wo": fin_wo, "route.rank": route_rank, "route.gather": route_gather,
                     "mod.pick": mod_pick, "mod.hnT": mod_hnT, "mod.qkv": mod_qkv, "mod.qkT": mod_qkT, "mod.S": mod_S,
                     "mod.PT": mod_PT, "mod.wo": mod_wo, "mod.w1": mod_w1, "late.w2": late_w2,
                     "late.sc0": lambda q, _: late_sc(q, 0), "late.sc1": lambda q, _: late_sc(q, 1)}

            def body(p):
                for s in range(16):
                    g = group(p, s, -1)
                    if g:
                        b, k, gi = g
                        if gi == 0:
                            ve["prep"].wait(t_, b, f"kst{NT - 1}")
                        for u in range(2):
                            scores(b, k, gi, u)
                    g = group(p, s, 3)
                    if g and g[2] % 2 == 0:
                        pv(g[0], g[1], g[2] // 2)
                    for name, unit, par in side_steps(p, s):
                        if name in table:
                            table[name](unit, par)
            iterations(t_, body, 3, PAIRS - 2)


SETUP_RED = 25
SETUP_ALL = 29


_INS = ['L0_attn_x', 'L0_attn_w_q', 'L0_attn_w_k', 'L0_attn_w_v', 'L0_attn_w_o', 'L0_ffn_attention_mask',
        'L0_ffn_position_ids', 'L0_ffn_router_w', 'L0_ffn_router_b', 'L0_ffn_wq', 'L0_ffn_wk', 'L0_ffn_wv',
        'L0_ffn_wo', 'L0_ffn_w1', 'L0_ffn_w2', 'L0_ffn_ln1', 'L0_ffn_ln2']


def kernel(**inputs):
    import numpy as _np
    import concourse.bacc as _bacc
    from concourse import mybir as _mybir
    from concourse.bass_utils import run_bass_kernel_spmd as _run

    nc = _bacc.Bacc("TRN2", target_bir_lowering=False, num_devices=1)
    arrays, args = {}, []
    for name in _INS:
        a = _np.ascontiguousarray(inputs[name])
        arrays[f"in_{name}"] = a
        args.append(nc.dram_tensor(f"in_{name}", a.shape, _mybir.dt.from_np(a.dtype), kind="ExternalInput").ap())
    args.append(nc.dram_tensor("result", (16, 512, 128), _mybir.dt.float32, kind="ExternalOutput").ap())
    build(nc, *args)
    r = _run(nc, [arrays], core_ids=[0])
    return r.results[0]["result"]
```

```python
from contextlib import ExitStack

import numpy as np

import concourse.bass as bass
from concourse import mybir

ALU = mybir.AluOpType
ACT = mybir.ActivationFunctionType
AX = mybir.AxisListType
F32 = mybir.dt.float32
F16 = mybir.dt.float16
I32 = mybir.dt.int32

P = 128
B, S, D = 16, 512, 128
H, DH = 16, 8
F = 512
NT = S // P
MASKS = 4
KSEL = int(0.125 * S) - 1
SLOTS = 64
PAIRS = B // 2
SOFTCAP = 50.0
EPS_QK = 1.1920929e-07
EPS_LN = 1e-05
EPS_RMS = 1e-06
QK_SCALE = 64.0
ROPE_BASE = 10000.0
RSQRT_GUESS = 1597463007.0

COL = {(0, 1): 0, (0, 3): 384, (0, 0): 512, (0, 2): 1024, (1, 2): 1280, (1, 1): 1536, (1, 3): 1920, (1, 0): 2048}
GROUP = 5 * 512
UNIT = ((0, 1024), (1024, GROUP))
UNIT_BLOCKS = (((0, 1), (0, 3), (0, 0)), ((0, 2), (1, 2), (1, 1), (1, 3), (1, 0)))


def newton(name):
    return [f"{name}_{s}" for s in ("var", "guess", "a0", "b0", "c0", "a1", "b1", "c1", "a2", "b2", "c2")]


LN = ["sum", "dif", "sq", "mean", "dif2", "dev"]

VE_PREP = ["xT", "qk0", "qk1", "va", "vb", "ss"] + newton("qkr") + ["qkn", "hi_q", "hi_k"] + \
    [f"{n}{t}" for t in range(NT) for n in ("qst", "kst")]
VE_FIN = ["yU0", "rd0", "y0", "yU1", "rd1", "y1", "yT", "res"] + [f"bs{c}" for c in range(NT)] + \
    LN + newton("ln") + [f"x1_{c}" for c in range(NT)]
VE_ROUTE = ["w", "w_b", "wide"] + [f"ge{c}" for c in range(NT)] + [f"eq{c}" for c in range(NT)] + \
    ["rank", "coef", "E"]
VE_MOD = ["xs", "ET", "R", "ss"] + newton("r1") + ["hn", "RT", "hnT", "cosp", "sin0", "sin1", "rope", "vv0", "vv1",
    "msel", "qkT", "sc0", "mx0", "sub0", "sc1", "mx1", "sub1", "den", "rden", "PT0", "PT1", "o0", "o1", "oT", "x1f",
    "ss2"] + newton("r2") + ["hn2", "h2T", "h", "hp", "g"]
VE_LATE = ["x2", "proc", "z0", "z1"] + [f"bs{c}_" for c in range(2 * NT)] + [f"{n}_" for n in LN] + newton("ln_") + \
    [f"o{c}_" for c in range(2 * NT)]
PE_PREP = ["xT", "qk0", "qk1", "v"] + [f"st{t}" for t in range(NT)]
PE_FIN = ["y0T", "y1T", "yT", "wo"]
PE_ROUTE = ["wrow"]
PE_MOD = ["gather", "ET", "R", "RT", "hnT", "qkv", "msel", "qkT", "S0", "S1", "P0T", "P1T", "PV", "oT", "wo", "h2T",
          "w1"]
PE_LATE = ["w2", "sc0", "sc1"]
POOL_PREP = ["sq", "lo_q", "lo_k"]
POOL_ROUTE = ["xw"]
POOL_MOD = ["zb0", "zb1", "kw0", "kw1", "hh", "hu"]

SCHEDULE = {
    0: (["prep.xT", "mod.S0"], ["prep.qk0", "mod.S1"]),
    1: (["prep.qk1", "prep.sq"], ["fin.yU1", "prep.v", "mod.exp", "mod.P0"]),
    2: (["prep.norm", "mod.P1"], ["fin.y1"]),
    3: (["mod.PV", "fin.yT"], ["prep.split", "fin.wo"]),
    4: (["prep.lo", "mod.oT", "fin.ln"], ["mod.wo"]),
    5: (["prep.st0", "route.w"], ["own.yU0", "prep.st1", "mod.h2T"]),
    6: (["prep.st2", "route.ge"], ["prep.st3", "route.eq", "mod.w1"]),
    7: (["own.y0", "mod.tanh"], ["late.w2"]),
    8: (["prep.xT", "late.sc0"], ["prep.qk0", "late.sc1"]),
    9: (["prep.qk1", "prep.sq", "mod.gather", "mod.zb"], ["fin.yU1", "prep.v", "mod.ET"]),
    10: (["prep.norm", "mod.R"], ["fin.y1"]),
    11: (["fin.yT", "mod.rms"], ["prep.split", "fin.wo"]),
    12: (["prep.lo", "mod.RT", "fin.ln"], ["mod.hnT", "late.stats"]),
    13: (["prep.st0", "mod.qkv"], ["own.yU0", "prep.st1", "mod.msel", "route.w"]),
    14: (["prep.st2", "route.ge"], ["prep.st3", "route.eq", "mod.qkT"]),
    15: (["own.y0", "late.norm"], []),
}


class Batch:

    def __init__(self, pair, k):
        self.pair, self.k = pair + k // 2, k % 2
        self.no = self.pair * 2 + self.k

    def __add__(self, n):
        return Batch(self.pair, self.k + n)

    def __sub__(self, n):
        return self + -n

    def at_least(self, n):
        return not isinstance(self.no, int) or self.no >= n


class Track:

    def __init__(self, sem, names, units):
        self.sem, self.names, self.units, self.next = sem, names, units, 0
        assert len(set(names)) == len(names)

    def done(self, ins, name):
        assert self.names[self.next] == name, (self.names[self.next], name)
        self.next = (self.next + 1) % len(self.names)
        ins.then_inc(self.sem, 1)

    def wait(self, eng, unit, name):
        if isinstance(unit, Batch):
            unit = unit.no
        if isinstance(unit, int) and not 0 <= unit < self.units:
            return
        eng.wait_ge(self.sem, unit * len(self.names) + (self.names.index(name) + 1))


def build(nc, x, w_q, w_k, w_v, w_o, amask, pos, router_w, router_b, wq, wk, wv, wo, w1, w2, ln1, ln2, out):
    ctx = ExitStack()
    with ctx:
        def sb(name, shape, dt=F32):
            return ctx.enter_context(nc.sbuf_tensor(name, shape, dt))

        def sem(name):
            return ctx.enter_context(nc.semaphore(name))

        ident = sb("ident", [P, P])
        ident16 = sb("ident16", [P, P], F16)
        later = sb("later", [P, S])
        slot_no = sb("slot_no", [P, SLOTS])
        slot_i = sb("slot_i", [P, SLOTS], I32)
        head_of = sb("head_of", [P, H])
        half_of = sb("half_of", [P, 2, DH])
        ones1 = sb("ones1", [1, P])
        wT = sb("wT", [P, 4, P])
        rw_col = sb("rw_col", [P, 1])
        rw_row = sb("rw_row", [P, P])
        rb_one = sb("rb_one", [1, 1])
        rb = sb("rb", [P, 1])
        g1 = sb("g1", [P, 1])
        g2 = sb("g2", [P, 1])
        wqkv2 = sb("wqkv2", [P, 3, P])
        wo2 = sb("wo2", [P, P])
        w1_sb = sb("w1_sb", [P, F])
        w2_sb = sb("w2_sb", [P, F // P, P])
        masks = sb("masks", [P, 2, NT, S])
        NPC = MASKS * NT
        pos_i = sb("pos_i", [NPC, P], I32)
        pos_f = sb("pos_f", [NPC, P])
        inv = sb("inv", [P, DH // 2])
        angle = sb("angle", [P, NPC, 4])
        turn_i = sb("turn_i", [P, 2, NPC, 4], I32)
        turn = sb("turn", [P, 2, NPC, 4])
        red = sb("red", [P, 2, NPC, 4])
        trig = sb("trig", [P, NPC, 2 * DH])

        x_in = sb("x_in", [P, 2, NT, D])
        xT = sb("xT", [P, S])
        qk = sb("qk", [P, 2, NT, D])
        qn_v = sb("qn_v", [P, 3, 2 * NT * H])
        st = sb("st", [P, 2, NT, H, 4, DH], F16)
        qk2 = st[:, :, :, :, :, :].rearrange("p s t h c d -> p (s t h c d)")[:, 0:4 * NT * D].bitcast(F32)\
            .rearrange("p (s t d) -> p s t d", s=2, t=NT)
        hi_parts = [st[:, 0].rearrange("p t h c d -> p (t h) c d")[:, :, 0:2, :],
                    st[:, 1].rearrange("p t h c d -> p (t h) c d")[:, :, 0:4:2, :]]
        lo_parts = [st[:, 0].rearrange("p t h c d -> p (t h) c d")[:, :, 2:4, :],
                    st[:, 1].rearrange("p t h c d -> p (t h) c d")[:, :, 1:4:2, :]]
        qk_twice = [qk[:, s].rearrange("p t (h d) -> p (t h) d", d=DH)[:, :, None, :].to_broadcast([P, NT * H, 2, DH])
                    for s in range(2)]
        q_st = sb("q_st", [P, 2, 4, S], F16)
        k_st = sb("k_st", [P, 2, 4, S], F16)
        v_aug = sb("v_aug", [P, 2, NT, H, 32])
        th = sb("th", [P, 2, GROUP])
        pr = sb("pr", [P, 4, GROUP])
        w_raw = pr[:, 0, 0:4 * P].rearrange("p (t d) -> p t d", t=4)
        wo_perm = pr[:, 0, 4 * P:5 * P]
        rw_wide = pr[:, 0, 5 * P:6 * P]
        y_u = sb("y_u", [P, S])
        rd = sb("rd", [P, NT * 8])
        y_tm = sb("y_tm", [P, NT, D])
        yT = sb("yT", [P, S])
        x_res = sb("x_res", [P, 2, NT, D])
        r1 = sb("r1", [P, NT, D])
        stats = sb("stats", [P, NT, 6])
        mv = sb("mv", [P, 3, NT])
        ln_v = sb("ln_v", [P, 3, NT])
        x1 = sb("x1", [P, 2, NT, D + 1])

        w_wide = sb("w_wide", [P, S])
        junk = sb("junk", [P, S])
        cnt_ge = sb("cnt_ge", [P, NT])
        cnt_eq = sb("cnt_eq", [P, NT])
        rank = sb("rank", [P, NT])
        coef = sb("coef", [P, 2, NT])
        E = sb("E", [P, NT, P])
        xs = sb("xs", [P, D + 1 + 2 * DH])
        z_base = sb("z_base", [P, 2, NT, D])
        sel_v = sb("sel_v", [P, 3, 1])
        sel_ss = sb("sel_ss", [P, 1])
        hn = sb("hn", [P, D])
        ET = sb("ET", [P, S])
        R = w_wide
        RT = sb("RT", [P, NT, P])
        hnT = sb("hnT", [P, 2, 2, SLOTS])
        hb = sb("hb", [P, F])
        t_cos, t_sin = (hb[:, 256 * i:256 * i + 256].rearrange("p (h d) -> p h d", d=DH) for i in range(2))
        qk_r = sb("qk_r", [P, 2 * H * DH])
        vv = sb("vv", [P, H // 2, 2, 2 * DH])
        qkT = sb("qkT", [P, 2, P])
        k_wide = sb("k_wide", [P, 2, H, SLOTS])
        msel = sb("msel", [P, SLOTS])
        sc = sb("sc", [P, 8, SLOTS])
        mx = sb("mx", [P, 8])
        pool_mark = sb("pool_mark", [P, 8])
        pm = sb("pm", [P, H, SLOTS])
        den = sb("den", [P, H])
        rden = sb("rden", [P, H])
        PT = k_wide[:, 0].rearrange("p h s -> p (h s)").rearrange("p (n c) -> p n c", n=H // 2)
        o_tm = sb("o_tm", [P, H // 2, 2, DH])
        oT = sb("oT", [P, P])
        x1f = sb("x1f", [P, D])
        h2T = sb("h2T", [P, P])
        hq = sb("hq", [P, F])
        hu = sb("hu", [P, F])
        x2 = sb("x2", [P, D])
        proc = sb("proc", [P, D])
        stats2 = sb("stats2", [P, 2 * NT, 6])
        mv2 = sb("mv2", [P, 3, 2 * NT])
        lo_v = sb("lo_v", [P, 3, 2 * NT])
        y_out = sb("y_out", [P, 2, NT, D])

        ps_s = ctx.enter_context(nc.psum_tensor("ps_s", [P, GROUP], F32))
        ps_y = ctx.enter_context(nc.psum_tensor("ps_y", [P, S], F32))
        ps_a = ctx.enter_context(nc.psum_tensor("ps_a", [P, S], F32))
        ps_m = ctx.enter_context(nc.psum_tensor("ps_m", [P, S], F32))

        weights_in = sem("weights_in")
        const_ready = sem("const_ready")
        setup_pe = sem("setup_pe")
        setup_ve = sem("setup_ve")
        setup_act = sem("setup_act")
        zeroed = sem("zeroed")
        mask_loaded = sem("mask_loaded")
        x_in_loaded = [sem(f"x_in_loaded{i}") for i in range(2)]
        x_res_loaded = [sem(f"x_res_loaded{i}") for i in range(2)]
        out_stored = [sem(f"out_stored{i}") for i in range(2)]
        scores_ready = sem("scores_ready")
        tanh_done = sem("tanh_done")
        exp_done = sem("exp_done")
        masked = sem("masked")
        pv_done = sem("pv_done")
        probs_ready = sem("probs_ready")
        gate_ready = sem("gate_ready")
        ve = {n: Track(sem(f"ve_{n}"), names, top) for n, names, top in
              (("prep", VE_PREP, B), ("fin", VE_FIN, B), ("route", VE_ROUTE, B), ("mod", VE_MOD, PAIRS),
               ("late", VE_LATE, PAIRS))}
        pe = {n: Track(sem(f"pe_{n}"), names, top) for n, names, top in
              (("prep", PE_PREP, B), ("fin", PE_FIN, B), ("route", PE_ROUTE, B), ("mod", PE_MOD, PAIRS),
               ("late", PE_LATE, PAIRS))}
        pl = {n: Track(sem(f"pool_{n}"), names, top) for n, names, top in
              (("prep", POOL_PREP, B), ("route", POOL_ROUTE, B), ("mod", POOL_MOD, PAIRS))}

        block = ctx.enter_context(nc.Block())

        def live(n, top):
            n = n.no if isinstance(n, Batch) else n
            return not isinstance(n, int) or 0 <= n < top

        def iterations(eng, body, first, last):
            for p in range(-1, first):
                body(p)
            with eng.Fori(first, last + 1) as p:
                body(p)
            for p in range(last + 1, PAIRS + 2):
                body(p)

        def side_steps(p, s, half):
            steps = []
            for name in SCHEDULE[s][half]:
                kind = name.split(".")[0]
                if kind in ("mod", "late"):
                    unit, top = (p - 1 if kind == "mod" and s >= 9 else p - 2), PAIRS
                else:
                    unit, top = Batch(p, s // 8 + {"prep": 1, "fin": -1, "route": -1, "own": 0}[kind]), B
                if live(unit, top):
                    steps.append((name.replace("own.", "fin."), unit, unit.k if top == B else None))
            return steps

        def run_side(table, p, s, half):
            for name, unit, k in side_steps(p, s, half):
                if name in table:
                    table[name](unit, k)

        def group(p, s, lag=0):
            s -= lag
            b = Batch(p, s // 8)
            return (b, b.k, s % 8) if live(b, B) else None

        @block.sync
        def _(sp):
            def load_mask(m, k):
                sp.dma_start(masks[:, k], amask[m, 0].rearrange("(c p) j -> p c j", p=P)).then_inc(mask_loaded, 16)

            for i, (w, t) in enumerate(((w_q, 0), (w_k, 1), (w_v, 2), (w_o, 3))):
                sp.dma_start(w_raw[:, t, :], w).then_inc(weights_in, 16)
            for b in range(2):
                sp.dma_start(x_in[:, b], x[b].rearrange("(t p) d -> p t d", p=P)).then_inc(x_in_loaded[b], 16)
            for t, w in enumerate((wq, wk, wv)):
                sp.dma_start(wqkv2[:, t, :], w).then_inc(weights_in, 16)
            sp.dma_start(wo2[:, :], wo).then_inc(weights_in, 16)
            sp.dma_start(w1_sb[:, :], w1).then_inc(weights_in, 16)
            sp.dma_start(w2_sb[:, :, :], w2.rearrange("(c p) d -> p c d", p=P)).then_inc(weights_in, 16)
            sp.dma_start(rw_col[:, :], router_w).then_inc(weights_in, 16)
            sp.dma_start(rb_one[:, :], router_b.rearrange("(a n) -> a n", a=1)).then_inc(weights_in, 16)
            sp.dma_start(g1[:, :], ln1.rearrange("(n a) -> n a", a=1)).then_inc(weights_in, 16)
            sp.dma_start(g2[:, :], ln2.rearrange("(n a) -> n a", a=1)).then_inc(weights_in, 16)
            sp.dma_start(pos_i[:, :], pos.rearrange("b (c p) -> (b c) p", p=P)).then_inc(weights_in, 16)
            for k in range(2):
                load_mask(k, k)

            def load_res(b, k):
                ve["fin"].wait(sp, b - 2, "res")
                sp.dma_start(x_res[:, k], x[b.no].rearrange("(t p) d -> p t d", p=P)).then_inc(x_res_loaded[k], 16)

            def load_x(b, k):
                pe["prep"].wait(sp, b - 2, "xT")
                sp.dma_start(x_in[:, k], x[b.no].rearrange("(t p) d -> p t d", p=P)).then_inc(x_in_loaded[k], 16)

            def store(q, k):
                ve["late"].wait(sp, q, f"o{NT * k + NT - 1}_")
                sp.dma_start(out[2 * q + k].rearrange("(t p) d -> p t d", p=P), y_out[:, k])\
                  .then_inc(out_stored[k], 16)

            def body(p):
                if live(p, PAIRS):
                    load_res(Batch(p, 0), 0)
                if live(p + 1, PAIRS) and live(p, PAIRS):
                    load_x(Batch(p, 3), 1)
                if live(p, PAIRS):
                    load_res(Batch(p, 1), 1)
                if live(p + 2, PAIRS):
                    load_x(Batch(p, 4), 0)
                if isinstance(p, int) and p in (1, 2):
                    pe["mod"].wait(sp, p - 1, "R")
                    for k in range(2):
                        if min(2 * p + k, MASKS - 1) != min(2 * p - 2 + k, MASKS - 1):
                            load_mask(min(2 * p + k, MASKS - 1), k)
                if live(p - 2, PAIRS):
                    store(p - 2, 0)
                    store(p - 2, 1)
            iterations(sp, body, 3, PAIRS - 3)
            for k in range(2):
                sp.wait_ge(out_stored[k], 16 * PAIRS)

        @block.gpsimd
        def _(pool):
            nc.gpsimd.memset(ident[:, :], 0.0).then_inc(const_ready, 1)
            nc.gpsimd.memset(ident16[:, :], 0.0).then_inc(const_ready, 1)
            nc.gpsimd.memset(later[:, :], 1.0).then_inc(const_ready, 1)
            nc.gpsimd.memset(head_of[:, :], 1.0).then_inc(const_ready, 1)
            nc.gpsimd.memset(half_of[:, :, :], 1.0).then_inc(const_ready, 1)
            nc.gpsimd.memset(ones1[:, :], 1.0).then_inc(const_ready, 1)
            nc.gpsimd.iota(slot_i[:, :], pattern=[[1, SLOTS]], base=0, channel_multiplier=0).then_inc(const_ready, 1)
            pool.wait_ge(const_ready, 7)
            nc.gpsimd.affine_select(out=ident[:, :], in_=ident[:, :], compare_op=ALU.not_equal, fill=1.0, base=0,
                                    pattern=[[-1, P]], channel_multiplier=1).then_inc(const_ready, 1)
            nc.gpsimd.affine_select(out=ident16[:, :], in_=ident16[:, :], compare_op=ALU.not_equal, fill=1.0, base=0,
                                    pattern=[[-1, P]], channel_multiplier=1).then_inc(const_ready, 1)
            nc.gpsimd.affine_select(out=later[:, :], in_=later[:, :], compare_op=ALU.is_ge, fill=0.0, base=0,
                                    pattern=[[1, S]], channel_multiplier=-1).then_inc(const_ready, 1)
            nc.gpsimd.affine_select(out=head_of[:, :], in_=head_of[:, :], compare_op=ALU.is_ge, fill=0.0, base=0,
                                    pattern=[[-DH, H]], channel_multiplier=1).then_inc(const_ready, 1)
            nc.gpsimd.affine_select(out=half_of[:, :, :], in_=half_of[:, :, :], compare_op=ALU.is_ge, fill=0.0, base=0,
                                    pattern=[[-64, 2], [0, DH]], channel_multiplier=1).then_inc(const_ready, 1)
            nc.gpsimd.tensor_copy(slot_no[:, :], slot_i[:, :]).then_inc(const_ready, 1)
            pool.wait_ge(const_ready, 13)
            nc.gpsimd.affine_select(out=head_of[:, :], in_=head_of[:, :], compare_op=ALU.is_ge, fill=0.0, base=DH - 1,
                                    pattern=[[DH, H]], channel_multiplier=-1).then_inc(const_ready, 1)
            nc.gpsimd.affine_select(out=half_of[:, :, :], in_=half_of[:, :, :], compare_op=ALU.is_ge, fill=0.0,
                                    base=63, pattern=[[64, 2], [0, DH]], channel_multiplier=-1)\
                .then_inc(const_ready, 1)
            nc.gpsimd.memset(slot_no[:, KSEL:], -1.0).then_inc(const_ready, 1)
            nc.gpsimd.memset(v_aug[:, :, :, :, :], 0.0).then_inc(zeroed, 1)
            nc.gpsimd.memset(pm[:, :, :], 0.0).then_inc(zeroed, 1)
            pool.wait_ge(zeroed, 2)
            for s in range(2):
                nc.gpsimd.memset(v_aug[:, :, :, :, :].rearrange("p a t (g s j) c -> p (a t g) s j c", g=4, s=2)
                                 [:, :, s, :, 16 * s + DH], 1.0).then_inc(zeroed, 1)

            def causal(g, n0, n, col, step):
                buf = pr[:, g % 4, col:col + P]
                if n > 1:
                    buf = pr[:, g % 4, col:col + step * n].rearrange("p (n c) -> p n c", c=step)[:, :, 0:P]
                return nc.gpsimd.affine_select(out=buf, in_=buf, compare_op=ALU.is_ge, fill=0.0, base=0,
                                               pattern=[[0, n], [1, P]] if n > 1 else [[1, P]], channel_multiplier=-1)

            mul = lambda out, a, b: nc.gpsimd.tensor_tensor(out, a, b, ALU.mult)

            def prep_sq(b, k):
                ve["prep"].wait(pool, b, "qk1")
                pe["prep"].wait(pool, b - 1, f"st{NT - 1}")
                pl["prep"].done(mul(qk2, qk[:, :, :, :], qk[:, :, :, :]), "sq")

            def prep_lo(b, k):
                ve["prep"].wait(pool, b, "hi_k")
                for s, name in enumerate(("lo_q", "lo_k")):
                    pl["prep"].done(nc.gpsimd.tensor_tensor(lo_parts[s], qk_twice[s], hi_parts[s], ALU.subtract), name)

            def route_xw(b, k):
                ve["fin"].wait(pool, b, f"x1_{NT - 1}")
                pl["route"].done(mul(r1[:, :, :], x1[:, k, :, 0:D], rw_row[:, None, :].to_broadcast([P, NT, D])), "xw")

            def mod_zb(q, _):
                ve["late"].wait(pool, q - 1, "z1")
                ve["route"].wait(pool, Batch(q, 1), "coef")
                for k in range(2):
                    pl["mod"].done(mul(z_base[:, k], x1[:, k, :, 0:D], coef[:, k, :, None].to_broadcast([P, NT, D])),
                                   f"zb{k}")

            def mod_kw(q, _):
                ve["mod"].wait(pool, q, "qkT")
                pe["mod"].wait(pool, q - 1, "PV")
                for k in range(2):
                    pl["mod"].done(mul(
                        k_wide[:, k], qkT[:, 1, None, SLOTS * k:SLOTS * k + SLOTS].to_broadcast([P, H, SLOTS]),
                        head_of[:, :, None].to_broadcast([P, H, SLOTS])), f"kw{k}")

            def mod_gelu(q, _):
                ve["mod"].wait(pool, q, "h")
                pl["mod"].done(mul(hq[:, :], hb[:, :], hb[:, :]), "hh")
                pe["late"].wait(pool, q - 1, "w2")
                ve["mod"].wait(pool, q, "hp")
                pl["mod"].done(mul(hu[:, :], hq[:, :], hb[:, :]), "hu")

            table = {"prep.sq": prep_sq, "prep.lo": prep_lo, "route.w": route_xw, "mod.zb": mod_zb, "mod.qkT": mod_kw,
                     "mod.w1": mod_gelu}

            def body(p):
                for s in range(16):
                    g = group(p, s, 1)
                    if g:
                        b, _, gi = g
                        pool.wait_ge(exp_done, b.no * 8 + (gi + 1))
                        nc.gpsimd.tensor_tensor(pool_mark[:, gi:gi + 1], head_of[:, 0:1], head_of[:, 0:1], ALU.mult)
                        causal(gi, 0, 1, 0, P)
                        causal(gi, 0, 2, 384, P)
                        causal(gi, 0, 3, 1024, 256)
                        causal(gi, 0, 2, 1920, P).then_inc(masked, 1)
                    for half in range(2):
                        run_side(table, p, s, half)
            iterations(pool, body, 3, PAIRS - 2)

        @block.scalar
        def _(act):
            act.wait_ge(setup_ve, SETUP_RED)
            nc.scalar.activation(turn[:, :, :, :], red[:, :, :, :], ACT.Sin).then_inc(setup_act, 1)

            def mod_exp(q, _):
                ve["mod"].wait(act, q, "sub1")
                nc.scalar.activation(pm[:, :, 0:KSEL], pm[:, :, 0:KSEL], ACT.Exp).then_inc(probs_ready, 1)

            def mod_tanh(q, _):
                pl["mod"].wait(act, q, "hu")
                nc.scalar.activation(hq[:, :], hu[:, :], ACT.Tanh, scale=float(np.sqrt(2.0 / np.pi)))\
                    .then_inc(gate_ready, 1)

            table = {"mod.exp": mod_exp, "mod.tanh": mod_tanh}

            def body(p):
                for s in range(16):
                    g = group(p, s)
                    if g:
                        b, _, gi = g
                        for u, (c0, c1) in enumerate(UNIT):
                            act.wait_ge(scores_ready, b.no * 16 + (2 * gi + u + 1))
                            if gi >= 2 or b.at_least(1):
                                act.wait_ge(exp_done, b.no * 8 + (gi - 1))
                            nc.scalar.activation(th[:, gi % 2, c0:c1], ps_s[:, c0:c1], ACT.Tanh,
                                                 scale=1.0 / (QK_SCALE ** 2 * DH ** 0.5 * SOFTCAP))\
                                .then_inc(tanh_done, 1)
                    for half in range(2):
                        run_side(table, p, s, half)
                    g = group(p, s, 1)
                    if g:
                        b, _, gi = g
                        act.wait_ge(tanh_done, b.no * 16 + (2 * gi + 2))
                        if gi >= 4 or b.at_least(1):
                            act.wait_ge(pv_done, b.no * 4 + (gi // 2 - 1))
                        nc.scalar.activation(pr[:, gi % 4, :], th[:, gi % 2, :], ACT.Exp, scale=SOFTCAP)\
                            .then_inc(exp_done, 1)
            iterations(act, body, 2, PAIRS - 1)

        @block.vector
        def _(v):
            count = [0]

            def setup(ins):
                count[0] += 1
                ins.then_inc(setup_ve, 1)
                v.wait_ge(setup_ve, count[0])

            v.wait_ge(weights_in, 16 * 15)
            v.wait_ge(const_ready, 16)
            v.wait_ge(zeroed, 4)
            for half in range(2):
                for s in range(2):
                    setup(nc.vector.tensor_copy(
                        wo_perm[:, 64 * half:64 * half + 64].rearrange("p (j a s d) -> p s j a d", j=2, a=2, s=2)[:, s],
                        w_raw[:, 3, 64 * half:64 * half + 64].rearrange("p (a s j d) -> p s j a d", j=2, a=2, s=2)[:, s]))
            setup(nc.vector.tensor_copy(rw_wide, rw_col[:, 0:1].to_broadcast([P, P])))
            setup(nc.vector.tensor_copy(pos_f[:, :], pos_i[:, :]))
            for i in range(DH // 2):
                setup(nc.vector.memset(inv[:, i:i + 1], float(np.float32(1.0 / ROPE_BASE ** (2 * i / DH)))))
            v.wait_ge(setup_pe, 1)
            setup(nc.vector.tensor_copy(wT[:, :, :], ps_a[:, :].rearrange("p (t d) -> p t d", t=4)))
            v.wait_ge(setup_pe, 2)
            setup(nc.vector.tensor_copy(rw_row[:, :], ps_m[:, 0:P]))
            setup(nc.vector.tensor_copy(rb[:, :], ps_m[:, 256:257]))
            setup(nc.vector.tensor_tensor(angle[:, :, :], ps_m[:, P:P + NPC, None].to_broadcast([P, NPC, 4]),
                                          inv[:, None, :].to_broadcast([P, NPC, 4]), ALU.mult))
            for i, quarter in enumerate((0.25, 0.0)):
                setup(nc.vector.tensor_scalar(turn_i[:, i], angle[:, :, :], 1.0 / (2 * np.pi), quarter,
                                              ALU.mult, ALU.add))
            setup(nc.vector.tensor_copy(turn[:, :, :, :], turn_i[:, :, :, :]))
            c1 = 6.28125
            c2 = float(np.float32(np.floor((2 * np.pi - c1) * 2 ** 20) / 2 ** 20))
            c3 = float(2 * np.pi - c1 - c2)
            for i in range(2):
                setup(nc.vector.scalar_tensor_tensor(red[:, i], turn[:, i], -c1, angle[:, :, :], ALU.mult, ALU.add))
                setup(nc.vector.scalar_tensor_tensor(red[:, i], turn[:, i], -c2, red[:, i], ALU.mult, ALU.add))
                setup(nc.vector.scalar_tensor_tensor(red[:, i], turn[:, i], -c3, red[:, i], ALU.mult, ALU.add))
            setup(nc.vector.tensor_scalar(red[:, 0], red[:, 0], float(np.pi / 2), None, ALU.add))
            setup(nc.vector.tensor_scalar(red[:, :, :, :], red[:, :, :, :], 3.1415925, -3.1415925, ALU.min, ALU.max))
            assert count[0] == SETUP_RED, count[0]
            v.wait_ge(setup_act, 1)
            for i in range(2):
                setup(nc.vector.tensor_copy(trig[:, :, 4 * i:4 * i + 4], turn[:, 0]))
            setup(nc.vector.tensor_scalar(trig[:, :, 8:12], turn[:, 1], -1.0, None, ALU.mult))
            setup(nc.vector.tensor_copy(trig[:, :, 12:16], turn[:, 1]))
            assert count[0] == SETUP_ALL, count[0]

            def chain(track, unit):
                def step(make, name, after=None):
                    i = track.names.index(name)
                    prev = after or (track.names[i - 1] if i else None)
                    if prev:
                        track.wait(v, unit, prev)
                    track.done(make(), name)
                return step

            def rsqrt(step, name, buf, src, mul, eps, shape_of=lambda a: a):
                var, y, t = buf[:, 0], buf[:, 1], buf[:, 2]
                step(lambda: nc.vector.tensor_scalar(var, src, mul, eps, ALU.mult, ALU.add), f"{name}_var")
                step(lambda: nc.vector.tensor_scalar(y.bitcast(I32), var.bitcast(I32), -0.5, RSQRT_GUESS,
                                                     ALU.mult, ALU.add), f"{name}_guess")
                for i in range(3):
                    step(lambda: nc.vector.tensor_tensor(t, y, y, ALU.mult), f"{name}_a{i}")
                    step(lambda: nc.vector.scalar_tensor_tensor(t, t, -0.5, var, ALU.mult, ALU.mult), f"{name}_b{i}")
                    step(lambda: nc.vector.scalar_tensor_tensor(y, t, 1.5, y, ALU.add, ALU.mult), f"{name}_c{i}")

            def prep_xT(b, k):
                pe["prep"].wait(v, b, "xT")
                pe["prep"].wait(v, b - 1, "v")
                ve["prep"].done(nc.vector.tensor_copy(xT[:, :], ps_a[:, :]), "xT")

            def prep_qk(b, k, i):
                pe["prep"].wait(v, b, f"qk{i}")
                pl["prep"].wait(v, b - 1, "lo_k")
                ve["prep"].done(nc.vector.tensor_copy(
                    qk[:, :, 2 * i:2 * i + 2, :].rearrange("p s t d -> p t s d"),
                    ps_a[:, :].rearrange("p (t s d) -> p t s d", t=2, s=2)), f"qk{i}")

            def prep_v(b, k):
                pe["prep"].wait(v, b, "v")
                if b.at_least(2):
                    v.wait_ge(pv_done, (b - 1).no * 4)
                for s in range(2):
                    o = v_aug[:, k].rearrange("p t (g s j) c -> p s (t g) j c", g=4, s=2)
                    i = ps_a[:, :].rearrange("p (n s j d) -> p s n j d", s=2, j=2, d=DH)
                    ve["prep"].done(nc.vector.tensor_copy(o[:, s, :, :, 16 * s:16 * s + DH], i[:, s]), f"v{'ab'[s]}")

            def prep_norm(b, k):
                step = chain(ve["prep"], b)
                pl["prep"].wait(v, b, "sq")
                step(lambda: nc.vector.tensor_reduce(
                    qn_v[:, 2], qk2.rearrange("p s t (h d) -> p (s t h) d", d=DH), AX.X, ALU.add), "ss")
                rsqrt(step, "qkr", qn_v, qn_v[:, 2], 1.0 / (DH * QK_SCALE ** 2), EPS_QK / QK_SCALE ** 2)
                qf = qk[:, :, :, :].rearrange("p s t (h d) -> p (s t h) d", d=DH)
                step(lambda: nc.vector.tensor_tensor(qf, qf, qn_v[:, 1, :, None].to_broadcast([P, 2 * NT * H, DH]),
                                                     ALU.mult), "qkn")

            def prep_split(b, k):
                step = chain(ve["prep"], b)
                for s, name in enumerate(("hi_q", "hi_k")):
                    step(lambda: nc.vector.tensor_copy(hi_parts[s], qk_twice[s]), name, "qkn")

            def prep_st(b, k, t):
                pe["prep"].wait(v, b, f"st{t}")
                if t == 0 and b.at_least(2):
                    v.wait_ge(scores_ready, (b - 1).no * 16)
                parts = ps_a[:, :].bitcast(F16).rearrange("p (s g q) -> p s g q", s=2, g=4)
                ve["prep"].done(nc.vector.tensor_copy(q_st[:, k, :, P * t:P * t + P], parts[:, 0]), f"qst{t}")
                ve["prep"].done(nc.vector.tensor_copy(k_st[:, k, :, P * t:P * t + P], parts[:, 1]), f"kst{t}")

            def fin_yU(b, half):
                v.wait_ge(pv_done, b.no * 4 + (2 * half + 2))
                if half:
                    pe["fin"].wait(v, b, "y0T")
                else:
                    pe["fin"].wait(v, b - 1, "y1T")
                ve["fin"].done(nc.vector.tensor_copy(y_u[:, :], ps_y[:, :]), f"yU{half}")

            def fin_y(b, half):
                pe["fin"].wait(v, b, f"y{half}T")
                if half == 0:
                    pe["fin"].wait(v, b - 1, "yT")
                rows = ps_m[:, :].rearrange("p (n c) -> p n c", c=16)
                ve["fin"].done(nc.vector.reciprocal(rd[:, :], rows[:, :, DH]), f"rd{half}")
                ve["fin"].wait(v, b, f"rd{half}")
                ve["fin"].done(nc.vector.tensor_tensor(
                    y_tm[:, :, 64 * half:64 * half + 64].rearrange("p t (n d) -> p t n d", d=DH),
                    rows[:, :, 0:DH].rearrange("p (t n) d -> p t n d", t=NT),
                    rd[:, :].rearrange("p (t n) -> p t n", t=NT)[:, :, :, None].to_broadcast([P, NT, 8, DH]),
                    ALU.mult), f"y{half}")

            def fin_yT(b, k):
                pe["fin"].wait(v, b, "yT")
                pe["fin"].wait(v, b - 1, "wo")
                ve["fin"].done(nc.vector.tensor_copy(yT[:, :], ps_m[:, :]), "yT")

            def layer_norm(step, tag, src, st6, m, buf, after):
                for c in range(src.shape[1]):
                    step(lambda: nc.vector.bn_stats(st6[:, c, :], src[:, c, :]), f"bs{c}{tag}", after)
                even, odd = st6[:, :, 1], st6[:, :, 4]
                step(lambda: nc.vector.tensor_tensor(m[:, 0], even, odd, ALU.add), f"sum{tag}")
                step(lambda: nc.vector.tensor_tensor(m[:, 1], even, odd, ALU.subtract), f"dif{tag}", f"bs{src.shape[1] - 1}{tag}")
                step(lambda: nc.vector.tensor_tensor(m[:, 2], st6[:, :, 2], st6[:, :, 5], ALU.add), f"sq{tag}",
                     f"bs{src.shape[1] - 1}{tag}")
                step(lambda: nc.vector.tensor_scalar(m[:, 0], m[:, 0], 0.5, None, ALU.mult), f"mean{tag}", f"sum{tag}")
                step(lambda: nc.vector.tensor_tensor(m[:, 1], m[:, 1], m[:, 1], ALU.mult), f"dif2{tag}", f"dif{tag}")
                step(lambda: nc.vector.scalar_tensor_tensor(m[:, 2], m[:, 1], D / 4.0, m[:, 2], ALU.mult, ALU.add),
                     f"dev{tag}")
                rsqrt(step, f"ln{tag}", buf, m[:, 2], 1.0 / D, EPS_LN)

            def fin_wo(b, k):
                step = chain(ve["fin"], b)
                pe["fin"].wait(v, b, "wo")
                v.wait_ge(x_res_loaded[k], b.pair * 16 + 16)
                ve["route"].wait(v, b - 1, "w")
                step(lambda: nc.vector.tensor_tensor(r1[:, :, :], ps_m[:, :].rearrange("p (t d) -> p t d", t=NT),
                                                     x_res[:, k], ALU.add), "res")

            def fin_ln(b, k):
                step = chain(ve["fin"], b)
                layer_norm(step, "", r1, stats, mv, ln_v, "res")
                pl["mod"].wait(v, b.pair - 1, f"zb{k}")
                for c in range(NT):
                    step(lambda: nc.vector.tensor_scalar(x1[:, k, c, 0:D], r1[:, c, :], mv[:, 0, c:c + 1],
                                                         ln_v[:, 1, c:c + 1], ALU.subtract, ALU.mult),
                         f"x1_{c}", "ln_c2")

            def route_w(b, k):
                step = chain(ve["route"], b)
                pl["route"].wait(v, b, "xw")
                step(lambda: nc.vector.tensor_reduce(x1[:, k, :, D:D + 1], r1[:, :, :], AX.X, ALU.add), "w")
                step(lambda: nc.vector.tensor_scalar(x1[:, k, :, D:D + 1], x1[:, k, :, D:D + 1], rb[:, 0:1], None,
                                                     ALU.add), "w_b")
                pe["route"].wait(v, b - 1, "wrow")
                if k == 0:
                    pe["mod"].wait(v, b.pair - 1, "RT")
                step(lambda: nc.vector.tensor_copy(w_wide[:, :].rearrange("p (t m) -> p t m", t=NT),
                                                   x1[:, k, :, D:D + 1].to_broadcast([P, NT, P])), "wide")

            def route_ge(b, k):
                step = chain(ve["route"], b)
                pe["route"].wait(v, b, "wrow")
                for c in range(NT):
                    step(lambda: nc.vector.tensor_scalar(junk[:, :], ps_m[:, :], x1[:, k, c, D:D + 1], 0.0, ALU.is_ge,
                                                         ALU.add, accum_out=cnt_ge[:, c:c + 1]), f"ge{c}")

            def route_eq(b, k):
                step = chain(ve["route"], b)
                for c in range(NT):
                    n = S - P * c
                    step(lambda: nc.vector.scalar_tensor_tensor(
                        junk[:, 0:n], ps_m[:, P * c:], x1[:, k, c, D:D + 1], later[:, 0:n], ALU.is_equal, ALU.mult,
                        accum_out=cnt_eq[:, c:c + 1]), f"eq{c}")
                step(lambda: nc.vector.tensor_tensor(rank[:, :], cnt_ge[:, :], cnt_eq[:, :], ALU.subtract), "rank")
                pl["mod"].wait(v, b.pair - 1, "zb1")
                step(lambda: nc.vector.tensor_scalar(coef[:, k, :], cnt_ge[:, :], float(KSEL) + 0.5, 1.0, ALU.is_gt,
                                                     ALU.add), "coef")
                pe["mod"].wait(v, b.pair - 1, "msel")
                step(lambda: nc.vector.tensor_tensor(
                    E[:, :, SLOTS * k:SLOTS * k + SLOTS], rank[:, :, None].to_broadcast([P, NT, SLOTS]),
                    slot_no[:, None, :].to_broadcast([P, NT, SLOTS]), ALU.is_equal), "E")

            def copy_step(track, name, make, also=()):
                def run(q, _):
                    pe[track].wait(v, q, name)
                    for other, unit, n in also:
                        other.wait(v, unit(q), n)
                    ve[track].done(make(), name)
                return run

            def mod_gather(q, _):
                pe["mod"].wait(v, q, "gather")
                ve["late"].wait(v, q - 1, "proc")
                ve["mod"].done(nc.vector.tensor_copy(xs[:, :], ps_m[:, 0:D + 1 + 2 * DH]), "xs")

            mod_ET = copy_step("mod", "ET", lambda: nc.vector.tensor_copy(ET[:, :], ps_m[:, :]),
                               [(pe["late"], lambda q: q - 1, "sc1")])
            mod_R = copy_step("mod", "R", lambda: nc.vector.tensor_copy(R[:, :], ps_m[:, :]),
                              [(pe["route"], lambda q: Batch(q, 1), "wrow")])

            def mod_rms(q, _):
                step = chain(ve["mod"], q)
                step(lambda: nc.vector.tensor_tensor_reduce(hn[:, :], xs[:, 0:D], xs[:, 0:D], 1.0, 0.0, ALU.mult,
                                                            ALU.add, sel_ss[:, :]), "ss")
                rsqrt(step, "r1", sel_v, sel_ss[:, :], 1.0 / D, EPS_RMS)
                step(lambda: nc.vector.tensor_scalar(hn[:, :], xs[:, 0:D], sel_v[:, 1], None, ALU.mult), "hn")

            mod_RT = copy_step("mod", "RT", lambda: nc.vector.tensor_copy(
                RT[:, :, :], ps_m[:, :].rearrange("p (c s) -> p c s", c=NT)))
            mod_hnT = copy_step("mod", "hnT", lambda: nc.vector.tensor_scalar(
                hnT[:, :, :, :], ps_m[:, 0:P].rearrange("p (k s) -> p k s", k=2)[:, :, None, :]
                .to_broadcast([P, 2, 2, SLOTS]), g1[:, 0:1], None, ALU.mult))

            def mod_qkv(q, _):
                step = chain(ve["mod"], q)
                pe["mod"].wait(v, q, "qkv")
                t = ps_m[:, 0:2 * D].rearrange("p (h d) -> p h d", d=DH)
                cos = xs[:, D + 1:D + 1 + DH]
                sin = xs[:, D + 1 + DH:D + 1 + 2 * DH]
                step(lambda: nc.vector.tensor_tensor(t_cos, t, cos[:, None, :].to_broadcast([P, 2 * H, DH]),
                                                     ALU.mult), "cosp")
                for i in range(2):
                    step(lambda: nc.vector.tensor_tensor(
                        t_sin[:, :, 4 * i:4 * i + 4], t[:, :, 4 - 4 * i:8 - 4 * i],
                        sin[:, None, 4 * i:4 * i + 4].to_broadcast([P, 2 * H, 4]), ALU.mult), f"sin{i}", "hnT")
                step(lambda: nc.vector.tensor_tensor(qk_r[:, :].rearrange("p (h d) -> p h d", d=DH), t_cos,
                                                     t_sin, ALU.add), "rope")
                for k in range(2):
                    step(lambda: nc.vector.tensor_tensor(
                        vv[:, :, k, :], ps_m[:, 2 * D + D * k:3 * D + D * k].rearrange("p (n c) -> p n c", n=H // 2),
                        half_of[:, :, :].rearrange("p a d -> p (a d)")[:, None, :].to_broadcast([P, H // 2, 2 * DH]),
                        ALU.mult), f"vv{k}", "hnT")

            mod_msel = copy_step("mod", "msel", lambda: nc.vector.tensor_copy(msel[:, :], ps_m[:, 0:SLOTS]))
            mod_qkT = copy_step("mod", "qkT", lambda: nc.vector.tensor_copy(
                qkT[:, :, :], ps_m[:, 0:2 * P].rearrange("p (s c) -> p s c", s=2)))

            def mod_S(q, h):
                step = chain(ve["mod"], q)
                pe["mod"].wait(v, q, f"S{h}")
                step(lambda: nc.vector.scalar_tensor_tensor(
                    sc[:, :, :], ps_m[:, :].rearrange("p (h s) -> p h s", h=8), float(DH ** -0.5),
                    msel[:, None, :].to_broadcast([P, 8, SLOTS]), ALU.mult, ALU.add), f"sc{h}")
                step(lambda: nc.vector.tensor_reduce(mx[:, :], sc[:, :, 0:KSEL], AX.X, ALU.max), f"mx{h}")
                step(lambda: nc.vector.tensor_tensor(
                    pm[:, 8 * h:8 * h + 8, 0:KSEL], sc[:, :, 0:KSEL], mx[:, :, None].to_broadcast([P, 8, KSEL]),
                    ALU.subtract), f"sub{h}")

            def mod_P(q, h):
                step = chain(ve["mod"], q)
                if h == 0:
                    v.wait_ge(probs_ready, q + 1)
                    step(lambda: nc.vector.tensor_reduce(den[:, :], pm[:, :, 0:KSEL], AX.X, ALU.add), "den")
                    step(lambda: nc.vector.reciprocal(rden[:, :], den[:, :]), "rden")
                pe["mod"].wait(v, q, f"P{h}T")
                step(lambda: nc.vector.tensor_copy(PT[:, 4 * h:4 * h + 4, :],
                                                   ps_m[:, :].rearrange("p (n s) -> p n s", n=4)), f"PT{h}")

            def mod_PV(q, _):
                step = chain(ve["mod"], q)
                pe["mod"].wait(v, q, "PV")
                for k in range(2):
                    rows = slice(SLOTS * k, SLOTS * k + SLOTS)
                    step(lambda: nc.vector.tensor_tensor(
                        o_tm[rows], ps_m[rows, 0:2 * D].rearrange("p (n k a d) -> p k n a d", n=H // 2, k=2, a=2)[:, k],
                        rden[rows, :].rearrange("p (n a) -> p n a", a=2)[:, :, :, None]
                        .to_broadcast([SLOTS, H // 2, 2, DH]), ALU.mult), f"o{k}", "PT1")

            mod_oT = copy_step("mod", "oT", lambda: nc.vector.tensor_copy(oT[:, :], ps_m[:, 0:P]))

            def mod_wo(q, _):
                step = chain(ve["mod"], q)
                pe["mod"].wait(v, q, "wo")
                step(lambda: nc.vector.tensor_tensor(x1f[:, :], xs[:, 0:D], ps_m[:, 0:D], ALU.add), "x1f")
                step(lambda: nc.vector.tensor_tensor_reduce(hn[:, :], x1f[:, :], x1f[:, :], 1.0, 0.0, ALU.mult,
                                                            ALU.add, sel_ss[:, :]), "ss2")
                rsqrt(step, "r2", sel_v, sel_ss[:, :], 1.0 / D, EPS_RMS)
                step(lambda: nc.vector.tensor_scalar(hn[:, :], x1f[:, :], sel_v[:, 1], None, ALU.mult), "hn2")

            mod_h2T = copy_step("mod", "h2T", lambda: nc.vector.tensor_scalar(
                h2T[:, :], ps_m[:, 0:P], g2[:, 0:1], None, ALU.mult))

            def mod_w1(q, _):
                pe["mod"].wait(v, q, "w1")
                ve["mod"].done(nc.vector.tensor_copy(hb[:, :], ps_m[:, :]), "h")
                pl["mod"].wait(v, q, "hh")
                ve["mod"].done(nc.vector.tensor_scalar(hq[:, :], hq[:, :], 0.044715, 1.0, ALU.mult, ALU.add), "hp")

            def mod_gate(q, _):
                v.wait_ge(gate_ready, q + 1)
                ve["mod"].done(nc.vector.scalar_tensor_tensor(hu[:, :], hq[:, :], 1.0, hb[:, :], ALU.add, ALU.mult), "g")

            def late_w2(q, _):
                step = chain(ve["late"], q)
                mod_gate(q, _)
                pe["late"].wait(v, q, "w2")
                step(lambda: nc.vector.scalar_tensor_tensor(x2[:, :], ps_m[:, 0:D], 0.5, x1f[:, :], ALU.mult, ALU.add),
                     "x2")
                step(lambda: nc.vector.tensor_scalar(proc[:, :], x2[:, :], xs[:, D:D + 1], None, ALU.mult), "proc")

            def late_sc(q, k):
                pe["late"].wait(v, q, f"sc{k}")
                pl["mod"].wait(v, q, f"zb{k}")
                if not isinstance(q, int) or q >= 1:
                    v.wait_ge(out_stored[k], q * 16)
                ve["late"].done(nc.vector.tensor_tensor(y_out[:, k], ps_m[:, :].rearrange("p (t d) -> p t d", t=NT),
                                                        z_base[:, k], ALU.add), f"z{k}")

            zz = y_out[:, :, :, :].rearrange("p k t d -> p (k t) d")

            def late_stats(q, _):
                layer_norm(chain(ve["late"], q), "_", zz, stats2, mv2, lo_v, "z1")

            def late_norm(q, _):
                step = chain(ve["late"], q)
                for c in range(2 * NT):
                    step(lambda: nc.vector.tensor_scalar(zz[:, c, :], zz[:, c, :], mv2[:, 0, c:c + 1],
                                                         lo_v[:, 1, c:c + 1], ALU.subtract, ALU.mult),
                         f"o{c}_", "ln__c2")

            table = {"prep.xT": prep_xT, "prep.qk0": lambda b, k: prep_qk(b, k, 0),
                     "prep.qk1": lambda b, k: prep_qk(b, k, 1), "prep.v": prep_v, "prep.norm": prep_norm,
                     "prep.split": prep_split,
                     **{f"prep.st{t}": (lambda b, k, t=t: prep_st(b, k, t)) for t in range(NT)},
                     "fin.yU0": lambda b, k: fin_yU(b, 0), "fin.yU1": lambda b, k: fin_yU(b, 1),
                     "fin.y0": lambda b, k: fin_y(b, 0), "fin.y1": lambda b, k: fin_y(b, 1),
                     "fin.yT": fin_yT, "fin.wo": fin_wo, "fin.ln": fin_ln, "route.w": route_w, "route.ge": route_ge,
                     "route.eq": route_eq, "mod.gather": mod_gather, "mod.ET": mod_ET, "mod.R": mod_R,
                     "mod.rms": mod_rms, "mod.RT": mod_RT, "mod.hnT": mod_hnT, "mod.qkv": mod_qkv,
                     "mod.msel": mod_msel, "mod.qkT": mod_qkT, "mod.S0": lambda q, _: mod_S(q, 0),
                     "mod.S1": lambda q, _: mod_S(q, 1), "mod.P0": lambda q, _: mod_P(q, 0),
                     "mod.P1": lambda q, _: mod_P(q, 1), "mod.PV": mod_PV, "mod.oT": mod_oT, "mod.wo": mod_wo,
                     "mod.h2T": mod_h2T, "mod.w1": mod_w1, "late.w2": late_w2,
                     "late.sc0": lambda q, _: late_sc(q, 0), "late.sc1": lambda q, _: late_sc(q, 1),
                     "late.stats": late_stats, "late.norm": late_norm}

            def body(p):
                for s in range(16):
                    for half in range(2):
                        run_side(table, p, s, half)
            iterations(v, body, 3, PAIRS - 2)

        @block.tensor
        def _(t_):
            mm = nc.tensor.matmul
            tr = nc.tensor.transpose
            t_.wait_ge(const_ready, 16)
            t_.wait_ge(weights_in, 16 * 15)
            t_.wait_ge(setup_ve, 10)
            for i in range(4):
                last = tr(ps_a[:, P * i:P * i + P], w_raw[:, i, :] if i < 3 else wo_perm, ident[:, :])
            last.then_inc(setup_pe, 1)
            tr(ps_m[:, 0:P], rw_wide, ident[:, :])
            tr(ps_m[:, P:P + NPC], pos_f[:, :], ident[0:NPC, 0:NPC])
            mm(ps_m[:, 256:257], ones1[:, :], rb_one[:, :], start=True, stop=True).then_inc(setup_pe, 1)
            t_.wait_ge(setup_ve, SETUP_ALL)

            def scores(b, k, gi, u):
                if gi > 0 or b.at_least(1):
                    t_.wait_ge(tanh_done, b.no * 16 + (2 * gi + u - 1))
                for hb_, kb in UNIT_BLOCKS[u]:
                    g, j = 2 * (gi // 4) + hb_, gi % 4
                    c = COL[(hb_, kb)]
                    last = mm(ps_s[:, c:c + S - P * kb], k_st[32 * j:32 * j + 32, k, g, P * kb:P * kb + P],
                              q_st[32 * j:32 * j + 32, k, g, P * kb:S], start=True, stop=True)
                last.then_inc(scores_ready, 1)

            def pv(b, k, q):
                t_.wait_ge(masked, b.no * 8 + (2 * q + 2))
                if q % 2 == 0:
                    ve["fin"].wait(t_, b if q else b - 1, "yU0" if q else "yU1")
                for kb in range(NT):
                    for j in range(4):
                        ab, gi = j % 2, 2 * q + j // 2
                        h = 8 * (q // 2) + 4 * ab + gi % 4
                        c = COL[(ab, kb)]
                        last = mm(ps_y[32 * j:32 * j + 32, P * kb:S], v_aug[:, k, kb, h, :],
                                  pr[:, gi % 4, c:c + S - P * kb], start=(q % 2 == 0 and kb == 0),
                                  stop=(q % 2 == 1 and kb == 3), skip_group_check=True)
                last.then_inc(pv_done, 1)

            def four(src, track, name, idn=None):
                for c in range(4):
                    last = tr(ps_m[:, P * c:P * c + P], src(c), ident[:, :])
                track.done(last, name)

            def prep_xT(b, k):
                t_.wait_ge(x_in_loaded[k], b.pair * 16 + 16)
                ve["prep"].wait(t_, b - 1, f"kst{NT - 1}")
                for c in range(NT):
                    last = tr(ps_a[:, P * c:P * c + P], x_in[:, k, c, :], ident[:, :])
                pe["prep"].done(last, "xT")

            def prep_qk(b, k, i):
                ve["prep"].wait(t_, b, "qk0" if i else "xT")
                for t in range(2 * i, 2 * i + 2):
                    last = mm(ps_a[:, 2 * D * (t % 2):2 * D * (t % 2) + 2 * D], xT[:, P * t:P * t + P],
                              wT[:, 0:2, :].rearrange("p a d -> p (a d)"), start=True, stop=True)
                pe["prep"].done(last, f"qk{i}")

            def prep_v(b, k):
                ve["prep"].wait(t_, b, "qk1")
                for t in range(NT):
                    last = mm(ps_a[:, P * t:P * t + P], xT[:, P * t:P * t + P], wT[:, 2, :], start=True, stop=True)
                pe["prep"].done(last, "v")

            def prep_st(b, k, t):
                ve["prep"].wait(t_, b, "vb" if t == 0 else f"kst{t - 1}")
                if t == 0:
                    pl["prep"].wait(t_, b, "lo_k")
                dst = ps_a[:, :].bitcast(F16)
                for s in range(2):
                    for g in range(4):
                        c = (4 * s + g) * P
                        last = tr(dst[:, c:c + P], st[:, s, t, 4 * g:4 * g + 4].rearrange("p h c d -> p (h c d)"),
                                  ident16[:, :])
                pe["prep"].done(last, f"st{t}")

            def fin_y(b, half, k):
                ve["fin"].wait(t_, b, f"yU{half}")
                if half:
                    ve["fin"].wait(t_, b, "y0")
                    ve["mod"].wait(t_, b.pair - 1, "PT1" if k else "R")
                else:
                    ve["route"].wait(t_, b - 1, f"eq{NT - 1}")
                    ve["mod"].wait(t_, b.pair - (1 if k else 2), "qkT" if k else "h")
                four(lambda c: y_u[:, P * c:P * c + P], pe["fin"], f"y{half}T")

            def fin_yT(b, k):
                ve["fin"].wait(t_, b, "y1")
                if k:
                    ve["mod"].wait(t_, b.pair - 1, "o1")
                four(lambda c: y_tm[:, c, :], pe["fin"], "yT")

            def fin_wo(b, k):
                ve["fin"].wait(t_, b, "yT")
                for c in range(NT):
                    last = mm(ps_m[:, P * c:P * c + P], yT[:, P * c:P * c + P], wT[:, 3, :], start=True, stop=True)
                pe["fin"].done(last, "wo")

            def route_wrow(b, k):
                ve["route"].wait(t_, b, "wide")
                ve["mod"].wait(t_, b.pair - 1, "h2T" if k else "msel")
                four(lambda c: w_wide[:, P * c:P * c + P], pe["route"], "wrow")

            def trig_row(b):
                return min(b.no, MASKS - 1) if isinstance(b.no, int) else MASKS - 1

            def mod_gather(q, _):
                ve["route"].wait(t_, Batch(q, 1), "E")
                ve["fin"].wait(t_, Batch(q, 2), "y0")
                ve["late"].wait(t_, q - 1, "z1")
                for k in range(2):
                    rows = slice(SLOTS * k, SLOTS * k + SLOTS)
                    for c in range(NT):
                        mm(ps_m[rows, 0:D + 1], E[:, c, rows], x1[:, k, c, :], start=(c == 0), stop=(c == NT - 1))
                    for c in range(NT):
                        last = mm(ps_m[rows, D + 1:D + 1 + 2 * DH], E[:, c, rows],
                                  trig[:, NT * trig_row(Batch(q, k)) + c, :], start=(c == 0), stop=(c == NT - 1))
                pe["mod"].done(last, "gather")

            def mod_ET(q, _):
                ve["mod"].wait(t_, q, "xs")
                four(lambda c: E[:, c, :], pe["mod"], "ET")

            def mod_R(q, _):
                ve["mod"].wait(t_, q, "ET")
                t_.wait_ge(mask_loaded, {0: 32, 1: 64}.get(q, 80) if isinstance(q, int) else 80)
                for c in range(NT):
                    for k in range(2):
                        last = mm(ps_m[SLOTS * k:SLOTS * k + SLOTS, :], E[:, c, SLOTS * k:SLOTS * k + SLOTS],
                                  masks[:, k, c, :], start=(c == 0), stop=(c == NT - 1))
                pe["mod"].done(last, "R")

            def mod_RT(q, _):
                ve["mod"].wait(t_, q, "R")
                ve["fin"].wait(t_, Batch(q, 2), "res")
                four(lambda c: R[:, P * c:P * c + P], pe["mod"], "RT")

            def mod_hnT(q, _):
                ve["mod"].wait(t_, q, "RT")
                pe["mod"].done(tr(ps_m[:, 0:P], hn[:, :], ident[:, :]), "hnT")

            def mod_qkv(q, _):
                ve["mod"].wait(t_, q, "hnT")
                mm(ps_m[:, 0:2 * D], hnT[:, :, :, :].rearrange("p k a s -> p (k a s)")[:, SLOTS:3 * SLOTS],
                   wqkv2[:, 0:2, :].rearrange("p a d -> p (a d)"), start=True, stop=True)
                for k in range(2):
                    last = mm(ps_m[:, D * (2 + k):D * (3 + k)], hnT[:, k, :, :].rearrange("p a s -> p (a s)"),
                              wqkv2[:, 2, :], start=True, stop=True)
                pe["mod"].done(last, "qkv")

            def mod_msel(q, _):
                ve["mod"].wait(t_, q, "vv1")
                for k in range(2):
                    rows = slice(SLOTS * k, SLOTS * k + SLOTS)
                    for c in range(NT):
                        last = mm(ps_m[rows, 0:SLOTS], RT[:, c, rows], E[:, c, rows], start=(c == 0),
                                  stop=(c == NT - 1))
                pe["mod"].done(last, "msel")

            def mod_qkT(q, _):
                ve["mod"].wait(t_, q, "msel")
                ve["route"].wait(t_, Batch(q, 2), f"eq{NT - 1}")
                for s in range(2):
                    last = tr(ps_m[:, P * s:P * s + P], qk_r[:, D * s:D * s + D], ident[:, :])
                pe["mod"].done(last, "qkT")

            def mod_S(q, h):
                if h:
                    ve["mod"].wait(t_, q, "sc0")
                else:
                    pl["mod"].wait(t_, q, "kw1")
                    ve["fin"].wait(t_, Batch(q, 3), "y0")
                for k in range(2):
                    rows = slice(SLOTS * k, SLOTS * k + SLOTS)
                    last = mm(ps_m[rows, :], qkT[:, 0, rows],
                              k_wide[:, k, 8 * h:8 * h + 8, :].rearrange("p h s -> p (h s)"), start=True, stop=True)
                pe["mod"].done(last, f"S{h}")

            def mod_P(q, h):
                if h:
                    ve["mod"].wait(t_, q, "PT0")
                else:
                    t_.wait_ge(probs_ready, q + 1)
                    ve["mod"].wait(t_, q, "sc1")
                four(lambda c: pm[:, 8 * h + 2 * c:8 * h + 2 * c + 2, :].rearrange("p a s -> p (a s)"), pe["mod"],
                     f"P{h}T")

            def mod_PV(q, _):
                ve["mod"].wait(t_, q, "PT1")
                ve["fin"].wait(t_, Batch(q, 3), "y1")
                for n in range(H // 2):
                    last = mm(ps_m[:, 32 * n:32 * n + 32], PT[:, n, :], vv[:, n, :, :].rearrange("p k c -> p (k c)"),
                              start=True, stop=True)
                pe["mod"].done(last, "PV")

            def mod_oT(q, _):
                ve["mod"].wait(t_, q, "o1")
                ve["fin"].wait(t_, Batch(q, 3), "res")
                pe["mod"].done(tr(ps_m[:, 0:P], o_tm[:, :, :, :].rearrange("p n a d -> p (n a d)"), ident[:, :]), "oT")

            def mod_wo(q, _):
                ve["mod"].wait(t_, q, "oT")
                pe["mod"].done(mm(ps_m[:, 0:D], oT[:, :], wo2[:, :], start=True, stop=True), "wo")

            def mod_h2T(q, _):
                ve["mod"].wait(t_, q, "hn2")
                pe["mod"].done(tr(ps_m[:, 0:P], hn[:, :], ident[:, :]), "h2T")

            def mod_w1(q, _):
                ve["mod"].wait(t_, q, "h2T")
                ve["route"].wait(t_, Batch(q, 3), f"eq{NT - 1}")
                for c in range(F // P):
                    last = mm(ps_m[:, P * c:P * c + P], w1_sb[:, P * c:P * c + P], h2T[:, :], start=True, stop=True)
                pe["mod"].done(last, "w1")

            def late_w2(q, _):
                ve["mod"].wait(t_, q, "g")
                ve["fin"].wait(t_, Batch(q, 4), "y0")
                for c in range(F // P):
                    last = mm(ps_m[:, 0:D], hu[:, P * c:P * c + P], w2_sb[:, c, :], start=(c == 0),
                              stop=(c == F // P - 1))
                pe["late"].done(last, "w2")

            def late_sc(q, k):
                ve["late"].wait(t_, q, "z0" if k else "proc")
                rows = slice(SLOTS * k, SLOTS * k + SLOTS)
                for c in range(NT):
                    last = mm(ps_m[:, P * c:P * c + P], ET[rows, P * c:P * c + P], proc[rows, :], start=True, stop=True)
                pe["late"].done(last, f"sc{k}")

            table = {"prep.xT": prep_xT, "prep.qk0": lambda b, k: prep_qk(b, k, 0),
                     "prep.qk1": lambda b, k: prep_qk(b, k, 1), "prep.v": prep_v,
                     **{f"prep.st{t}": (lambda b, k, t=t: prep_st(b, k, t)) for t in range(NT)},
                     "fin.y0": lambda b, k: fin_y(b, 0, k), "fin.y1": lambda b, k: fin_y(b, 1, k),
                     "fin.yT": fin_yT, "fin.wo": fin_wo, "route.ge": route_wrow, "mod.gather": mod_gather,
                     "mod.ET": mod_ET, "mod.R": mod_R, "mod.RT": mod_RT, "mod.hnT": mod_hnT, "mod.qkv": mod_qkv,
                     "mod.msel": mod_msel, "mod.qkT": mod_qkT, "mod.S0": lambda q, _: mod_S(q, 0),
                     "mod.S1": lambda q, _: mod_S(q, 1), "mod.P0": lambda q, _: mod_P(q, 0),
                     "mod.P1": lambda q, _: mod_P(q, 1), "mod.PV": mod_PV, "mod.oT": mod_oT, "mod.wo": mod_wo,
                     "mod.h2T": mod_h2T, "mod.w1": mod_w1, "late.w2": late_w2,
                     "late.sc0": lambda q, _: late_sc(q, 0), "late.sc1": lambda q, _: late_sc(q, 1)}

            def body(p):
                for s in range(16):
                    g = group(p, s, -1)
                    if g and g[2] == 0:
                        ve["prep"].wait(t_, g[0], f"kst{NT - 1}")
                    if g:
                        scores(g[0], g[1], g[2], 0)
                    run_side(table, p, s, 0)
                    if g:
                        scores(g[0], g[1], g[2], 1)
                    g = group(p, s, 3)
                    if g and g[2] % 2 == 0:
                        pv(g[0], g[1], g[2] // 2)
                    run_side(table, p, s, 1)
            iterations(t_, body, 3, PAIRS - 2)


SETUP_RED = 25
SETUP_ALL = 29


_INS = ['L0_attn_x', 'L0_attn_w_q', 'L0_attn_w_k', 'L0_attn_w_v', 'L0_attn_w_o', 'L0_ffn_attention_mask',
        'L0_ffn_position_ids', 'L0_ffn_router_w', 'L0_ffn_router_b', 'L0_ffn_wq', 'L0_ffn_wk', 'L0_ffn_wv',
        'L0_ffn_wo', 'L0_ffn_w1', 'L0_ffn_w2', 'L0_ffn_ln1', 'L0_ffn_ln2']


def kernel(**inputs):
    import numpy as _np
    import concourse.bacc as _bacc
    from concourse import mybir as _mybir
    from concourse.bass_utils import run_bass_kernel_spmd as _run

    nc = _bacc.Bacc("TRN2", target_bir_lowering=False, num_devices=1)
    arrays, args = {}, []
    for name in _INS:
        a = _np.ascontiguousarray(inputs[name])
        arrays[f"in_{name}"] = a
        args.append(nc.dram_tensor(f"in_{name}", a.shape, _mybir.dt.from_np(a.dtype), kind="ExternalInput").ap())
    args.append(nc.dram_tensor("result", (16, 512, 128), _mybir.dt.float32, kind="ExternalOutput").ap())
    build(nc, *args)
    r = _run(nc, [arrays], core_ids=[0])
    return r.results[0]["result"]
```

```python
from contextlib import ExitStack

import numpy as np

import concourse.bass as bass
from concourse import mybir

ALU = mybir.AluOpType
ACT = mybir.ActivationFunctionType
AX = mybir.AxisListType
F32 = mybir.dt.float32
F16 = mybir.dt.float16
I32 = mybir.dt.int32

P = 128
B, S, D = 16, 512, 128
H, DH = 16, 8
F = 512
NT = S // P
MASKS = 4
KSEL = int(0.125 * S) - 1
SLOTS = 64
PAIRS = B // 2
SOFTCAP = 50.0
EPS_QK = 1.1920929e-07
EPS_LN = 1e-05
EPS_RMS = 1e-06
QK_SCALE = 64.0
ROPE_BASE = 10000.0
RSQRT_GUESS = 1597463007.0

COL = {(0, 1): 0, (0, 3): 384, (0, 0): 512, (0, 2): 1024, (1, 2): 1280, (1, 1): 1536, (1, 3): 1920, (1, 0): 2048}
GROUP = 5 * 512
UNIT = ((0, 1024), (1024, GROUP))
UNIT_BLOCKS = (((0, 1), (0, 3), (0, 0)), ((0, 2), (1, 2), (1, 1), (1, 3), (1, 0)))


def newton(name, part):
    return [f"{name}_{s}" for s in (("var", "guess", "a0", "b0", "c0") if part == 1 else
                                    ("a1", "b1", "c1", "a2", "b2", "c2"))]


def moments_of(tiles, tag=""):
    return [f"bs{c}{tag}" for c in range(tiles)] + [f"{n}{tag}" for n in ("sum", "dif", "sq", "mean", "dif2", "dev")]


VE_STEPS = {
    "prep": ["xT", "qk0", "qk1", "va", "vb", "ss"] + newton("qkr", 1) + newton("qkr", 2) +
        ["qkn", "hi_q", "hi_k", "qst0", "kst0", "qst1", "kst1", "qst2", "kst2", "qst3", "kst3"],
    "fin": ["yU0", "rd0", "y0", "yU1", "rd1", "y1", "yT", "res"] + moments_of(NT) + newton("ln", 1) +
        newton("ln", 2) + ["x1_0", "x1_1", "x1_2", "x1_3"],
    "route": ["w", "w_b", "wide", "row", "ge0", "ge1", "ge2", "ge3", "eq0", "eq1", "eq2", "eq3", "rank",
        "coef", "E"],
    "sel": ["xs", "ss"] + newton("r1", 1) + newton("r1", 2) +
        ["hn", "ET", "hnT", "cosp", "sin0", "sin1", "rope", "vv0", "vv1", "R", "qkT", "RT", "msel"],
    "att": ["sc0", "mx0", "sub0", "sc1", "mx1", "sub1", "den", "rden", "PT0", "PT1", "o0", "o1", "oT", "x1f",
        "ss2"] + newton("r2", 1) + newton("r2", 2) + ["hn2", "h2T", "h", "hp", "g"],
    "late": ["x2", "proc", "z0", "z1"] + moments_of(2 * NT, "_") + newton("ln_", 1) + newton("ln_", 2) +
        [f"o{c}_" for c in range(2 * NT)],
}
PE_STEPS = {
    "prep": ["xT", "qk0", "qk1", "v", "st0", "st1", "st2", "st3"],
    "fin": ["y0T", "y1T", "yT", "wo"],
    "route": ["wrow"],
    "sel": ["gather", "ET", "hnT", "qkv", "R", "qkT", "RT", "msel"],
    "att": ["S0", "S1", "P0T", "P1T", "PV", "oT", "wo", "h2T", "w1"],
    "late": ["w2", "sc0", "sc1"],
}
POOL_STEPS = {
    "prep": ["sq", "lo_q", "lo_k"],
    "route": ["xw"],
    "sel": ["zb0", "zb1"],
    "att": ["kw0", "kw1", "hh", "hu"],
}


PE_ORDER = (
    ["prep.qk0/1@0", "route.wrow/0@-1"], ["pv.2/1@-1"],
    ["pv.3/1@-1", "att.P0@-2"], ["prep.qk1/1@0"],
    ["att.P1@-2", "prep.v/1@0"], ["fin.y1T/1@-1"],
    ["fin.yT/1@-1"], ["fin.wo/1@-1", "pv.0/0@0"],
    ["att.PV@-2", "prep.xT/0@1"], [],
    ["att.oT@-2", "att.wo@-2", "prep.st0/1@0"], ["att.h2T@-2", "prep.st1/1@0"],
    ["prep.st2/1@0"], ["att.w1@-2", "prep.st3/1@0", "pv.1/0@0"],
    ["route.wrow/1@-1"], ["prep.qk0/0@1", "fin.y0T/0@0", "pv.2/0@0"],
    ["prep.qk1/0@1"], ["late.w2@-2"],
    ["late.sc0@-2", "pv.3/0@0", "prep.v/0@1", "late.sc1@-2"], ["sel.gather@-1"],
    ["fin.y1T/0@0"], ["fin.yT/0@0", "pv.0/1@0", "sel.ET@-1"],
    ["sel.hnT@-1"], ["fin.wo/0@0", "sel.qkv@-1"],
    [], ["prep.st0/0@1", "sel.R@-1", "prep.st1/0@1"],
    ["pv.1/1@0", "sel.qkT@-1"], ["prep.st2/0@1", "sel.RT@-1"],
    ["prep.st3/0@1", "fin.y0T/1@0"], ["sel.msel@-1", "att.S0@-1"],
    ["prep.xT/1@1"], ["att.S1@-1"],
)

VE_ORDER = (
    [], ["route.row/0@-1", "route.ge/0@-1", "route.eq/0@-1"],
    ["prep.qk0/1@0", "att.den@-2", "att.PT0@-2"],
    ["route.rank/0@-1", "prep.qk1/1@0", "att.PT1@-2", "fin.yU1/1@-1"],
    ["fin.y1/1@-1", "prep.v/1@0"],
    ["fin.yT/1@-1", "prep.ss/1@0", "prep.root1/1@0", "fin.res/1@-1", "prep.root2/1@0", "prep.qkn/1@0"],
    [], ["att.o@-2"],
    ["prep.hi/1@0", "att.oT@-2", "prep.xT/0@1", "fin.ln/1@-1"],
    ["att.x1f@-2", "att.ss@-2", "fin.root1/1@-1 & att.root1@-2", "fin.root2/1@-1 & att.root2@-2", "prep.st0/1@0"],
    ["att.hn@-2", "fin.x1/1@-1", "att.h2T@-2", "prep.st1/1@0", "prep.st2/1@0", "late.norm@-3"],
    ["prep.st3/1@0", "att.h@-2"],
    ["route.w/1@-1", "route.row/1@-1", "fin.yU0/0@0", "att.hp@-2", "route.ge/1@-1", "prep.qk0/0@1", "fin.y0/0@0",
     "att.g@-2"],
    ["late.proc@-2", "route.eq/1@-1"],
    ["prep.qk1/0@1"], ["late.z0@-2"],
    ["fin.yU1/0@0", "route.rank/1@-1"], ["late.z1@-2", "prep.v/0@1", "prep.ss/0@1", "sel.xs@-1"],
    ["sel.ss@-1"], ["fin.y1/0@0", "prep.root1/0@1 & sel.root1@-1", "fin.yT/0@0"],
    ["prep.root2/0@1 & sel.root2@-1", "sel.hn@-1"], ["sel.ET@-1", "prep.qkn/0@1", "sel.hnT@-1", "prep.hi/0@1"],
    ["fin.res/0@0", "fin.ln/0@0"], [],
    ["sel.qkv@-1", "late.ln@-2", "prep.st0/0@1"],
    ["fin.root1/0@0 & late.root1@-2", "sel.R@-1", "fin.root2/0@0 & late.root2@-2"],
    ["prep.st1/0@1", "fin.x1/0@0", "sel.qkT@-1"], ["fin.yU0/1@0", "sel.RT@-1", "prep.st2/0@1", "fin.y0/1@0"],
    ["route.w/0@0", "sel.msel@-1"], ["prep.st3/0@1", "att.sc0@-1"],
    [], ["att.mx0@-1", "prep.xT/1@1", "att.sc1@-1", "att.mx1@-1"],
)

POOL_ORDER = (
    [], [],
    [], ["prep.sq/1@0"],
    ["prep.lo/1@0"], [],
    [], [],
    [], [],
    [], [],
    [], ["route.xw/1@-1", "att.hh@-2", "att.hu@-2"],
    [], [],
    [], ["prep.sq/0@1", "sel.zb@-1"],
    [], [],
    [], [],
    [], ["prep.lo/0@1"],
    [], [],
    ["route.xw/0@0"], ["att.kw@-1"],
    [], [],
    [], [],
)

ACT_ORDER = (
    [], [],
    ["att.exp@-2"], [],
    [], [],
    [], [],
    [], [],
    [], [],
    [], [],
    [], [],
    ["att.tanh@-2"], [],
    [], [],
    [], [],
    [], [],
    [], [],
    [], [],
    [], [],
    [], [],
)

BANK_READ = {
    "prep.qk0/0": ["prep.xT/0@0", "prep.kst3/1@-1"],
    "prep.qk0/1": ["prep.xT/1@0"],
    "prep.qk1/0": ["prep.qk0/0@0"],
    "prep.qk1/1": ["prep.qk0/1@0"],
    "prep.st0/0": ["prep.vb/0@0"],
    "prep.st0/1": ["prep.xT/0@1", "prep.vb/1@0"],
    "prep.st1/0": ["prep.kst0/0@0"],
    "prep.st1/1": ["prep.kst0/1@0"],
    "prep.st2/0": ["prep.kst1/0@0"],
    "prep.st2/1": ["prep.kst1/1@0"],
    "prep.st3/0": ["prep.kst2/0@0"],
    "prep.st3/1": ["prep.kst2/1@0"],
    "prep.v/0": ["prep.qk1/0@0"],
    "prep.v/1": ["prep.qk1/1@0"],
    "prep.xT/0": ["prep.vb/1@-1"],
    "prep.xT/1": ["prep.kst3/0@0"],
    "fin.wo/0": ["fin.yT/0@0", "sel.hnT@-1"],
    "fin.wo/1": ["fin.yT/1@0"],
    "fin.y0T/0": ["route.row/1@-1"],
    "fin.y0T/1": ["fin.res/0@0", "sel.RT@-1"],
    "fin.y1T/0": ["fin.y0/0@0", "sel.xs@-1"],
    "fin.y1T/1": ["route.row/0@0", "att.PT1@-1"],
    "fin.yT/0": ["fin.y1/0@0"],
    "fin.yT/1": ["fin.y1/1@0"],
    "route.wrow/0": ["fin.y0/1@0", "att.sc1@-1"],
    "route.wrow/1": ["fin.res/1@0", "att.h@-1"],
    "sel.ET": ["fin.yT/0@1", "sel.xs@0"],
    "sel.R": ["sel.vv1@0"],
    "sel.RT": ["sel.qkT@0"],
    "sel.gather": ["fin.y0/0@1", "late.z1@-1"],
    "sel.hnT": ["sel.ET@0"],
    "sel.msel": ["fin.y0/1@1", "sel.RT@0"],
    "sel.qkT": ["sel.R@0"],
    "sel.qkv": ["fin.res/0@1", "sel.hnT@0"],
    "att.P0": ["route.row/0@1", "att.sc1@0"],
    "att.P1": ["att.PT0@0"],
    "att.PV": ["fin.res/1@1", "att.PT1@0"],
    "att.S0": ["sel.msel@0"],
    "att.S1": ["att.sc0@0"],
    "att.h2T": ["att.x1f@0"],
    "att.oT": ["att.o1@0"],
    "att.w1": ["att.h2T@0"],
    "att.wo": ["att.oT@0"],
    "late.sc0": ["late.x2@0"],
    "late.sc1": ["late.z0@0"],
    "late.w2": ["fin.y0/0@2", "route.row/1@1", "att.h@0"],
}


class Batch:

    def __init__(self, pair, k):
        self.pair, self.k = pair + k // 2, k % 2
        self.no = self.pair * 2 + self.k

    def __add__(self, n):
        return Batch(self.pair, self.k + n)

    def __sub__(self, n):
        return self + -n

    def at_least(self, n):
        return not isinstance(self.no, int) or self.no >= n


class Track:

    def __init__(self, sems, names):
        self.sems, self.names, self.next = sems, names, [0] * len(sems)
        assert len(set(names)) == len(names)

    def where(self, unit):
        return (unit.pair, unit.k) if isinstance(unit, Batch) else (unit, 0)

    def done(self, ins, name, unit):
        k = self.where(unit)[1]
        assert self.names[self.next[k]] == name, (self.names[self.next[k]], name)
        self.next[k] = (self.next[k] + 1) % len(self.names)
        ins.then_inc(self.sems[k], 1)

    def wait(self, eng, unit, name):
        pair, k = self.where(unit)
        if not isinstance(pair, int) or 0 <= pair < PAIRS:
            eng.wait_ge(self.sems[k], pair * len(self.names) + (self.names.index(name) + 1))


def build(nc, x, w_q, w_k, w_v, w_o, amask, pos, router_w, router_b, wq, wk, wv, wo, w1, w2, ln1, ln2, out):
    ctx = ExitStack()
    with ctx:
        def sb(name, shape, dt=F32):
            return ctx.enter_context(nc.sbuf_tensor(name, shape, dt))

        def sem(name):
            return ctx.enter_context(nc.semaphore(name))

        ident = sb("ident", [P, P])
        ident16 = sb("ident16", [P, P], F16)
        later = sb("later", [P, S])
        slot_no = sb("slot_no", [P, SLOTS])
        slot_i = sb("slot_i", [P, SLOTS], I32)
        head_of = sb("head_of", [P, H])
        half_of = sb("half_of", [P, 2, DH])
        ones1 = sb("ones1", [1, P])
        wT = sb("wT", [P, 4, P])
        rw_col = sb("rw_col", [P, 1])
        rw_row = sb("rw_row", [P, P])
        rb_one = sb("rb_one", [1, 1])
        rb = sb("rb", [P, 1])
        g1 = sb("g1", [P, 1])
        g2 = sb("g2", [P, 1])
        wqkv2 = sb("wqkv2", [P, 3, P])
        wo2 = sb("wo2", [P, P])
        w1_sb = sb("w1_sb", [P, F])
        w2_sb = sb("w2_sb", [P, F // P, P])
        masks = sb("masks", [P, 2, NT, S])
        NPC = MASKS * NT
        pos_i = sb("pos_i", [NPC, P], I32)
        pos_f = sb("pos_f", [NPC, P])
        inv = sb("inv", [P, DH // 2])
        angle = sb("angle", [P, NPC, 4])
        turn_i = sb("turn_i", [P, 2, NPC, 4], I32)
        turn = sb("turn", [P, 2, NPC, 4])
        red = sb("red", [P, 2, NPC, 4])
        trig = sb("trig", [P, NPC, 2 * DH])

        x_in = sb("x_in", [P, 2, NT, D])
        xT = sb("xT", [P, S])
        qk = sb("qk", [P, 2, NT, D])
        qn_v = sb("qn_v", [P, 3, 2 * NT * H])
        st = sb("st", [P, 2, NT, H, 4, DH], F16)
        qk2 = st[:, :, :, :, :, :].rearrange("p s t h c d -> p (s t h c d)")[:, 0:4 * NT * D].bitcast(F32)\
            .rearrange("p (s t d) -> p s t d", s=2, t=NT)
        hi_parts = [st[:, 0].rearrange("p t h c d -> p (t h) c d")[:, :, 0:2, :],
                    st[:, 1].rearrange("p t h c d -> p (t h) c d")[:, :, 0:4:2, :]]
        lo_parts = [st[:, 0].rearrange("p t h c d -> p (t h) c d")[:, :, 2:4, :],
                    st[:, 1].rearrange("p t h c d -> p (t h) c d")[:, :, 1:4:2, :]]
        qk_twice = [qk[:, s].rearrange("p t (h d) -> p (t h) d", d=DH)[:, :, None, :].to_broadcast([P, NT * H, 2, DH])
                    for s in range(2)]
        q_st = sb("q_st", [P, 2, 4, S], F16)
        k_st = sb("k_st", [P, 2, 4, S], F16)
        v_aug = sb("v_aug", [P, 2, NT, H, 32])
        th = sb("th", [P, 2, GROUP])
        pr = sb("pr", [P, 4, GROUP])
        w_raw = pr[:, 0, 0:4 * P].rearrange("p (t d) -> p t d", t=4)
        wo_perm = pr[:, 0, 4 * P:5 * P]
        rw_wide = pr[:, 0, 5 * P:6 * P]
        y_u = sb("y_u", [P, S])
        rd = sb("rd", [P, NT * 8])
        y_tm = sb("y_tm", [P, NT, D])
        yT = sb("yT", [P, S])
        x_res = sb("x_res", [P, 2, NT, D])
        r1 = sb("r1", [P, NT, D])
        stats = sb("stats", [P, NT, 6])
        mv = sb("mv", [P, 3, NT])
        ln_v = sb("ln_v", [P, 3, NT])
        x1 = sb("x1", [P, 2, NT, D + 1])

        w_wide = sb("w_wide", [P, S])
        junk = sb("junk", [P, S])
        cnt_ge = sb("cnt_ge", [P, NT])
        cnt_eq = sb("cnt_eq", [P, NT])
        rank = sb("rank", [P, NT])
        coef = sb("coef", [P, 2, NT])
        E = sb("E", [P, NT, P])
        xs = sb("xs", [P, D + 1 + 2 * DH])
        z_base = sb("z_base", [P, 2, NT, D])
        sel_v = sb("sel_v", [P, 3, 1])
        sel_ss = sb("sel_ss", [P, 1])
        hn = sb("hn", [P, D])
        ET = sb("ET", [P, S])
        R = w_wide
        RT = sb("RT", [P, NT, P])
        hnT = sb("hnT", [P, 2, 2, SLOTS])
        hb = sb("hb", [P, F])
        t_cos, t_sin = (hb[:, 256 * i:256 * i + 256].rearrange("p (h d) -> p h d", d=DH) for i in range(2))
        qk_r = sb("qk_r", [P, 2 * H * DH])
        vv = sb("vv", [P, H // 2, 2, 2 * DH])
        qkT = sb("qkT", [P, 2, P])
        k_wide = sb("k_wide", [P, 2, H, SLOTS])
        msel = sb("msel", [P, SLOTS])
        sc = sb("sc", [P, 8, SLOTS])
        mx = sb("mx", [P, 8])
        pool_mark = sb("pool_mark", [P, 8])
        pm = sb("pm", [P, H, SLOTS])
        den = sb("den", [P, H])
        rden = sb("rden", [P, H])
        PT = k_wide[:, 0].rearrange("p h s -> p (h s)").rearrange("p (n c) -> p n c", n=H // 2)
        o_tm = sb("o_tm", [P, H // 2, 2, DH])
        oT = sb("oT", [P, P])
        x1f = sb("x1f", [P, D])
        h2T = sb("h2T", [P, P])
        hq = sb("hq", [P, F])
        hu = sb("hu", [P, F])
        x2 = sb("x2", [P, D])
        proc = sb("proc", [P, D])
        stats2 = sb("stats2", [P, 2 * NT, 6])
        mv2 = sb("mv2", [P, 3, 2 * NT])
        lo_v = sb("lo_v", [P, 3, 2 * NT])
        y_out = sb("y_out", [P, 2, NT, D])

        ps_s = ctx.enter_context(nc.psum_tensor("ps_s", [P, GROUP], F32))
        ps_y = ctx.enter_context(nc.psum_tensor("ps_y", [P, S], F32))
        ps_a = ctx.enter_context(nc.psum_tensor("ps_a", [P, S], F32))
        ps_m = ctx.enter_context(nc.psum_tensor("ps_m", [P, S], F32))

        attn_weights_in = sem("attn_weights_in")
        weights_in = sem("weights_in")
        const_ready = sem("const_ready")
        setup_pe = sem("setup_pe")
        setup_ve = sem("setup_ve")
        setup_act = sem("setup_act")
        zeroed = sem("zeroed")
        mask_loaded = sem("mask_loaded")
        x_in_loaded = [sem(f"x_in_loaded{i}") for i in range(2)]
        x_res_loaded = [sem(f"x_res_loaded{i}") for i in range(2)]
        out_stored = [sem(f"out_stored{i}") for i in range(2)]
        scores_ready = sem("scores_ready")
        tanh_done = sem("tanh_done")
        exp_done = sem("exp_done")
        masked = sem("masked")
        pv_done = sem("pv_done")
        probs_ready = sem("probs_ready")
        gate_ready = sem("gate_ready")
        def tracks(engine, steps):
            return {n: Track([sem(f"{engine}_{n}{k}") for k in range(2 if n in ("prep", "fin", "route") else 1)], names)
                    for n, names in steps.items()}

        ve = tracks("ve", VE_STEPS)
        pe = tracks("pe", PE_STEPS)
        pl = tracks("pool", POOL_STEPS)

        block = ctx.enter_context(nc.Block())

        def live(n, top):
            n = n.no if isinstance(n, Batch) else n
            return not isinstance(n, int) or 0 <= n < top

        def iterations(eng, body, first, last):
            for p in range(-1, first):
                body(p)
            with eng.Fori(first, last + 1) as p:
                body(p)
            for p in range(last + 1, PAIRS + 3):
                body(p)

        def run_side(order, table, p, s, half, together=None):
            for entry in order[2 * s + half]:
                members = []
                for member in entry.split(" & "):
                    name, shift = member.split("@")
                    name, _, k = name.partition("/")
                    unit = Batch(p + int(shift), int(k)) if k else p + int(shift)
                    if live(unit, B if k else PAIRS):
                        members.append((name, unit))
                if together and "root" in entry:
                    if members:
                        together(members)
                else:
                    for name, unit in members:
                        table[name](unit, unit.k if isinstance(unit, Batch) else None)

        def group(p, s, lag=0):
            s -= lag
            b = Batch(p, s // 8)
            return (b, b.k, s % 8) if live(b, B) else None

        @block.sync
        def _(sp):
            def load_mask(m, k):
                sp.dma_start(masks[:, k], amask[m, 0].rearrange("(c p) j -> p c j", p=P)).then_inc(mask_loaded, 16)

            for i, (w, t) in enumerate(((w_q, 0), (w_k, 1), (w_v, 2), (w_o, 3))):
                sp.dma_start(w_raw[:, t, :], w).then_inc(attn_weights_in, 16)
            for b in range(2):
                sp.dma_start(x_in[:, b], x[b].rearrange("(t p) d -> p t d", p=P)).then_inc(x_in_loaded[b], 16)
            for t, w in enumerate((wq, wk, wv)):
                sp.dma_start(wqkv2[:, t, :], w).then_inc(weights_in, 16)
            sp.dma_start(wo2[:, :], wo).then_inc(weights_in, 16)
            sp.dma_start(w1_sb[:, :], w1).then_inc(weights_in, 16)
            sp.dma_start(w2_sb[:, :, :], w2.rearrange("(c p) d -> p c d", p=P)).then_inc(weights_in, 16)
            sp.dma_start(rw_col[:, :], router_w).then_inc(weights_in, 16)
            sp.dma_start(rb_one[:, :], router_b.rearrange("(a n) -> a n", a=1)).then_inc(weights_in, 16)
            sp.dma_start(g1[:, :], ln1.rearrange("(n a) -> n a", a=1)).then_inc(weights_in, 16)
            sp.dma_start(g2[:, :], ln2.rearrange("(n a) -> n a", a=1)).then_inc(weights_in, 16)
            sp.dma_start(pos_i[:, :], pos.rearrange("b (c p) -> (b c) p", p=P)).then_inc(weights_in, 16)
            for k in range(2):
                load_mask(k, k)

            def load_res(b, k):
                ve["fin"].wait(sp, b - 2, "res")
                sp.dma_start(x_res[:, k], x[b.no].rearrange("(t p) d -> p t d", p=P)).then_inc(x_res_loaded[k], 16)

            def load_x(b, k):
                pe["prep"].wait(sp, b - 2, "xT")
                sp.dma_start(x_in[:, k], x[b.no].rearrange("(t p) d -> p t d", p=P)).then_inc(x_in_loaded[k], 16)

            def store(q, k):
                ve["late"].wait(sp, q, f"o{NT * k + NT - 1}_")
                sp.dma_start(out[2 * q + k].rearrange("(t p) d -> p t d", p=P), y_out[:, k])\
                  .then_inc(out_stored[k], 16)

            def body(p):
                if live(p, PAIRS):
                    load_res(Batch(p, 0), 0)
                if live(p + 1, PAIRS) and live(p, PAIRS):
                    load_x(Batch(p, 3), 1)
                if live(p, PAIRS):
                    load_res(Batch(p, 1), 1)
                if live(p + 2, PAIRS):
                    load_x(Batch(p, 4), 0)
                if isinstance(p, int) and p in (1, 2):
                    pe["sel"].wait(sp, p - 1, "R")
                    for k in range(2):
                        if min(2 * p + k, MASKS - 1) != min(2 * p - 2 + k, MASKS - 1):
                            load_mask(min(2 * p + k, MASKS - 1), k)
                if live(p - 2, PAIRS):
                    store(p - 2, 0)
                    store(p - 2, 1)
            iterations(sp, body, 3, PAIRS - 3)
            for k in range(2):
                sp.wait_ge(out_stored[k], 16 * PAIRS)

        @block.gpsimd
        def _(pool):
            nc.gpsimd.memset(ident[:, :], 0.0).then_inc(const_ready, 1)
            nc.gpsimd.memset(ident16[:, :], 0.0).then_inc(const_ready, 1)
            nc.gpsimd.memset(later[:, :], 1.0).then_inc(const_ready, 1)
            nc.gpsimd.memset(head_of[:, :], 1.0).then_inc(const_ready, 1)
            nc.gpsimd.memset(half_of[:, :, :], 1.0).then_inc(const_ready, 1)
            nc.gpsimd.memset(ones1[:, :], 1.0).then_inc(const_ready, 1)
            nc.gpsimd.iota(slot_i[:, :], pattern=[[1, SLOTS]], base=0, channel_multiplier=0).then_inc(const_ready, 1)
            pool.wait_ge(const_ready, 7)
            nc.gpsimd.affine_select(out=ident[:, :], in_=ident[:, :], compare_op=ALU.not_equal, fill=1.0, base=0,
                                    pattern=[[-1, P]], channel_multiplier=1).then_inc(const_ready, 1)
            nc.gpsimd.affine_select(out=ident16[:, :], in_=ident16[:, :], compare_op=ALU.not_equal, fill=1.0, base=0,
                                    pattern=[[-1, P]], channel_multiplier=1).then_inc(const_ready, 1)
            nc.gpsimd.affine_select(out=later[:, :], in_=later[:, :], compare_op=ALU.is_ge, fill=0.0, base=0,
                                    pattern=[[1, S]], channel_multiplier=-1).then_inc(const_ready, 1)
            nc.gpsimd.affine_select(out=head_of[:, :], in_=head_of[:, :], compare_op=ALU.is_ge, fill=0.0, base=0,
                                    pattern=[[-DH, H]], channel_multiplier=1).then_inc(const_ready, 1)
            nc.gpsimd.affine_select(out=half_of[:, :, :], in_=half_of[:, :, :], compare_op=ALU.is_ge, fill=0.0, base=0,
                                    pattern=[[-64, 2], [0, DH]], channel_multiplier=1).then_inc(const_ready, 1)
            nc.gpsimd.tensor_copy(slot_no[:, :], slot_i[:, :]).then_inc(const_ready, 1)
            pool.wait_ge(const_ready, 13)
            nc.gpsimd.affine_select(out=head_of[:, :], in_=head_of[:, :], compare_op=ALU.is_ge, fill=0.0, base=DH - 1,
                                    pattern=[[DH, H]], channel_multiplier=-1).then_inc(const_ready, 1)
            nc.gpsimd.affine_select(out=half_of[:, :, :], in_=half_of[:, :, :], compare_op=ALU.is_ge, fill=0.0,
                                    base=63, pattern=[[64, 2], [0, DH]], channel_multiplier=-1)\
                .then_inc(const_ready, 1)
            nc.gpsimd.memset(slot_no[:, KSEL:], -1.0).then_inc(const_ready, 1)
            nc.gpsimd.memset(v_aug[:, :, :, :, :], 0.0).then_inc(zeroed, 1)
            nc.gpsimd.memset(pm[:, :, :], 0.0).then_inc(zeroed, 1)
            pool.wait_ge(zeroed, 2)
            for s in range(2):
                nc.gpsimd.memset(v_aug[:, :, :, :, :].rearrange("p a t (g s j) c -> p (a t g) s j c", g=4, s=2)
                                 [:, :, s, :, 16 * s + DH], 1.0).then_inc(zeroed, 1)

            def causal(g, n0, n, col, step):
                buf = pr[:, g % 4, col:col + P]
                if n > 1:
                    buf = pr[:, g % 4, col:col + step * n].rearrange("p (n c) -> p n c", c=step)[:, :, 0:P]
                return nc.gpsimd.affine_select(out=buf, in_=buf, compare_op=ALU.is_ge, fill=0.0, base=0,
                                               pattern=[[0, n], [1, P]] if n > 1 else [[1, P]], channel_multiplier=-1)

            mul = lambda out, a, b: nc.gpsimd.tensor_tensor(out, a, b, ALU.mult)

            def prep_sq(b, k):
                ve["prep"].wait(pool, b, "qk1")
                pe["prep"].wait(pool, b - 1, f"st{NT - 1}")
                pl["prep"].done(mul(qk2, qk[:, :, :, :], qk[:, :, :, :]), "sq", b)

            def prep_lo(b, k):
                for s, part in enumerate("qk"):
                    ve["prep"].wait(pool, b, f"hi_{part}")
                    pl["prep"].done(nc.gpsimd.tensor_tensor(lo_parts[s], qk_twice[s], hi_parts[s], ALU.subtract),
                                    f"lo_{part}", b)

            def route_xw(b, k):
                ve["fin"].wait(pool, b, f"x1_{NT - 1}")
                pl["route"].done(mul(r1[:, :, :], x1[:, k, :, 0:D], rw_row[:, None, :].to_broadcast([P, NT, D])), "xw", b)

            def sel_zb(q, _):
                ve["late"].wait(pool, q - 1, "z1")
                for k in range(2):
                    ve["route"].wait(pool, Batch(q, k), "coef")
                    pl["sel"].done(mul(z_base[:, k], x1[:, k, :, 0:D], coef[:, k, :, None].to_broadcast([P, NT, D])),
                                   f"zb{k}", q)

            def att_kw(q, _):
                ve["sel"].wait(pool, q, "qkT")
                pe["att"].wait(pool, q - 1, "PV")
                for k in range(2):
                    pl["att"].done(mul(
                        k_wide[:, k], qkT[:, 1, None, SLOTS * k:SLOTS * k + SLOTS].to_broadcast([P, H, SLOTS]),
                        head_of[:, :, None].to_broadcast([P, H, SLOTS])), f"kw{k}", q)

            def att_hh(q, _):
                ve["att"].wait(pool, q, "h")
                pl["att"].done(mul(hq[:, :], hb[:, :], hb[:, :]), "hh", q)

            def att_hu(q, _):
                pe["late"].wait(pool, q - 1, "w2")
                ve["att"].wait(pool, q, "hp")
                pl["att"].done(mul(hu[:, :], hq[:, :], hb[:, :]), "hu", q)

            table = {"prep.sq": prep_sq, "prep.lo": prep_lo, "route.xw": route_xw, "sel.zb": sel_zb, "att.kw": att_kw,
                     "att.hh": att_hh, "att.hu": att_hu}

            def body(p):
                for s in range(16):
                    g = group(p, s, 1)
                    if g:
                        b, _, gi = g
                        pool.wait_ge(exp_done, b.no * 8 + (gi + 1))
                        nc.gpsimd.tensor_tensor(pool_mark[:, gi:gi + 1], head_of[:, 0:1], head_of[:, 0:1], ALU.mult)
                        causal(gi, 0, 1, 0, P)
                        causal(gi, 0, 2, 384, P)
                        causal(gi, 0, 3, 1024, 256)
                        causal(gi, 0, 2, 1920, P).then_inc(masked, 1)
                    for half in range(2):
                        run_side(POOL_ORDER, table, p, s, half)
            iterations(pool, body, 3, PAIRS - 2)

        @block.scalar
        def _(act):
            act.wait_ge(setup_ve, SETUP_RED)
            nc.scalar.activation(turn[:, :, :, :], red[:, :, :, :], ACT.Sin).then_inc(setup_act, 1)

            def att_exp(q, _):
                ve["att"].wait(act, q, "sub1")
                nc.scalar.activation(pm[:, :, 0:KSEL], pm[:, :, 0:KSEL], ACT.Exp).then_inc(probs_ready, 1)

            def att_tanh(q, _):
                pl["att"].wait(act, q, "hu")
                nc.scalar.activation(hq[:, :], hu[:, :], ACT.Tanh, scale=float(np.sqrt(2.0 / np.pi)))\
                    .then_inc(gate_ready, 1)

            table = {"att.exp": att_exp, "att.tanh": att_tanh}

            def body(p):
                for s in range(16):
                    g = group(p, s)
                    if g:
                        b, _, gi = g
                        for u, (c0, c1) in enumerate(UNIT):
                            act.wait_ge(scores_ready, b.no * 16 + (2 * gi + u + 1))
                            if gi >= 2 or b.at_least(1):
                                act.wait_ge(exp_done, b.no * 8 + (gi - 1))
                            nc.scalar.activation(th[:, gi % 2, c0:c1], ps_s[:, c0:c1], ACT.Tanh,
                                                 scale=1.0 / (QK_SCALE ** 2 * DH ** 0.5 * SOFTCAP))\
                                .then_inc(tanh_done, 1)
                    for half in range(2):
                        run_side(ACT_ORDER, table, p, s, half)
                    g = group(p, s, 1)
                    if g:
                        b, _, gi = g
                        act.wait_ge(tanh_done, b.no * 16 + (2 * gi + 2))
                        if gi >= 4 or b.at_least(1):
                            act.wait_ge(pv_done, b.no * 4 + (gi // 2 - 1))
                        nc.scalar.activation(pr[:, gi % 4, :], th[:, gi % 2, :], ACT.Exp, scale=SOFTCAP)\
                            .then_inc(exp_done, 1)
            iterations(act, body, 2, PAIRS - 1)

        @block.vector
        def _(v):
            count = [0]

            def setup(ins):
                count[0] += 1
                ins.then_inc(setup_ve, 1)
                v.wait_ge(setup_ve, count[0])

            v.wait_ge(attn_weights_in, 16 * 4)
            v.wait_ge(const_ready, 16)
            for half in range(2):
                for s in range(2):
                    setup(nc.vector.tensor_copy(
                        wo_perm[:, 64 * half:64 * half + 64].rearrange("p (j a s d) -> p s j a d", j=2, a=2, s=2)[:, s],
                        w_raw[:, 3, 64 * half:64 * half + 64].rearrange("p (a s j d) -> p s j a d", j=2, a=2, s=2)[:, s]))
            v.wait_ge(setup_pe, 1)
            setup(nc.vector.tensor_copy(wT[:, :, :], ps_a[:, :].rearrange("p (t d) -> p t d", t=4)))
            def setup_routed():
                v.wait_ge(weights_in, 16 * 11)
                setup(nc.vector.tensor_copy(rw_wide, rw_col[:, 0:1].to_broadcast([P, P])))
                setup(nc.vector.tensor_copy(pos_f[:, :], pos_i[:, :]))
                for i in range(DH // 2):
                    setup(nc.vector.memset(inv[:, i:i + 1], float(np.float32(1.0 / ROPE_BASE ** (2 * i / DH)))))
                v.wait_ge(setup_pe, 2)
                setup(nc.vector.tensor_copy(rw_row[:, :], ps_m[:, 0:P]))
                setup(nc.vector.tensor_copy(rb[:, :], ps_m[:, 256:257]))
                setup(nc.vector.tensor_tensor(angle[:, :, :], ps_m[:, P:P + NPC, None].to_broadcast([P, NPC, 4]),
                                              inv[:, None, :].to_broadcast([P, NPC, 4]), ALU.mult))
                for i, quarter in enumerate((0.25, 0.0)):
                    setup(nc.vector.tensor_scalar(turn_i[:, i], angle[:, :, :], 1.0 / (2 * np.pi), quarter,
                                                  ALU.mult, ALU.add))
                setup(nc.vector.tensor_copy(turn[:, :, :, :], turn_i[:, :, :, :]))
                c1 = 6.28125
                c2 = float(np.float32(np.floor((2 * np.pi - c1) * 2 ** 20) / 2 ** 20))
                c3 = float(2 * np.pi - c1 - c2)
                for i in range(2):
                    setup(nc.vector.scalar_tensor_tensor(red[:, i], turn[:, i], -c1, angle[:, :, :], ALU.mult, ALU.add))
                    setup(nc.vector.scalar_tensor_tensor(red[:, i], turn[:, i], -c2, red[:, i], ALU.mult, ALU.add))
                    setup(nc.vector.scalar_tensor_tensor(red[:, i], turn[:, i], -c3, red[:, i], ALU.mult, ALU.add))
                setup(nc.vector.tensor_scalar(red[:, 0], red[:, 0], float(np.pi / 2), None, ALU.add))
                setup(nc.vector.tensor_scalar(red[:, :, :, :], red[:, :, :, :], 3.1415925, -3.1415925, ALU.min, ALU.max))
                assert count[0] == SETUP_RED, count[0]
                v.wait_ge(setup_act, 1)
                for i in range(2):
                    setup(nc.vector.tensor_copy(trig[:, :, 4 * i:4 * i + 4], turn[:, 0]))
                setup(nc.vector.tensor_scalar(trig[:, :, 8:12], turn[:, 1], -1.0, None, ALU.mult))
                setup(nc.vector.tensor_copy(trig[:, :, 12:16], turn[:, 1]))
                assert count[0] == SETUP_ALL, count[0]

            def chain(track, unit):
                def step(make, name, after=None):
                    i = track.names.index(name)
                    prev = after or (track.names[i - 1] if i else None)
                    if prev:
                        track.wait(v, unit, prev)
                    track.done(make(), name, unit)
                return step

            def roots(members):
                first = members[0][0].endswith("root1")
                problems = [root_of[name.split(".")[0]](unit) for name, unit in members]
                if first:
                    for step, name, buf, src, mul, eps in problems:
                        step(lambda: nc.vector.tensor_scalar(buf[:, 0], src, mul, eps, ALU.mult, ALU.add), f"{name}_var")
                    for step, name, buf, *_ in problems:
                        step(lambda: nc.vector.tensor_scalar(buf[:, 1].bitcast(I32), buf[:, 0].bitcast(I32), -0.5,
                                                             RSQRT_GUESS, ALU.mult, ALU.add), f"{name}_guess")
                for i in (0,) if first else (1, 2):
                    for step, name, buf, *_ in problems:
                        step(lambda: nc.vector.tensor_tensor(buf[:, 2], buf[:, 1], buf[:, 1], ALU.mult), f"{name}_a{i}")
                    for step, name, buf, *_ in problems:
                        step(lambda: nc.vector.scalar_tensor_tensor(buf[:, 2], buf[:, 2], -0.5, buf[:, 0], ALU.mult,
                                                                    ALU.mult), f"{name}_b{i}")
                    for step, name, buf, *_ in problems:
                        step(lambda: nc.vector.scalar_tensor_tensor(buf[:, 1], buf[:, 2], 1.5, buf[:, 1], ALU.add,
                                                                    ALU.mult), f"{name}_c{i}")

            root_of = {
                "prep": lambda b: (chain(ve["prep"], b), "qkr", qn_v, qn_v[:, 2], 1.0 / (DH * QK_SCALE ** 2),
                                   EPS_QK / QK_SCALE ** 2),
                "fin": lambda b: (chain(ve["fin"], b), "ln", ln_v, mv[:, 2], 1.0 / D, EPS_LN),
                "sel": lambda q: (chain(ve["sel"], q), "r1", sel_v, sel_ss[:, :], 1.0 / D, EPS_RMS),
                "att": lambda q: (chain(ve["att"], q), "r2", sel_v, sel_ss[:, :], 1.0 / D, EPS_RMS),
                "late": lambda q: (chain(ve["late"], q), "ln_", lo_v, mv2[:, 2], 1.0 / D, EPS_LN)}

            def prep_xT(b, k):
                pe["prep"].wait(v, b, "xT")
                pe["prep"].wait(v, b - 1, "v")
                ve["prep"].done(nc.vector.tensor_copy(xT[:, :], ps_a[:, :]), "xT", b)

            def prep_qk(b, k, i):
                pe["prep"].wait(v, b, f"qk{i}")
                pl["prep"].wait(v, b - 1, "lo_k")
                ve["prep"].done(nc.vector.tensor_copy(
                    qk[:, :, 2 * i:2 * i + 2, :].rearrange("p s t d -> p t s d"),
                    ps_a[:, :].rearrange("p (t s d) -> p t s d", t=2, s=2)), f"qk{i}", b)

            def prep_v(b, k):
                pe["prep"].wait(v, b, "v")
                v.wait_ge(zeroed, 4)
                if b.at_least(2):
                    v.wait_ge(pv_done, (b - 1).no * 4)
                for s in range(2):
                    o = v_aug[:, k].rearrange("p t (g s j) c -> p s (t g) j c", g=4, s=2)
                    i = ps_a[:, :].rearrange("p (n s j d) -> p s n j d", s=2, j=2, d=DH)
                    ve["prep"].done(nc.vector.tensor_copy(o[:, s, :, :, 16 * s:16 * s + DH], i[:, s]), f"v{'ab'[s]}", b)

            def prep_ss(b, k):
                pl["prep"].wait(v, b, "sq")
                chain(ve["prep"], b)(lambda: nc.vector.tensor_reduce(
                    qn_v[:, 2], qk2.rearrange("p s t (h d) -> p (s t h) d", d=DH), AX.X, ALU.add), "ss")

            def prep_qkn(b, k):
                qf = qk[:, :, :, :].rearrange("p s t (h d) -> p (s t h) d", d=DH)
                chain(ve["prep"], b)(lambda: nc.vector.tensor_tensor(
                    qf, qf, qn_v[:, 1, :, None].to_broadcast([P, 2 * NT * H, DH]), ALU.mult), "qkn")

            def prep_split(b, k):
                step = chain(ve["prep"], b)
                for s, name in enumerate(("hi_q", "hi_k")):
                    step(lambda: nc.vector.tensor_copy(hi_parts[s], qk_twice[s]), name, "qkn")
                if isinstance(b.no, int) and b.no == 0:
                    setup_routed()

            def prep_st(b, k, t):
                pe["prep"].wait(v, b, f"st{t}")
                if t == 0 and b.at_least(2):
                    v.wait_ge(scores_ready, (b - 1).no * 16)
                parts = ps_a[:, :].bitcast(F16).rearrange("p (s g q) -> p s g q", s=2, g=4)
                ve["prep"].done(nc.vector.tensor_copy(q_st[:, k, :, P * t:P * t + P], parts[:, 0]), f"qst{t}", b)
                ve["prep"].done(nc.vector.tensor_copy(k_st[:, k, :, P * t:P * t + P], parts[:, 1]), f"kst{t}", b)

            def fin_yU(b, half):
                v.wait_ge(pv_done, b.no * 4 + (2 * half + 2))
                if half:
                    pe["fin"].wait(v, b, "y0T")
                else:
                    pe["fin"].wait(v, b - 1, "y1T")
                ve["fin"].done(nc.vector.tensor_copy(y_u[:, :], ps_y[:, :]), f"yU{half}", b)

            def fin_y(b, half):
                pe["fin"].wait(v, b, f"y{half}T")
                if half == 0:
                    pe["fin"].wait(v, b - 1, "yT")
                rows = ps_m[:, :].rearrange("p (n c) -> p n c", c=16)
                ve["fin"].done(nc.vector.reciprocal(rd[:, :], rows[:, :, DH]), f"rd{half}", b)
                ve["fin"].wait(v, b, f"rd{half}")
                ve["fin"].done(nc.vector.tensor_tensor(
                    y_tm[:, :, 64 * half:64 * half + 64].rearrange("p t (n d) -> p t n d", d=DH),
                    rows[:, :, 0:DH].rearrange("p (t n) d -> p t n d", t=NT),
                    rd[:, :].rearrange("p (t n) -> p t n", t=NT)[:, :, :, None].to_broadcast([P, NT, 8, DH]),
                    ALU.mult), f"y{half}", b)

            def fin_yT(b, k):
                pe["fin"].wait(v, b, "yT")
                pe["fin"].wait(v, b - 1, "wo")
                ve["fin"].done(nc.vector.tensor_copy(yT[:, :], ps_m[:, :]), "yT", b)

            def moments(step, tag, src, st6, m, after):
                for c in range(src.shape[1]):
                    step(lambda: nc.vector.bn_stats(st6[:, c, :], src[:, c, :]), f"bs{c}{tag}", after)
                even, odd = st6[:, :, 1], st6[:, :, 4]
                step(lambda: nc.vector.tensor_tensor(m[:, 0], even, odd, ALU.add), f"sum{tag}")
                all_in = f"bs{src.shape[1] - 1}{tag}"
                step(lambda: nc.vector.tensor_tensor(m[:, 1], even, odd, ALU.subtract), f"dif{tag}", all_in)
                step(lambda: nc.vector.tensor_tensor(m[:, 2], st6[:, :, 2], st6[:, :, 5], ALU.add), f"sq{tag}", all_in)
                step(lambda: nc.vector.tensor_scalar(m[:, 0], m[:, 0], 0.5, None, ALU.mult), f"mean{tag}", f"sum{tag}")
                step(lambda: nc.vector.tensor_tensor(m[:, 1], m[:, 1], m[:, 1], ALU.mult), f"dif2{tag}", f"dif{tag}")
                step(lambda: nc.vector.scalar_tensor_tensor(m[:, 2], m[:, 1], D / 4.0, m[:, 2], ALU.mult, ALU.add),
                     f"dev{tag}")

            def fin_wo(b, k):
                step = chain(ve["fin"], b)
                pe["fin"].wait(v, b, "wo")
                v.wait_ge(x_res_loaded[k], b.pair * 16 + 16)
                ve["route"].wait(v, b - 1, "w")
                step(lambda: nc.vector.tensor_tensor(r1[:, :, :], ps_m[:, :].rearrange("p (t d) -> p t d", t=NT),
                                                     x_res[:, k], ALU.add), "res")

            def fin_ln(b, k):
                moments(chain(ve["fin"], b), "", r1, stats, mv, "res")

            def fin_x1(b, k):
                step = chain(ve["fin"], b)
                pl["sel"].wait(v, b.pair - 1, f"zb{k}")
                pe["sel"].wait(v, b.pair - 1, "gather")
                for c in range(NT):
                    step(lambda: nc.vector.tensor_scalar(x1[:, k, c, 0:D], r1[:, c, :], mv[:, 0, c:c + 1],
                                                         ln_v[:, 1, c:c + 1], ALU.subtract, ALU.mult),
                         f"x1_{c}", "ln_c2")

            def route_w(b, k):
                step = chain(ve["route"], b)
                pl["route"].wait(v, b, "xw")
                step(lambda: nc.vector.tensor_reduce(x1[:, k, :, D:D + 1], r1[:, :, :], AX.X, ALU.add), "w")
                step(lambda: nc.vector.tensor_scalar(x1[:, k, :, D:D + 1], x1[:, k, :, D:D + 1], rb[:, 0:1], None,
                                                     ALU.add), "w_b")
                ve["route"].wait(v, b - 1, f"eq{NT - 1}")
                if k == 0:
                    pe["sel"].wait(v, b.pair - 1, "RT")
                step(lambda: nc.vector.tensor_copy(w_wide[:, :].rearrange("p (t m) -> p t m", t=NT),
                                                   x1[:, k, :, D:D + 1].to_broadcast([P, NT, P])), "wide")

            def route_row(b, k):
                pe["route"].wait(v, b, "wrow")
                ve["route"].done(nc.vector.tensor_copy(w_wide[:, :], ps_m[:, :]), "row", b)

            def route_ge(b, k):
                step = chain(ve["route"], b)
                for c in range(NT):
                    step(lambda: nc.vector.tensor_scalar(junk[:, :], w_wide[:, :], x1[:, k, c, D:D + 1], 0.0, ALU.is_ge,
                                                         ALU.add, accum_out=cnt_ge[:, c:c + 1]), f"ge{c}")

            def route_eq(b, k):
                step = chain(ve["route"], b)
                for c in range(NT):
                    n = S - P * c
                    step(lambda: nc.vector.scalar_tensor_tensor(
                        junk[:, 0:n], w_wide[:, P * c:], x1[:, k, c, D:D + 1], later[:, 0:n], ALU.is_equal, ALU.mult,
                        accum_out=cnt_eq[:, c:c + 1]), f"eq{c}")

            def route_rank(b, k):
                step = chain(ve["route"], b)
                step(lambda: nc.vector.tensor_tensor(rank[:, :], cnt_ge[:, :], cnt_eq[:, :], ALU.subtract), "rank")
                pl["sel"].wait(v, b.pair - 1, "zb1")
                step(lambda: nc.vector.tensor_scalar(coef[:, k, :], cnt_ge[:, :], float(KSEL) + 0.5, 1.0, ALU.is_gt,
                                                     ALU.add), "coef")
                pe["sel"].wait(v, b.pair - 1, "msel")
                step(lambda: nc.vector.tensor_tensor(
                    E[:, :, SLOTS * k:SLOTS * k + SLOTS], rank[:, :, None].to_broadcast([P, NT, SLOTS]),
                    slot_no[:, None, :].to_broadcast([P, NT, SLOTS]), ALU.is_equal), "E")

            def copy_step(track, name, make, also=()):
                def run(q, _):
                    pe[track].wait(v, q, name)
                    for other, unit, n in also:
                        other.wait(v, unit(q), n)
                    ve[track].done(make(), name, q)
                return run

            def sel_gather(q, _):
                pe["sel"].wait(v, q, "gather")
                ve["late"].wait(v, q - 1, "proc")
                ve["sel"].done(nc.vector.tensor_copy(xs[:, :], ps_m[:, 0:D + 1 + 2 * DH]), "xs", q)

            sel_ET = copy_step("sel", "ET", lambda: nc.vector.tensor_copy(ET[:, :], ps_m[:, :]),
                               [(pe["late"], lambda q: q - 1, "sc1")])
            sel_R = copy_step("sel", "R", lambda: nc.vector.tensor_copy(R[:, :], ps_m[:, :]),
                              [(ve["route"], lambda q: Batch(q, 1), f"eq{NT - 1}")])

            def sel_squares(q, _):
                chain(ve["sel"], q)(lambda: nc.vector.tensor_tensor_reduce(
                    hn[:, :], xs[:, 0:D], xs[:, 0:D], 1.0, 0.0, ALU.mult, ALU.add, sel_ss[:, :]), "ss")

            def sel_hn(q, _):
                chain(ve["sel"], q)(lambda: nc.vector.tensor_scalar(hn[:, :], xs[:, 0:D], sel_v[:, 1], None, ALU.mult),
                                    "hn")

            sel_RT = copy_step("sel", "RT", lambda: nc.vector.tensor_copy(
                RT[:, :, :], ps_m[:, :].rearrange("p (c s) -> p c s", c=NT)))
            sel_hnT = copy_step("sel", "hnT", lambda: nc.vector.tensor_scalar(
                hnT[:, :, :, :], ps_m[:, 0:P].rearrange("p (k s) -> p k s", k=2)[:, :, None, :]
                .to_broadcast([P, 2, 2, SLOTS]), g1[:, 0:1], None, ALU.mult))

            def sel_qkv(q, _):
                step = chain(ve["sel"], q)
                pe["sel"].wait(v, q, "qkv")
                t = ps_m[:, 0:2 * D].rearrange("p (h d) -> p h d", d=DH)
                cos = xs[:, D + 1:D + 1 + DH]
                sin = xs[:, D + 1 + DH:D + 1 + 2 * DH]
                step(lambda: nc.vector.tensor_tensor(t_cos, t, cos[:, None, :].to_broadcast([P, 2 * H, DH]),
                                                     ALU.mult), "cosp")
                for i in range(2):
                    step(lambda: nc.vector.tensor_tensor(
                        t_sin[:, :, 4 * i:4 * i + 4], t[:, :, 4 - 4 * i:8 - 4 * i],
                        sin[:, None, 4 * i:4 * i + 4].to_broadcast([P, 2 * H, 4]), ALU.mult), f"sin{i}", "hnT")
                step(lambda: nc.vector.tensor_tensor(qk_r[:, :].rearrange("p (h d) -> p h d", d=DH), t_cos,
                                                     t_sin, ALU.add), "rope")
                for k in range(2):
                    step(lambda: nc.vector.tensor_tensor(
                        vv[:, :, k, :], ps_m[:, 2 * D + D * k:3 * D + D * k].rearrange("p (n c) -> p n c", n=H // 2),
                        half_of[:, :, :].rearrange("p a d -> p (a d)")[:, None, :].to_broadcast([P, H // 2, 2 * DH]),
                        ALU.mult), f"vv{k}", "hnT")

            sel_msel = copy_step("sel", "msel", lambda: nc.vector.tensor_copy(msel[:, :], ps_m[:, 0:SLOTS]))
            sel_qkT = copy_step("sel", "qkT", lambda: nc.vector.tensor_copy(
                qkT[:, :, :], ps_m[:, 0:2 * P].rearrange("p (s c) -> p s c", s=2)))

            def att_scores(q, h):
                step = chain(ve["att"], q)
                pe["att"].wait(v, q, f"S{h}")
                step(lambda: nc.vector.scalar_tensor_tensor(
                    sc[:, :, :], ps_m[:, :].rearrange("p (h s) -> p h s", h=8), float(DH ** -0.5),
                    msel[:, None, :].to_broadcast([P, 8, SLOTS]), ALU.mult, ALU.add), f"sc{h}")

            def att_max(q, h):
                step = chain(ve["att"], q)
                step(lambda: nc.vector.tensor_reduce(mx[:, :], sc[:, :, 0:KSEL], AX.X, ALU.max), f"mx{h}")
                step(lambda: nc.vector.tensor_tensor(
                    pm[:, 8 * h:8 * h + 8, 0:KSEL], sc[:, :, 0:KSEL], mx[:, :, None].to_broadcast([P, 8, KSEL]),
                    ALU.subtract), f"sub{h}")

            def att_den(q, _):
                step = chain(ve["att"], q)
                v.wait_ge(probs_ready, q + 1)
                step(lambda: nc.vector.tensor_reduce(den[:, :], pm[:, :, 0:KSEL], AX.X, ALU.add), "den")
                step(lambda: nc.vector.reciprocal(rden[:, :], den[:, :]), "rden")

            def att_PT(q, h):
                pe["att"].wait(v, q, f"P{h}T")
                chain(ve["att"], q)(lambda: nc.vector.tensor_copy(
                    PT[:, 4 * h:4 * h + 4, :], ps_m[:, :].rearrange("p (n s) -> p n s", n=4)), f"PT{h}")

            def att_PV(q, _):
                step = chain(ve["att"], q)
                pe["att"].wait(v, q, "PV")
                for k in range(2):
                    rows = slice(SLOTS * k, SLOTS * k + SLOTS)
                    step(lambda: nc.vector.tensor_tensor(
                        o_tm[rows], ps_m[rows, 0:2 * D].rearrange("p (n k a d) -> p k n a d", n=H // 2, k=2, a=2)[:, k],
                        rden[rows, :].rearrange("p (n a) -> p n a", a=2)[:, :, :, None]
                        .to_broadcast([SLOTS, H // 2, 2, DH]), ALU.mult), f"o{k}", "PT1")

            att_oT = copy_step("att", "oT", lambda: nc.vector.tensor_copy(oT[:, :], ps_m[:, 0:P]))

            def att_wo(q, _):
                step = chain(ve["att"], q)
                pe["att"].wait(v, q, "wo")
                step(lambda: nc.vector.tensor_tensor(x1f[:, :], xs[:, 0:D], ps_m[:, 0:D], ALU.add), "x1f")

            def att_squares(q, _):
                pe["sel"].wait(v, q, "hnT")
                chain(ve["att"], q)(lambda: nc.vector.tensor_tensor_reduce(
                    hn[:, :], x1f[:, :], x1f[:, :], 1.0, 0.0, ALU.mult, ALU.add, sel_ss[:, :]), "ss2")

            def att_hn(q, _):
                chain(ve["att"], q)(lambda: nc.vector.tensor_scalar(hn[:, :], x1f[:, :], sel_v[:, 1], None, ALU.mult),
                                    "hn2")

            att_h2T = copy_step("att", "h2T", lambda: nc.vector.tensor_scalar(
                h2T[:, :], ps_m[:, 0:P], g2[:, 0:1], None, ALU.mult))

            def att_w1(q, _):
                pe["att"].wait(v, q, "w1")
                ve["att"].done(nc.vector.tensor_copy(hb[:, :], ps_m[:, :]), "h", q)

            def att_hp(q, _):
                pl["att"].wait(v, q, "hh")
                ve["att"].done(nc.vector.tensor_scalar(hq[:, :], hq[:, :], 0.044715, 1.0, ALU.mult, ALU.add), "hp", q)

            def att_gate(q, _):
                v.wait_ge(gate_ready, q + 1)
                ve["att"].done(nc.vector.scalar_tensor_tensor(hu[:, :], hq[:, :], 1.0, hb[:, :], ALU.add, ALU.mult), "g", q)

            def late_w2(q, _):
                step = chain(ve["late"], q)
                pe["late"].wait(v, q, "w2")
                step(lambda: nc.vector.scalar_tensor_tensor(x2[:, :], ps_m[:, 0:D], 0.5, x1f[:, :], ALU.mult, ALU.add),
                     "x2")
                step(lambda: nc.vector.tensor_scalar(proc[:, :], x2[:, :], xs[:, D:D + 1], None, ALU.mult), "proc")

            def late_sc(q, k):
                pe["late"].wait(v, q, f"sc{k}")
                pl["sel"].wait(v, q, f"zb{k}")
                if not isinstance(q, int) or q >= 1:
                    v.wait_ge(out_stored[k], q * 16)
                ve["late"].done(nc.vector.tensor_tensor(y_out[:, k], ps_m[:, :].rearrange("p (t d) -> p t d", t=NT),
                                                        z_base[:, k], ALU.add), f"z{k}", q)

            zz = y_out[:, :, :, :].rearrange("p k t d -> p (k t) d")

            def late_ln(q, _):
                moments(chain(ve["late"], q), "_", zz, stats2, mv2, "z1")

            def late_norm(q, _):
                step = chain(ve["late"], q)
                for c in range(2 * NT):
                    step(lambda: nc.vector.tensor_scalar(zz[:, c, :], zz[:, c, :], mv2[:, 0, c:c + 1],
                                                         lo_v[:, 1, c:c + 1], ALU.subtract, ALU.mult),
                         f"o{c}_", "ln__c2")

            table = {"prep.xT": prep_xT, "prep.qk0": lambda b, k: prep_qk(b, k, 0),
                     "prep.qk1": lambda b, k: prep_qk(b, k, 1), "prep.v": prep_v, "prep.ss": prep_ss,
                     "prep.qkn": prep_qkn, "prep.hi": prep_split,
                     **{f"prep.st{t}": (lambda b, k, t=t: prep_st(b, k, t)) for t in range(NT)},
                     "fin.yU0": lambda b, k: fin_yU(b, 0), "fin.yU1": lambda b, k: fin_yU(b, 1),
                     "fin.y0": lambda b, k: fin_y(b, 0), "fin.y1": lambda b, k: fin_y(b, 1),
                     "fin.yT": fin_yT, "fin.res": fin_wo, "fin.ln": fin_ln, "fin.x1": fin_x1, "route.w": route_w,
                     "route.row": route_row, "route.ge": route_ge, "route.eq": route_eq, "route.rank": route_rank,
                     "sel.xs": sel_gather, "sel.ET": sel_ET, "sel.R": sel_R, "sel.ss": sel_squares, "sel.hn": sel_hn,
                     "sel.RT": sel_RT, "sel.hnT": sel_hnT, "sel.qkv": sel_qkv, "sel.msel": sel_msel,
                     "sel.qkT": sel_qkT, "att.sc0": lambda q, _: att_scores(q, 0), "att.sc1": lambda q, _: att_scores(q, 1),
                     "att.mx0": lambda q, _: att_max(q, 0), "att.mx1": lambda q, _: att_max(q, 1), "att.den": att_den,
                     "att.PT0": lambda q, _: att_PT(q, 0), "att.PT1": lambda q, _: att_PT(q, 1), "att.o": att_PV,
                     "att.oT": att_oT, "att.x1f": att_wo, "att.ss": att_squares, "att.hn": att_hn, "att.h2T": att_h2T,
                     "att.h": att_w1, "att.hp": att_hp, "att.g": att_gate, "late.proc": late_w2,
                     "late.z0": lambda q, _: late_sc(q, 0), "late.z1": lambda q, _: late_sc(q, 1), "late.ln": late_ln,
                     "late.norm": late_norm}

            def body(p):
                for s in range(16):
                    for half in range(2):
                        run_side(VE_ORDER, table, p, s, half, roots)
            iterations(v, body, 3, PAIRS - 2)

        @block.tensor
        def _(t_):
            mm = nc.tensor.matmul
            tr = nc.tensor.transpose
            t_.wait_ge(const_ready, 16)
            t_.wait_ge(attn_weights_in, 16 * 4)
            t_.wait_ge(setup_ve, 4)
            for i in range(4):
                last = tr(ps_a[:, P * i:P * i + P], w_raw[:, i, :] if i < 3 else wo_perm, ident[:, :])
            last.then_inc(setup_pe, 1)
            t_.wait_ge(setup_ve, 5)

            def setup_routed():
                t_.wait_ge(weights_in, 16 * 11)
                t_.wait_ge(setup_ve, 7)
                tr(ps_m[:, 0:P], rw_wide, ident[:, :])
                tr(ps_m[:, P:P + NPC], pos_f[:, :], ident[0:NPC, 0:NPC])
                mm(ps_m[:, 256:257], ones1[:, :], rb_one[:, :], start=True, stop=True).then_inc(setup_pe, 1)

            def scores(b, k, gi, u):
                if gi > 0 or b.at_least(1):
                    t_.wait_ge(tanh_done, b.no * 16 + (2 * gi + u - 1))
                for hb_, kb in UNIT_BLOCKS[u]:
                    g, j = 2 * (gi // 4) + hb_, gi % 4
                    c = COL[(hb_, kb)]
                    last = mm(ps_s[:, c:c + S - P * kb], k_st[32 * j:32 * j + 32, k, g, P * kb:P * kb + P],
                              q_st[32 * j:32 * j + 32, k, g, P * kb:S], start=True, stop=True)
                last.then_inc(scores_ready, 1)

            def pv(b, k, q):
                t_.wait_ge(masked, b.no * 8 + (2 * q + 2))
                if q % 2 == 0:
                    ve["fin"].wait(t_, b if q else b - 1, "yU0" if q else "yU1")
                for kb in range(NT):
                    for j in range(4):
                        ab, gi = j % 2, 2 * q + j // 2
                        h = 8 * (q // 2) + 4 * ab + gi % 4
                        c = COL[(ab, kb)]
                        last = mm(ps_y[32 * j:32 * j + 32, P * kb:S], v_aug[:, k, kb, h, :],
                                  pr[:, gi % 4, c:c + S - P * kb], start=(q % 2 == 0 and kb == 0),
                                  stop=(q % 2 == 1 and kb == 3), skip_group_check=True)
                last.then_inc(pv_done, 1)

            def four(src, track, name, unit):
                for c in range(4):
                    last = tr(ps_m[:, P * c:P * c + P], src(c), ident[:, :])
                track.done(last, name, unit)

            def bank_free(use, unit):
                pair = unit.pair if isinstance(unit, Batch) else unit
                for reader in BANK_READ[use if not isinstance(unit, Batch) else f"{use}/{unit.k}"]:
                    name, shift = reader.split("@")
                    name, _, k = name.partition("/")
                    track, step = name.split(".")
                    before = pair + int(shift)
                    ve[track].wait(t_, Batch(before, int(k)) if k else before, step)

            def prep_xT(b, k):
                t_.wait_ge(x_in_loaded[k], b.pair * 16 + 16)
                bank_free("prep.xT", b)
                for c in range(NT):
                    last = tr(ps_a[:, P * c:P * c + P], x_in[:, k, c, :], ident[:, :])
                pe["prep"].done(last, "xT", b)

            def prep_qk(b, k, i):
                ve["prep"].wait(t_, b, "xT")
                bank_free(f"prep.qk{i}", b)
                for t in range(2 * i, 2 * i + 2):
                    last = mm(ps_a[:, 2 * D * (t % 2):2 * D * (t % 2) + 2 * D], xT[:, P * t:P * t + P],
                              wT[:, 0:2, :].rearrange("p a d -> p (a d)"), start=True, stop=True)
                pe["prep"].done(last, f"qk{i}", b)

            def prep_v(b, k):
                bank_free("prep.v", b)
                for t in range(NT):
                    last = mm(ps_a[:, P * t:P * t + P], xT[:, P * t:P * t + P], wT[:, 2, :], start=True, stop=True)
                pe["prep"].done(last, "v", b)

            def prep_st(b, k, t):
                if t == 0 and isinstance(b.no, int) and b.no == 0:
                    setup_routed()
                pl["prep"].wait(t_, b, "lo_k")
                bank_free(f"prep.st{t}", b)
                dst = ps_a[:, :].bitcast(F16)
                for s in range(2):
                    for g in range(4):
                        c = (4 * s + g) * P
                        last = tr(dst[:, c:c + P], st[:, s, t, 4 * g:4 * g + 4].rearrange("p h c d -> p (h c d)"),
                                  ident16[:, :])
                pe["prep"].done(last, f"st{t}", b)

            def fin_y(b, half, k):
                ve["fin"].wait(t_, b, f"yU{half}")
                bank_free(f"fin.y{half}T", b)
                four(lambda c: y_u[:, P * c:P * c + P], pe["fin"], f"y{half}T", b)

            def fin_yT(b, k):
                ve["fin"].wait(t_, b, "y1")
                bank_free("fin.yT", b)
                four(lambda c: y_tm[:, c, :], pe["fin"], "yT", b)

            def fin_wo(b, k):
                ve["fin"].wait(t_, b, "yT")
                bank_free("fin.wo", b)
                for c in range(NT):
                    last = mm(ps_m[:, P * c:P * c + P], yT[:, P * c:P * c + P], wT[:, 3, :], start=True, stop=True)
                pe["fin"].done(last, "wo", b)

            def route_wrow(b, k):
                ve["route"].wait(t_, b, "wide")
                bank_free("route.wrow", b)
                four(lambda c: w_wide[:, P * c:P * c + P], pe["route"], "wrow", b)

            def trig_row(b):
                return min(b.no, MASKS - 1) if isinstance(b.no, int) else MASKS - 1

            def sel_gather(q, _):
                for k in range(2):
                    ve["route"].wait(t_, Batch(q, k), "E")
                bank_free("sel.gather", q)
                for k in range(2):
                    rows = slice(SLOTS * k, SLOTS * k + SLOTS)
                    for c in range(NT):
                        mm(ps_m[rows, 0:D + 1], E[:, c, rows], x1[:, k, c, :], start=(c == 0), stop=(c == NT - 1))
                    for c in range(NT):
                        last = mm(ps_m[rows, D + 1:D + 1 + 2 * DH], E[:, c, rows],
                                  trig[:, NT * trig_row(Batch(q, k)) + c, :], start=(c == 0), stop=(c == NT - 1))
                pe["sel"].done(last, "gather", q)

            def sel_ET(q, _):
                bank_free("sel.ET", q)
                four(lambda c: E[:, c, :], pe["sel"], "ET", q)

            def sel_R(q, _):
                bank_free("sel.R", q)
                t_.wait_ge(mask_loaded, {0: 32, 1: 64}.get(q, 80) if isinstance(q, int) else 80)
                for c in range(NT):
                    for k in range(2):
                        last = mm(ps_m[SLOTS * k:SLOTS * k + SLOTS, :], E[:, c, SLOTS * k:SLOTS * k + SLOTS],
                                  masks[:, k, c, :], start=(c == 0), stop=(c == NT - 1))
                pe["sel"].done(last, "R", q)

            def sel_RT(q, _):
                ve["sel"].wait(t_, q, "R")
                bank_free("sel.RT", q)
                four(lambda c: R[:, P * c:P * c + P], pe["sel"], "RT", q)

            def sel_hnT(q, _):
                ve["sel"].wait(t_, q, "hn")
                bank_free("sel.hnT", q)
                pe["sel"].done(tr(ps_m[:, 0:P], hn[:, :], ident[:, :]), "hnT", q)

            def sel_qkv(q, _):
                ve["sel"].wait(t_, q, "hnT")
                bank_free("sel.qkv", q)
                mm(ps_m[:, 0:2 * D], hnT[:, :, :, :].rearrange("p k a s -> p (k a s)")[:, SLOTS:3 * SLOTS],
                   wqkv2[:, 0:2, :].rearrange("p a d -> p (a d)"), start=True, stop=True)
                for k in range(2):
                    last = mm(ps_m[:, D * (2 + k):D * (3 + k)], hnT[:, k, :, :].rearrange("p a s -> p (a s)"),
                              wqkv2[:, 2, :], start=True, stop=True)
                pe["sel"].done(last, "qkv", q)

            def sel_msel(q, _):
                ve["sel"].wait(t_, q, "RT")
                bank_free("sel.msel", q)
                for k in range(2):
                    rows = slice(SLOTS * k, SLOTS * k + SLOTS)
                    for c in range(NT):
                        last = mm(ps_m[rows, 0:SLOTS], RT[:, c, rows], E[:, c, rows], start=(c == 0),
                                  stop=(c == NT - 1))
                pe["sel"].done(last, "msel", q)

            def sel_qkT(q, _):
                ve["sel"].wait(t_, q, "rope")
                bank_free("sel.qkT", q)
                for s in range(2):
                    last = tr(ps_m[:, P * s:P * s + P], qk_r[:, D * s:D * s + D], ident[:, :])
                pe["sel"].done(last, "qkT", q)

            def att_scores(q, h):
                pl["att"].wait(t_, q, "kw1")
                bank_free(f"att.S{h}", q)
                for k in range(2):
                    rows = slice(SLOTS * k, SLOTS * k + SLOTS)
                    last = mm(ps_m[rows, :], qkT[:, 0, rows],
                              k_wide[:, k, 8 * h:8 * h + 8, :].rearrange("p h s -> p (h s)"), start=True, stop=True)
                pe["att"].done(last, f"S{h}", q)

            def att_P(q, h):
                t_.wait_ge(probs_ready, q + 1)
                bank_free(f"att.P{h}", q)
                four(lambda c: pm[:, 8 * h + 2 * c:8 * h + 2 * c + 2, :].rearrange("p a s -> p (a s)"), pe["att"],
                     f"P{h}T", q)

            def att_PV(q, _):
                ve["att"].wait(t_, q, "PT1")
                bank_free("att.PV", q)
                for n in range(H // 2):
                    last = mm(ps_m[:, 32 * n:32 * n + 32], PT[:, n, :], vv[:, n, :, :].rearrange("p k c -> p (k c)"),
                              start=True, stop=True)
                pe["att"].done(last, "PV", q)

            def att_oT(q, _):
                ve["att"].wait(t_, q, "o1")
                bank_free("att.oT", q)
                pe["att"].done(tr(ps_m[:, 0:P], o_tm[:, :, :, :].rearrange("p n a d -> p (n a d)"), ident[:, :]), "oT", q)

            def att_wo(q, _):
                ve["att"].wait(t_, q, "oT")
                bank_free("att.wo", q)
                pe["att"].done(mm(ps_m[:, 0:D], oT[:, :], wo2[:, :], start=True, stop=True), "wo", q)

            def att_h2T(q, _):
                ve["att"].wait(t_, q, "hn2")
                bank_free("att.h2T", q)
                pe["att"].done(tr(ps_m[:, 0:P], hn[:, :], ident[:, :]), "h2T", q)

            def att_w1(q, _):
                ve["att"].wait(t_, q, "h2T")
                bank_free("att.w1", q)
                for c in range(F // P):
                    last = mm(ps_m[:, P * c:P * c + P], w1_sb[:, P * c:P * c + P], h2T[:, :], start=True, stop=True)
                pe["att"].done(last, "w1", q)

            def late_w2(q, _):
                ve["att"].wait(t_, q, "g")
                bank_free("late.w2", q)
                for c in range(F // P):
                    last = mm(ps_m[:, 0:D], hu[:, P * c:P * c + P], w2_sb[:, c, :], start=(c == 0),
                              stop=(c == F // P - 1))
                pe["late"].done(last, "w2", q)

            def late_sc(q, k):
                ve["late"].wait(t_, q, "proc")
                bank_free(f"late.sc{k}", q)
                rows = slice(SLOTS * k, SLOTS * k + SLOTS)
                for c in range(NT):
                    last = mm(ps_m[:, P * c:P * c + P], ET[rows, P * c:P * c + P], proc[rows, :], start=True, stop=True)
                pe["late"].done(last, f"sc{k}", q)

            table = {"prep.xT": prep_xT, "prep.qk0": lambda b, k: prep_qk(b, k, 0),
                     "prep.qk1": lambda b, k: prep_qk(b, k, 1), "prep.v": prep_v,
                     **{f"prep.st{t}": (lambda b, k, t=t: prep_st(b, k, t)) for t in range(NT)},
                     **{f"pv.{q}": (lambda b, k, q=q: pv(b, k, q)) for q in range(4)},
                     "fin.y0T": lambda b, k: fin_y(b, 0, k), "fin.y1T": lambda b, k: fin_y(b, 1, k),
                     "fin.yT": fin_yT, "fin.wo": fin_wo, "route.wrow": route_wrow, "sel.gather": sel_gather,
                     "sel.ET": sel_ET, "sel.R": sel_R, "sel.RT": sel_RT, "sel.hnT": sel_hnT, "sel.qkv": sel_qkv,
                     "sel.msel": sel_msel, "sel.qkT": sel_qkT, "att.S0": lambda q, _: att_scores(q, 0),
                     "att.S1": lambda q, _: att_scores(q, 1), "att.P0": lambda q, _: att_P(q, 0),
                     "att.P1": lambda q, _: att_P(q, 1), "att.PV": att_PV, "att.oT": att_oT, "att.wo": att_wo,
                     "att.h2T": att_h2T, "att.w1": att_w1, "late.w2": late_w2,
                     "late.sc0": lambda q, _: late_sc(q, 0), "late.sc1": lambda q, _: late_sc(q, 1)}

            def body(p):
                for s in range(16):
                    for half in range(2):
                        g = group(p, s, -1)
                        if g and g[2] == 0 and half == 0:
                            ve["prep"].wait(t_, g[0], f"kst{NT - 1}")
                        if g:
                            scores(g[0], g[1], g[2], half)
                        run_side(PE_ORDER, table, p, s, half)
            iterations(t_, body, 3, PAIRS - 2)


SETUP_RED = 25
SETUP_ALL = 29


_INS = ['L0_attn_x', 'L0_attn_w_q', 'L0_attn_w_k', 'L0_attn_w_v', 'L0_attn_w_o', 'L0_ffn_attention_mask',
        'L0_ffn_position_ids', 'L0_ffn_router_w', 'L0_ffn_router_b', 'L0_ffn_wq', 'L0_ffn_wk', 'L0_ffn_wv',
        'L0_ffn_wo', 'L0_ffn_w1', 'L0_ffn_w2', 'L0_ffn_ln1', 'L0_ffn_ln2']


def kernel(**inputs):
    import numpy as _np
    import concourse.bacc as _bacc
    from concourse import mybir as _mybir
    from concourse.bass_utils import run_bass_kernel_spmd as _run

    nc = _bacc.Bacc("TRN2", target_bir_lowering=False, num_devices=1)
    arrays, args = {}, []
    for name in _INS:
        a = _np.ascontiguousarray(inputs[name])
        arrays[f"in_{name}"] = a
        args.append(nc.dram_tensor(f"in_{name}", a.shape, _mybir.dt.from_np(a.dtype), kind="ExternalInput").ap())
    args.append(nc.dram_tensor("result", (16, 512, 128), _mybir.dt.float32, kind="ExternalOutput").ap())
    build(nc, *args)
    r = _run(nc, [arrays], core_ids=[0])
    return r.results[0]["result"]
```
